# Optimizing a Trainium2 kernel written in Bass

```python
import numpy as np
import jax
import jax.numpy as jnp

def _softmax(x, axis=-1):
    return jax.nn.softmax(x, axis=axis)

def _gelu(x):
    return jax.nn.gelu(x, approximate=True)

def _silu(x):
    return jax.nn.silu(x)

def _sigmoid(x):
    return jax.nn.sigmoid(x)

def _layernorm(x, axis=-1, eps=1e-05):
    m = jnp.mean(x, axis=axis, keepdims=True)
    v = jnp.var(x, axis=axis, keepdims=True)
    return (x - m) / jnp.sqrt(v + eps)

def _scatter_add(tgt, idx, src, axis=0):
    return tgt.at[idx].add(src)

def _segment_sum(src, seg, n):
    return jax.ops.segment_sum(src, seg, n)
kernel_name = 'mk_gnn_ffn_d4_gnn_r16_bab3b4'

def setup_inputs(seed: int=0):
    np.random.seed(seed)
    _w = jnp.asarray

    def _rec_inputs():
        import jax
        import jax.numpy as jnp
        _gk = jax.random.key(seed)
        x = -8.776e-05 + 1 * jax.random.normal(jax.random.fold_in(_gk, 1), (625, 512), jnp.float32)
        src = jax.random.randint(jax.random.fold_in(_gk, 2), (20000,), 0, 625, jnp.int32)
        dst = jnp.minimum((625 * jax.random.uniform(jax.random.fold_in(_gk, 3), (20000,)) ** 2.0).astype(jnp.int32), 9999)
        _o = jnp.argsort(dst, stable=True)
        src = src[_o]
        dst = dst[_o]
        edge_attr_4 = 0.00171547 + 0.999346 * jax.random.normal(jax.random.fold_in(_gk, 11), (20000, 4), jnp.float32)
        edge_attr_8 = 0.000126197 + 0.999763 * jax.random.normal(jax.random.fold_in(_gk, 12), (20000, 8), jnp.float32)
        return (x, src, dst, edge_attr_4, edge_attr_8)
    x, src, dst, edge_attr_4, edge_attr_8 = _rec_inputs()

    def _L0_gnn_setup():
        import jax, jax.numpy as jnp
        import numpy as np
        N_NODES = 625

        def gcn_conv(x, edge_index, W, b):
            n = x.shape[0]
            h = x @ W
            loop = jnp.arange(n, dtype=edge_index.dtype)
            src = jnp.concatenate([edge_index[0], loop])
            dst = jnp.concatenate([edge_index[1], loop])
            ones = jnp.ones(src.shape[0], dtype=h.dtype)
            deg = jax.ops.segment_sum(ones, dst, num_segments=n)
            dis = jnp.where(deg > 0, jax.lax.rsqrt(deg), 0.0)
            norm = dis[src] * dis[dst]
            msg = h[src] * norm[:, None]
            out = jax.ops.segment_sum(msg, dst, num_segments=n)
            return out + b
        key = jax.random.key(seed)
        k1, k2, k3, k4, k5 = jax.random.split(key, 5)
        num_features, hidden, num_classes = (512, 512, 512)
        x = jax.random.normal(k1, (N_NODES, num_features), dtype=jnp.float32)
        edge_index = jax.random.randint(k2, (2, 10000), 0, N_NODES, dtype=jnp.int64)
        s1 = 1.0 / np.sqrt(num_features)
        s2 = 1.0 / np.sqrt(hidden)
        W1 = jax.random.uniform(k3, (num_features, hidden), jnp.float32, -s1, s1)
        b1 = jnp.zeros((hidden,), jnp.float32)
        W2 = jax.random.uniform(k4, (hidden, num_classes), jnp.float32, -s2, s2)
        b2 = jnp.zeros((num_classes,), jnp.float32)
        return {'x': x, 'edge_index': edge_index, 'W1': W1, 'b1': b1, 'W2': W2, 'b2': b2}
    _L0_gnn_all = _L0_gnn_setup()
    _L0_gnn_in = {k: v for k, v in _L0_gnn_all.items() if k in ('W1', 'b1', 'W2', 'b2')}
    del _L0_gnn_all

    def _L0_ffn_setup():
        import jax, jax.numpy as jnp
        import numpy as np
        B, S, D, F, E = (4, 128, 512, 128, 8)
        key = jax.random.key(seed)
        k = jax.random.split(key, 5)
        x = jax.random.normal(k[0], (B, S, D), dtype=jnp.float32)
        Ws = jax.random.normal(k[1], (D, E), dtype=jnp.float32) * 0.02
        bs = jnp.zeros((E,), dtype=jnp.float32)
        W1 = jax.random.normal(k[2], (E, D, F), dtype=jnp.float32) * 0.02
        b1 = jnp.zeros((E, F), dtype=jnp.float32)
        W2 = jax.random.normal(k[3], (E, F, D), dtype=jnp.float32) * 0.02
        b2 = jnp.zeros((E, D), dtype=jnp.float32)
        return {'x': x, 'Ws': Ws, 'bs': bs, 'W1': W1, 'b1': b1, 'W2': W2, 'b2': b2}
    _L0_ffn_all = _L0_ffn_setup()
    _L0_ffn_in = {k: v for k, v in _L0_ffn_all.items() if k in ('Ws', 'bs', 'W1', 'b1', 'W2', 'b2')}
    del _L0_ffn_all

    def _L1_gnn_setup():
        import jax, jax.numpy as jnp
        import numpy as np
        MUL = 128
        N_NODES = 625
        N_EDGES = 10000
        R_BASIS = 8
        HIDDEN = 64
        W_NUMEL = 4 * MUL
        SQRT3 = 3.0 ** 0.5
        SILU_2MOM = 1.679177
        AVG_NUM_NEIGHBORS = 10.0

        def _lin_irreps(x0, x1, W0, W1):
            y0 = x0 @ W0 / jnp.sqrt(jnp.float32(W0.shape[0]))
            y1 = jnp.einsum('num,uv->nvm', x1, W1) / jnp.sqrt(jnp.float32(W1.shape[0]))
            return (y0, y1)

        def _forward(node_feats, edge_attrs, edge_feats, edge_index, W_up0, W_up1, W_mlp1, W_mlp2, W_mlp3, W_mlp4, W_out0, W_out1):
            num_nodes = node_feats.shape[0]
            sender, receiver = (edge_index[0], edge_index[1])
            x0 = node_feats[:, :MUL]
            x1 = node_feats[:, MUL:].reshape(num_nodes, MUL, 3)
            x0, x1 = _lin_irreps(x0, x1, W_up0, W_up1)
            h = edge_feats
            for W in (W_mlp1, W_mlp2, W_mlp3):
                h = SILU_2MOM * jax.nn.silu(h @ W / jnp.sqrt(jnp.float32(W.shape[0])))
            tpw = h @ W_mlp4 / jnp.sqrt(jnp.float32(W_mlp4.shape[0]))
            w1, w2, w3, w4 = jnp.split(tpw, 4, axis=-1)
            s0 = x0[sender]
            s1 = x1[sender]
            y0 = edge_attrs[:, 0:1]
            y1 = edge_attrs[:, 1:4]
            p1 = w1 * s0 * y0
            p2 = (w2 * s0)[:, :, None] * y1[:, None, :]
            p3 = w3[:, :, None] * s1 * y0[:, None, :]
            p4 = w4 * jnp.einsum('eum,em->eu', s1, y1) / SQRT3
            m0 = jnp.concatenate([p1, p4], axis=-1)
            m1 = jnp.concatenate([p2, p3], axis=1)
            msg0 = jax.ops.segment_sum(m0, receiver, num_segments=num_nodes)
            msg1 = jax.ops.segment_sum(m1, receiver, num_segments=num_nodes)
            o0, o1 = _lin_irreps(msg0, msg1, W_out0, W_out1)
            out = jnp.concatenate([o0, o1.reshape(num_nodes, 3 * MUL)], axis=-1)
            return out / AVG_NUM_NEIGHBORS
        key = jax.random.key(seed)
        ks = jax.random.split(key, 12)
        rn = lambda k, s: jax.random.normal(k, s, dtype=jnp.float32)
        return {'node_feats': rn(ks[0], (N_NODES, 4 * MUL)), 'edge_attrs': rn(ks[1], (N_EDGES, 4)), 'edge_feats': rn(ks[2], (N_EDGES, R_BASIS)), 'edge_index': jax.random.randint(ks[3], (2, N_EDGES), 0, N_NODES), 'W_up0': rn(ks[4], (MUL, MUL)), 'W_up1': rn(ks[5], (MUL, MUL)), 'W_mlp1': rn(ks[6], (R_BASIS, HIDDEN)), 'W_mlp2': rn(ks[7], (HIDDEN, HIDDEN)), 'W_mlp3': rn(ks[8], (HIDDEN, HIDDEN)), 'W_mlp4': rn(ks[9], (HIDDEN, W_NUMEL)), 'W_out0': rn(ks[10], (2 * MUL, MUL)), 'W_out1': rn(ks[11], (2 * MUL, MUL))}
    _L1_gnn_all = _L1_gnn_setup()
    _L1_gnn_in = {k: v for k, v in _L1_gnn_all.items() if k in ('W_up0', 'W_up1', 'W_mlp1', 'W_mlp2', 'W_mlp3', 'W_mlp4', 'W_out0', 'W_out1')}
    del _L1_gnn_all

    def _L1_ffn_setup():
        import jax, jax.numpy as jnp
        import numpy as np
        STEP_SIZE = 0.1

        def _mlp(y, W1, b1, W2, b2, W3, b3):
            h = jnp.tanh(y @ W1.T + b1)
            h = jnp.tanh(h @ W2.T + b2)
            return h @ W3.T + b3

        def _rk4_step(y, dt, params):
            f = lambda z: _mlp(z, *params)
            k1 = f(y)
            k2 = f(y + dt / 2 * k1)
            k3 = f(y + dt / 2 * k2)
            k4 = f(y + dt * k3)
            return y + dt * (k1 + 2 * k2 + 2 * k3 + k4) / 6
        key = jax.random.key(seed)
        ks = jax.random.split(key, 7)
        B, S, D, H = (256, 64, 512, 128)
        return {'x': jax.random.normal(ks[0], (B, S, D), dtype=jnp.float32), 'W1': jax.random.normal(ks[1], (H, D), dtype=jnp.float32) * (1.0 / np.sqrt(D)), 'b1': jax.random.normal(ks[2], (H,), dtype=jnp.float32) * 0.01, 'W2': jax.random.normal(ks[3], (H, H), dtype=jnp.float32) * (1.0 / np.sqrt(H)), 'b2': jax.random.normal(ks[4], (H,), dtype=jnp.float32) * 0.01, 'W3': jax.random.normal(ks[5], (D, H), dtype=jnp.float32) * (1.0 / np.sqrt(H)), 'b3': jax.random.normal(ks[6], (D,), dtype=jnp.float32) * 0.01}
    _L1_ffn_all = _L1_ffn_setup()
    _L1_ffn_in = {k: v for k, v in _L1_ffn_all.items() if k in ('W1', 'b1', 'W2', 'b2', 'W3', 'b3')}
    del _L1_ffn_all

    def _L2_gnn_setup():
        import jax, jax.numpy as jnp
        import numpy as np
        N_NODES = 3125
        IN_CH = 512
        OUT_CH = 512
        N_EDGES = 50000
        key = jax.random.key(seed)
        k_x, k_e, k_w, k_b = jax.random.split(key, 4)
        x = jax.random.normal(k_x, (N_NODES, IN_CH), dtype=jnp.float32)
        edge_index = jax.random.randint(k_e, (2, N_EDGES), 0, N_NODES, dtype=jnp.int32)
        bound = 1.0 / np.sqrt(2 * IN_CH)
        W = jax.random.uniform(k_w, (OUT_CH, 2 * IN_CH), minval=-bound, maxval=bound, dtype=jnp.float32)
        b = jax.random.uniform(k_b, (OUT_CH,), minval=-bound, maxval=bound, dtype=jnp.float32)
        return {'x': x, 'edge_index': edge_index, 'W': W, 'b': b}
    _L2_gnn_all = _L2_gnn_setup()
    _L2_gnn_in = {k: v for k, v in _L2_gnn_all.items() if k in ('W', 'b')}
    del _L2_gnn_all

    def _L2_ffn_setup():
        import jax, jax.numpy as jnp
        import numpy as np
        B, T, I, H, S = (64, 128, 512, 512, 4)

        def _lstm_activate(gates, c):
            i, f, g, o = jnp.split(gates, 4, axis=-1)
            c_new = jax.nn.sigmoid(f) * c + jax.nn.sigmoid(i) * jnp.tanh(g)
            h_new = jax.nn.sigmoid(o) * jnp.tanh(c_new)
            return (h_new, c_new)
        key = jax.random.key(seed)
        ks = jax.random.split(key, 7)
        sc_i = 1.0 / np.sqrt(I)
        sc_h = 1.0 / np.sqrt(H)
        x = jax.random.normal(ks[0], (B, T, I), jnp.float32)
        W_ih = jax.random.normal(ks[1], (S, 4 * H, I), jnp.float32) * sc_i
        W_hh = jax.random.normal(ks[2], (S, 4 * H, H), jnp.float32) * sc_h
        b_ih = jax.random.normal(ks[3], (S, 4 * H), jnp.float32) * sc_h
        b_hh = jax.random.normal(ks[4], (S, 4 * H), jnp.float32) * sc_h
        W_sel = jax.random.normal(ks[5], (S, 2 * H + I), jnp.float32) * sc_h
        b_sel = jax.random.normal(ks[6], (S,), jnp.float32) * sc_h
        return {'x': x, 'W_ih': W_ih, 'W_hh': W_hh, 'b_ih': b_ih, 'b_hh': b_hh, 'W_sel': W_sel, 'b_sel': b_sel}
    _L2_ffn_all = _L2_ffn_setup()
    _L2_ffn_in = {k: v for k, v in _L2_ffn_all.items() if k in ('W_ih', 'W_hh', 'b_ih', 'b_hh', 'W_sel', 'b_sel')}
    del _L2_ffn_all

    def _L3_gnn_setup():
        import jax, jax.numpy as jnp
        import numpy as np
        N, E, D = (3125, 25000, 512)
        EPS = 1e-05
        key = jax.random.key(seed)
        ks = jax.random.split(key, 5)
        scale = 1.0 / np.sqrt(D)
        x = jax.random.normal(ks[0], (N, D), dtype=jnp.float32)
        edge_index = jax.random.randint(ks[1], (2, E), 0, N, dtype=jnp.int32)
        W_l = jax.random.normal(ks[2], (D, D), dtype=jnp.float32) * scale
        b_l = jnp.zeros((D,), dtype=jnp.float32)
        W_r = jax.random.normal(ks[3], (D, D), dtype=jnp.float32) * scale
        gamma = jnp.ones((D,), dtype=jnp.float32)
        beta = jnp.zeros((D,), dtype=jnp.float32)
        return {'x': x, 'edge_index': edge_index, 'W_l': W_l, 'b_l': b_l, 'W_r': W_r, 'gamma': gamma, 'beta': beta}
    _L3_gnn_all = _L3_gnn_setup()
    _L3_gnn_in = {k: v for k, v in _L3_gnn_all.items() if k in ('W_l', 'b_l', 'W_r', 'gamma', 'beta')}
    del _L3_gnn_all

    def _L3_ffn_setup():
        import jax, jax.numpy as jnp
        import numpy as np
        DIM = 512
        HEADS = 8
        DIM_KEY = 32
        NUM_EXPERTS = 4096
        NUM_KEYS = 256
        TOPK = 16
        BN_EPS = 1e-05

        def peer_forward(x, w_q, keys, weight_down_embed, weight_up_embed):
            b, n, _ = x.shape
            q = x @ w_q * (1.0 / np.sqrt(1.0 + BN_EPS))
            queries = q.reshape(b, n, 2, HEADS, DIM_KEY).transpose(2, 0, 1, 3, 4)
            sim = jnp.einsum('pbnhd,hkpd->pbnhk', queries, keys)
            v0, i0 = jax.lax.top_k(sim[0], TOPK)
            v1, i1 = jax.lax.top_k(sim[1], TOPK)
            all_scores = v0[..., :, None] + i0[..., None, :].astype(v0.dtype)
            all_scores = all_scores.reshape(*all_scores.shape[:-2], -1)
            scores, pk_indices = jax.lax.top_k(all_scores, TOPK)
            weights_down = jnp.take(weight_down_embed, pk_indices, axis=0)
            weights_up = jnp.take(weight_up_embed, pk_indices, axis=0)
            h = jnp.einsum('bnd,bnhkd->bnhk', q, weights_down)
            h = jax.nn.gelu(h)
            h = h * jax.nn.softmax(scores, axis=-1)
            out = jnp.einsum('bnhk,bnhkd->bnd', h, weights_up)
            return out
        key = jax.random.key(seed)
        k1, k2, k3, k4, k5 = jax.random.split(key, 5)
        b, n = (2, 512)
        x = jax.random.normal(k1, (b, n, DIM), dtype=jnp.float32)
        w_q = jax.random.normal(k2, (DIM, DIM_KEY * HEADS * 2), dtype=jnp.float32) / np.sqrt(DIM)
        keys = jax.random.normal(k3, (HEADS, NUM_KEYS, 2, DIM_KEY), dtype=jnp.float32) * 0.01
        weight_down_embed = jax.random.normal(k4, (NUM_EXPERTS, DIM), dtype=jnp.float32) * 0.01
        weight_up_embed = jax.random.normal(k5, (NUM_EXPERTS, DIM), dtype=jnp.float32) * 0.01
        return {'x': x, 'w_q': w_q, 'keys': keys, 'weight_down_embed': weight_down_embed, 'weight_up_embed': weight_up_embed}
    _L3_ffn_all = _L3_ffn_setup()
    _L3_ffn_in = {k: v for k, v in _L3_ffn_all.items() if k in ('w_q', 'keys', 'weight_down_embed', 'weight_up_embed')}
    del _L3_ffn_all
    return {'x': x, 'src': src, 'dst': dst, 'edge_attr_4': edge_attr_4, 'edge_attr_8': edge_attr_8, 'L0_gnn_W1': _L0_gnn_in['W1'], 'L0_gnn_b1': _L0_gnn_in['b1'], 'L0_gnn_W2': _L0_gnn_in['W2'], 'L0_gnn_b2': _L0_gnn_in['b2'], 'L0_ffn_Ws': _L0_ffn_in['Ws'], 'L0_ffn_bs': _L0_ffn_in['bs'], 'L0_ffn_W1': _L0_ffn_in['W1'], 'L0_ffn_b1': _L0_ffn_in['b1'], 'L0_ffn_W2': _L0_ffn_in['W2'], 'L0_ffn_b2': _L0_ffn_in['b2'], 'L1_gnn_W_up0': _L1_gnn_in['W_up0'], 'L1_gnn_W_up1': _L1_gnn_in['W_up1'], 'L1_gnn_W_mlp1': _L1_gnn_in['W_mlp1'], 'L1_gnn_W_mlp2': _L1_gnn_in['W_mlp2'], 'L1_gnn_W_mlp3': _L1_gnn_in['W_mlp3'], 'L1_gnn_W_mlp4': _L1_gnn_in['W_mlp4'], 'L1_gnn_W_out0': _L1_gnn_in['W_out0'], 'L1_gnn_W_out1': _L1_gnn_in['W_out1'], 'L1_ffn_W1': _L1_ffn_in['W1'], 'L1_ffn_b1': _L1_ffn_in['b1'], 'L1_ffn_W2': _L1_ffn_in['W2'], 'L1_ffn_b2': _L1_ffn_in['b2'], 'L1_ffn_W3': _L1_ffn_in['W3'], 'L1_ffn_b3': _L1_ffn_in['b3'], 'L2_gnn_W': _L2_gnn_in['W'], 'L2_gnn_b': _L2_gnn_in['b'], 'L2_ffn_W_ih': _L2_ffn_in['W_ih'], 'L2_ffn_W_hh': _L2_ffn_in['W_hh'], 'L2_ffn_b_ih': _L2_ffn_in['b_ih'], 'L2_ffn_b_hh': _L2_ffn_in['b_hh'], 'L2_ffn_W_sel': _L2_ffn_in['W_sel'], 'L2_ffn_b_sel': _L2_ffn_in['b_sel'], 'L3_gnn_W_l': _L3_gnn_in['W_l'], 'L3_gnn_b_l': _L3_gnn_in['b_l'], 'L3_gnn_W_r': _L3_gnn_in['W_r'], 'L3_gnn_gamma': _L3_gnn_in['gamma'], 'L3_gnn_beta': _L3_gnn_in['beta'], 'L3_ffn_w_q': _L3_ffn_in['w_q'], 'L3_ffn_keys': _L3_ffn_in['keys'], 'L3_ffn_weight_down_embed': _L3_ffn_in['weight_down_embed'], 'L3_ffn_weight_up_embed': _L3_ffn_in['weight_up_embed']}

def reference(x, src, dst, edge_attr_4, edge_attr_8, L0_gnn_W1, L0_gnn_b1, L0_gnn_W2, L0_gnn_b2, L0_ffn_Ws, L0_ffn_bs, L0_ffn_W1, L0_ffn_b1, L0_ffn_W2, L0_ffn_b2, L1_gnn_W_up0, L1_gnn_W_up1, L1_gnn_W_mlp1, L1_gnn_W_mlp2, L1_gnn_W_mlp3, L1_gnn_W_mlp4, L1_gnn_W_out0, L1_gnn_W_out1, L1_ffn_W1, L1_ffn_b1, L1_ffn_W2, L1_ffn_b2, L1_ffn_W3, L1_ffn_b3, L2_gnn_W, L2_gnn_b, L2_ffn_W_ih, L2_ffn_W_hh, L2_ffn_b_ih, L2_ffn_b_hh, L2_ffn_W_sel, L2_ffn_b_sel, L3_gnn_W_l, L3_gnn_b_l, L3_gnn_W_r, L3_gnn_gamma, L3_gnn_beta, L3_ffn_w_q, L3_ffn_keys, L3_ffn_weight_down_embed, L3_ffn_weight_up_embed):
    import jax
    import jax.numpy as jnp

    def _L0_gnn_ref(x, edge_index, W1, b1, W2, b2):
        import jax, jax.numpy as jnp
        import numpy as np
        N_NODES = 625

        def gcn_conv(x, edge_index, W, b):
            n = x.shape[0]
            h = x @ W
            loop = jnp.arange(n, dtype=edge_index.dtype)
            src = jnp.concatenate([edge_index[0], loop])
            dst = jnp.concatenate([edge_index[1], loop])
            ones = jnp.ones(src.shape[0], dtype=h.dtype)
            deg = jax.ops.segment_sum(ones, dst, num_segments=n)
            dis = jnp.where(deg > 0, jax.lax.rsqrt(deg), 0.0)
            norm = dis[src] * dis[dst]
            msg = h[src] * norm[:, None]
            out = jax.ops.segment_sum(msg, dst, num_segments=n)
            return out + b
        h = jax.nn.relu(gcn_conv(x, edge_index, W1, b1))
        out = gcn_conv(h, edge_index, W2, b2)
        return out

    def _L0_ffn_ref(x, Ws, bs, W1, b1, W2, b2):
        import jax, jax.numpy as jnp
        import numpy as np
        B, S, D, F, E = (4, 128, 512, 128, 8)
        Bb, Ss, Dd = x.shape
        xt = x.reshape(-1, Dd)
        logits = xt @ Ws + bs
        probs = jax.nn.softmax(logits, axis=-1)
        prob_max = jnp.max(probs, axis=-1)
        routes = jnp.argmax(probs, axis=-1)
        onehot = jax.nn.one_hot(routes, W1.shape[0], dtype=xt.dtype)

        def expert_ffn(w1, bb1, w2, bb2):
            h = jax.nn.gelu(xt @ w1 + bb1, approximate=False)
            return h @ w2 + bb2
        y = jax.vmap(expert_ffn)(W1, b1, W2, b2)
        out = jnp.einsum('te,etd->td', onehot, y)
        out = out * prob_max[:, None]
        return out.reshape(Bb, Ss, Dd)

    def _L1_gnn_ref(node_feats, edge_attrs, edge_feats, edge_index, W_up0, W_up1, W_mlp1, W_mlp2, W_mlp3, W_mlp4, W_out0, W_out1):
        import jax, jax.numpy as jnp
        import numpy as np
        MUL = 128
        N_NODES = 625
        N_EDGES = 10000
        R_BASIS = 8
        HIDDEN = 64
        W_NUMEL = 4 * MUL
        SQRT3 = 3.0 ** 0.5
        SILU_2MOM = 1.679177
        AVG_NUM_NEIGHBORS = 10.0

        def _lin_irreps(x0, x1, W0, W1):
            y0 = x0 @ W0 / jnp.sqrt(jnp.float32(W0.shape[0]))
            y1 = jnp.einsum('num,uv->nvm', x1, W1) / jnp.sqrt(jnp.float32(W1.shape[0]))
            return (y0, y1)

        def _forward(node_feats, edge_attrs, edge_feats, edge_index, W_up0, W_up1, W_mlp1, W_mlp2, W_mlp3, W_mlp4, W_out0, W_out1):
            num_nodes = node_feats.shape[0]
            sender, receiver = (edge_index[0], edge_index[1])
            x0 = node_feats[:, :MUL]
            x1 = node_feats[:, MUL:].reshape(num_nodes, MUL, 3)
            x0, x1 = _lin_irreps(x0, x1, W_up0, W_up1)
            h = edge_feats
            for W in (W_mlp1, W_mlp2, W_mlp3):
                h = SILU_2MOM * jax.nn.silu(h @ W / jnp.sqrt(jnp.float32(W.shape[0])))
            tpw = h @ W_mlp4 / jnp.sqrt(jnp.float32(W_mlp4.shape[0]))
            w1, w2, w3, w4 = jnp.split(tpw, 4, axis=-1)
            s0 = x0[sender]
            s1 = x1[sender]
            y0 = edge_attrs[:, 0:1]
            y1 = edge_attrs[:, 1:4]
            p1 = w1 * s0 * y0
            p2 = (w2 * s0)[:, :, None] * y1[:, None, :]
            p3 = w3[:, :, None] * s1 * y0[:, None, :]
            p4 = w4 * jnp.einsum('eum,em->eu', s1, y1) / SQRT3
            m0 = jnp.concatenate([p1, p4], axis=-1)
            m1 = jnp.concatenate([p2, p3], axis=1)
            msg0 = jax.ops.segment_sum(m0, receiver, num_segments=num_nodes)
            msg1 = jax.ops.segment_sum(m1, receiver, num_segments=num_nodes)
            o0, o1 = _lin_irreps(msg0, msg1, W_out0, W_out1)
            out = jnp.concatenate([o0, o1.reshape(num_nodes, 3 * MUL)], axis=-1)
            return out / AVG_NUM_NEIGHBORS
        return _forward(node_feats, edge_attrs, edge_feats, edge_index, W_up0, W_up1, W_mlp1, W_mlp2, W_mlp3, W_mlp4, W_out0, W_out1)

    def _L1_ffn_ref(x, W1, b1, W2, b2, W3, b3):
        import jax, jax.numpy as jnp
        import numpy as np
        STEP_SIZE = 0.1

        def _mlp(y, W1, b1, W2, b2, W3, b3):
            h = jnp.tanh(y @ W1.T + b1)
            h = jnp.tanh(h @ W2.T + b2)
            return h @ W3.T + b3

        def _rk4_step(y, dt, params):
            f = lambda z: _mlp(z, *params)
            k1 = f(y)
            k2 = f(y + dt / 2 * k1)
            k3 = f(y + dt / 2 * k2)
            k4 = f(y + dt * k3)
            return y + dt * (k1 + 2 * k2 + 2 * k3 + k4) / 6
        B, S, D = x.shape
        params = (W1, b1, W2, b2, W3, b3)
        span = 1.0 / (S - 1)
        steps = max(1, int(span / STEP_SIZE))
        dt = span / steps

        def interval(y, _):
            for _s in range(steps):
                y = _rk4_step(y, dt, params)
            return (y, y)
        y0 = x[:, 0]
        _, ys = jax.lax.scan(interval, y0, None, length=S - 1)
        return jnp.concatenate([y0[:, None], jnp.moveaxis(ys, 0, 1)], axis=1)

    def _L2_gnn_ref(x, edge_index, W, b):
        import jax, jax.numpy as jnp
        import numpy as np
        N_NODES = 3125
        IN_CH = 512
        OUT_CH = 512
        N_EDGES = 50000
        src, dst = (edge_index[0], edge_index[1])
        src_feats = x[src]
        neighbor_sum = jax.ops.segment_sum(src_feats, dst, num_segments=x.shape[0])
        neighbor_count = jax.ops.segment_sum(jnp.ones((src.shape[0],), dtype=x.dtype), dst, num_segments=x.shape[0])
        neighbor_count = jnp.maximum(neighbor_count, 1.0)
        neighbor_mean = neighbor_sum / neighbor_count[:, None]
        h = jnp.concatenate([x, neighbor_mean], axis=-1)
        return h @ W.T + b

    def _L2_ffn_ref(x, W_ih, W_hh, b_ih, b_hh, W_sel, b_sel):
        import jax, jax.numpy as jnp
        import numpy as np
        B, T, I, H, S = (64, 128, 512, 512, 4)

        def _lstm_activate(gates, c):
            i, f, g, o = jnp.split(gates, 4, axis=-1)
            c_new = jax.nn.sigmoid(f) * c + jax.nn.sigmoid(i) * jnp.tanh(g)
            h_new = jax.nn.sigmoid(o) * jnp.tanh(c_new)
            return (h_new, c_new)
        Bx, Tx, Ix = x.shape
        Sx, fourH, _ = W_ih.shape
        Hx = fourH // 4
        c0 = jnp.zeros((Bx, Hx), x.dtype)
        g0 = x[:, 0] @ W_ih[0].T + b_ih[0] + b_hh[0]
        h, c = _lstm_activate(g0, c0)

        def step(carry, x_t):
            h, c = carry
            sel_in = jnp.concatenate([h, c, x_t], axis=-1)
            logits = sel_in @ W_sel.T + b_sel
            onehot = jax.nn.one_hot(jnp.argmax(logits, axis=-1), Sx, dtype=x_t.dtype)
            g_all = jnp.einsum('bi,sgi->bsg', x_t, W_ih) + jnp.einsum('bh,sgh->bsg', h, W_hh) + b_ih + b_hh
            g = jnp.einsum('bsg,bs->bg', g_all, onehot)
            h2, c2 = _lstm_activate(g, c)
            return ((h2, c2), h2)
        xs = jnp.swapaxes(x[:, 1:], 0, 1)
        (_, _), hs = jax.lax.scan(step, (h, c), xs)
        outputs = jnp.concatenate([h[:, None], jnp.swapaxes(hs, 0, 1)], axis=1)
        return outputs

    def _L3_gnn_ref(x, edge_index, W_l, b_l, W_r, gamma, beta):
        import jax, jax.numpy as jnp
        import numpy as np
        N, E, D = (3125, 25000, 512)
        EPS = 1e-05
        n = x.shape[0]
        src, dst = (edge_index[0], edge_index[1])
        agg = jax.ops.segment_sum(x[src], dst, num_segments=n)
        cnt = jax.ops.segment_sum(jnp.ones((src.shape[0],), x.dtype), dst, num_segments=n)
        mean_agg = agg / jnp.maximum(cnt, 1.0)[:, None]
        h = mean_agg @ W_l.T + b_l + x @ W_r.T
        mu = jnp.mean(h, axis=0)
        var = jnp.var(h, axis=0)
        h = (h - mu) * jax.lax.rsqrt(var + EPS) * gamma + beta
        return jax.nn.relu(h) + x

    def _L3_ffn_ref(x, w_q, keys, weight_down_embed, weight_up_embed):
        import jax, jax.numpy as jnp
        import numpy as np
        DIM = 512
        HEADS = 8
        DIM_KEY = 32
        NUM_EXPERTS = 4096
        NUM_KEYS = 256
        TOPK = 16
        BN_EPS = 1e-05

        def peer_forward(x, w_q, keys, weight_down_embed, weight_up_embed):
            b, n, _ = x.shape
            q = x @ w_q * (1.0 / np.sqrt(1.0 + BN_EPS))
            queries = q.reshape(b, n, 2, HEADS, DIM_KEY).transpose(2, 0, 1, 3, 4)
            sim = jnp.einsum('pbnhd,hkpd->pbnhk', queries, keys)
            v0, i0 = jax.lax.top_k(sim[0], TOPK)
            v1, i1 = jax.lax.top_k(sim[1], TOPK)
            all_scores = v0[..., :, None] + i0[..., None, :].astype(v0.dtype)
            all_scores = all_scores.reshape(*all_scores.shape[:-2], -1)
            scores, pk_indices = jax.lax.top_k(all_scores, TOPK)
            weights_down = jnp.take(weight_down_embed, pk_indices, axis=0)
            weights_up = jnp.take(weight_up_embed, pk_indices, axis=0)
            h = jnp.einsum('bnd,bnhkd->bnhk', q, weights_down)
            h = jax.nn.gelu(h)
            h = h * jax.nn.softmax(scores, axis=-1)
            out = jnp.einsum('bnhk,bnhkd->bnd', h, weights_up)
            return out
        return peer_forward(x, w_q, keys, weight_down_embed, weight_up_embed)
    edge_index = jnp.stack([src, dst])
    x = x + _L0_gnn_ref(_layernorm(x, axis=-1), edge_index, L0_gnn_W1, L0_gnn_b1, L0_gnn_W2, L0_gnn_b2)
    x = x + _L0_ffn_ref(_layernorm(x, axis=-1)[None], L0_ffn_Ws, L0_ffn_bs, L0_ffn_W1, L0_ffn_b1, L0_ffn_W2, L0_ffn_b2)[0]
    x = x + _L1_gnn_ref(_layernorm(x, axis=-1), edge_attr_4, edge_attr_8, edge_index, L1_gnn_W_up0, L1_gnn_W_up1, L1_gnn_W_mlp1, L1_gnn_W_mlp2, L1_gnn_W_mlp3, L1_gnn_W_mlp4, L1_gnn_W_out0, L1_gnn_W_out1)
    x = x + _L1_ffn_ref(_layernorm(x, axis=-1)[None], L1_ffn_W1, L1_ffn_b1, L1_ffn_W2, L1_ffn_b2, L1_ffn_W3, L1_ffn_b3)[0]
    x = x + _L2_gnn_ref(_layernorm(x, axis=-1), edge_index, L2_gnn_W, L2_gnn_b)
    x = x + _L2_ffn_ref(_layernorm(x, axis=-1)[None], L2_ffn_W_ih, L2_ffn_W_hh, L2_ffn_b_ih, L2_ffn_b_hh, L2_ffn_W_sel, L2_ffn_b_sel)[0]
    x = x + _L3_gnn_ref(_layernorm(x, axis=-1), edge_index, L3_gnn_W_l, L3_gnn_b_l, L3_gnn_W_r, L3_gnn_gamma, L3_gnn_beta)
    x = x + _L3_ffn_ref(_layernorm(x, axis=-1)[None], L3_ffn_w_q, L3_ffn_keys, L3_ffn_weight_down_embed, L3_ffn_weight_up_embed)[0]
    return x

_drawn_inputs = setup_inputs


def setup_inputs(seed=0):
    import zlib

    import numpy as np

    out = dict(_drawn_inputs(seed))
    spreads = {'L0_gnn_b1': (0.0, 0.1),
     'L0_gnn_b2': (0.0, 0.1),
     'L0_ffn_bs': (0.0, 0.536),
     'L0_ffn_b1': (0.0, 0.637),
     'L0_ffn_b2': (0.0, 0.297),
     'L3_gnn_b_l': (0.0, 0.8),
     'L3_gnn_gamma': (1.0, 0.2),
     'L3_gnn_beta': (0.0, 0.319)}
    factors = {'L0_gnn_W1': 2.924,
     'L0_ffn_W1': 3.627,
     'L0_ffn_W2': 3.209,
     'L1_ffn_b1': 8.0,
     'L1_ffn_b2': 8.0,
     'L1_ffn_b3': 8.0,
     'L2_gnn_b': 4.292,
     'L2_ffn_b_ih': 2.716,
     'L2_ffn_b_sel': 3.625,
     'L3_ffn_w_q': 8.0,
     'L3_ffn_keys': 8.0,
     'L3_ffn_weight_down_embed': 8.0,
     'L3_ffn_weight_up_embed': 8.0}
    for name, (base, spread) in spreads.items():
        noise = np.random.default_rng([zlib.crc32(name.encode()), seed]).standard_normal(out[name].shape)
        drawn = base * np.exp(spread * noise) if base else spread * noise
        out[name] = jnp.asarray(drawn.astype(out[name].dtype))
    for name, factor in factors.items():
        out[name] = (out[name] * factor).astype(out[name].dtype)
    return out
```

```python
from contextlib import ExitStack

import numpy as np

import concourse.bass as bass
from concourse import mybir

F32 = mybir.dt.float32
F16 = mybir.dt.float16
BF16 = mybir.dt.bfloat16
I32 = mybir.dt.int32
U32 = mybir.dt.uint32
ALU = mybir.AluOpType
ACT = mybir.ActivationFunctionType
X_AXIS = mybir.AxisListType.X
ds = bass.ds

N = 625
D = 512
NT, TN = 5, 125
KC = D // 128
E = 20000
TE = 125
ET = E // TE
UNIT = 2 * TE
UNITS = E // UNIT
LN_EPS = 1e-5
HALVES = ((0, 313), (313, 312))
BANK = 512
EXPERTS, EXPERT_F = 8, 128
MUL, HIDDEN, RADIAL = 128, 64, 8
SILU_2MOM = 1.679177
CELLS, GATES = 4, 4 * D
CELL_COLS = 2 * KC * GATES
PAD_LOGIT = -1e30
HEADS, KEY, KEYS, TOPK = 8, 32, 256, 16
SENTINEL = -3e38


LIVE = []


def new_semaphore(nc, name):
    sem = nc.alloc_semaphore(name)
    LIVE.append(sem)
    return sem


def end_of_layer(nc):
    nc.clear_and_free_semaphores(LIVE)
    LIVE.clear()
    nc.all_engine_barrier()


def linker(eng, sem):
    count = [0]

    def link(ins):
        count[0] += 1
        ins.then_inc(sem, 1)
        eng.wait_ge(sem, count[0])

    return link


def load_all(nc, name, pairs):
    loaded = new_semaphore(nc, name + "_loaded")
    with nc.Block() as block:
        @block.sync
        def _(sp):
            for dst, src in pairs:
                sp.dma_start(dst, src).then_inc(loaded, 16)
            sp.wait_ge(loaded, 16 * len(pairs))


def stage_constants(nc, x_in, x, ident, ones, iota):
    loaded = new_semaphore(nc, "x_loaded")
    made = new_semaphore(nc, "constants_made")
    with nc.Block() as block:
        @block.sync
        def _(sp):
            sp.dma_start(x[:], x_in.rearrange("(i p) d -> p i d", p=TN)).then_inc(loaded, 16)
            sp.wait_ge(loaded, 16)

        @block.gpsimd
        def _(g):
            nc.gpsimd.memset(ident[:], 0.0).then_inc(made, 1)
            nc.gpsimd.memset(ones[:], 1.0).then_inc(made, 1)
            g.wait_ge(made, 2)
            nc.gpsimd.affine_select(out=ident[:], in_=ident[:], compare_op=ALU.not_equal, fill=1.0, base=0,
                                    pattern=[[-1, 128]], channel_multiplier=1).then_inc(made, 1)
            nc.gpsimd.iota(iota[:], pattern=[[1, N]], base=0, channel_multiplier=0).then_inc(made, 1)
            g.wait_ge(made, 4)


def stage_graph(nc, src_in, dst_in, dst_rows_in, iota, ident, ones, src_i, dst_f, adj, count, dis, rcount, bounds):
    RING = 4
    pieces = []
    for i in range(NT):
        at, end = i * N, (i + 1) * N
        while at < end:
            n = min(end, (at // BANK + 1) * BANK) - at
            pieces.append((at, i, at - i * N, n))
            at += n
    with ExitStack() as ctx:
        def sb(name, shape, dt):
            return ctx.enter_context(nc.sbuf_tensor(name, shape, dt))
        dst_i = sb("dst_i", [TE, ET], I32)
        src_f = sb("src_f", [TE, ET], F32)
        iota_h = sb("iota_h", [128, N], F16)
        zeros = sb("zeros_h", [128, BANK], F16)
        hot_s = [sb(f"hot_s{r}", [TE, N], F16) for r in range(RING)]
        hot_d = [sb(f"hot_d{r}", [TE, N], F16) for r in range(RING)]
        rows_i = sb("rows_i", [UNITS, UNIT], I32)
        rows_f = sb("rows_f", [UNITS, UNIT], F32)
        tile_of = sb("tile_of", [UNITS, UNIT], F32)
        hit = sb("hit", [UNITS, UNIT], F32)
        anyhit = sb("anyhit", [UNITS, NT], F32)
        unit_no = sb("unit_no", [UNITS, 1], F32)
        unit_i = sb("unit_i", [UNITS, 1], I32)
        unit_up = sb("unit_up", [UNITS, 1], F32)
        unit_dn = sb("unit_dn", [UNITS, 1], F32)
        votes = sb("votes", [UNITS, 2 * NT], F32)
        best = sb("vote_best", [2 * NT, 1], F32)
        row = sb("vote_row", [1, 2 * NT], F32)
        root = sb("deg_root", [TN, NT], F32)
        t1 = sb("deg_t1", [TN, NT], F32)
        t2 = sb("deg_t2", [TN, NT], F32)
        loaded = new_semaphore(nc, "edges_loaded")
        ready = new_semaphore(nc, "graph_ready")
        hots = new_semaphore(nc, "hots_ready")
        used = new_semaphore(nc, "hots_used")
        zeroed = new_semaphore(nc, "adj_zeroed")
        unit_made = new_semaphore(nc, "unit_made")
        step = new_semaphore(nc, "graph_dve_step")
        with nc.psum_tensor("ps_adj", [128, 8 * BANK], F32) as ps:
            with nc.Block() as block:
                @block.sync
                def _(sp):
                    sp.dma_start(src_i[:], src_in).then_inc(loaded, 16)
                    sp.dma_start(dst_i[:], dst_in).then_inc(loaded, 16)
                    sp.dma_start(rows_i[:], dst_rows_in).then_inc(loaded, 16)
                    sp.wait_ge(loaded, 48)

                @block.gpsimd
                def _(g):
                    nc.gpsimd.iota(unit_i[:], pattern=[[1, 1]], base=0, channel_multiplier=1).then_inc(unit_made, 1)

                @block.vector
                def _(v):
                    link = linker(v, step)
                    v.wait_ge(loaded, 48)
                    link(nc.vector.tensor_copy(src_f[:], src_i[:]))
                    link(nc.vector.tensor_copy(dst_f[:], dst_i[:]))
                    link(nc.vector.tensor_copy(rows_f[:], rows_i[:]))
                    link(nc.vector.tensor_copy(iota_h[:], iota[:]))
                    link(nc.vector.memset(zeros[:], 0.0))
                    v.sem_inc(ready, 1)
                    with v.Fori(0, ET // RING) as i:
                        for r in range(RING):
                            v.wait_ge(used, i * RING + (r + 1))
                            nc.vector.tensor_scalar(hot_s[r][:], iota_h[0:TE, :], src_f[:, ds(i * RING + r, 1)], None, ALU.is_equal).then_inc(hots, 1)
                            nc.vector.tensor_scalar(hot_d[r][:], iota_h[0:TE, :], dst_f[:, ds(i * RING + r, 1)], None, ALU.is_equal).then_inc(hots, 1)
                    v.wait_ge(unit_made, 1)
                    link(nc.vector.tensor_copy(unit_no[:], unit_i[:]))
                    link(nc.vector.tensor_scalar(unit_up[:], unit_no[:], 1.0, None, ALU.add))
                    link(nc.vector.tensor_scalar(unit_dn[:], unit_no[:], -1.0, float(UNITS), ALU.mult, ALU.add))
                    link(nc.vector.tensor_scalar(tile_of[:], rows_f[:], float(TN), None, ALU.is_ge))
                    for j in range(2, NT):
                        link(nc.vector.scalar_tensor_tensor(tile_of[:], rows_f[:], float(TN * j), tile_of[:], ALU.is_ge, ALU.add))
                    for j in range(NT):
                        link(nc.vector.tensor_scalar(hit[:], tile_of[:], float(j), None, ALU.is_equal))
                        link(nc.vector.tensor_reduce(anyhit[:, j:j + 1], hit[:], X_AXIS, ALU.max))
                    link(nc.vector.tensor_scalar(votes[:, 0:NT], anyhit[:], unit_dn[:], None, ALU.mult))
                    link(nc.vector.tensor_scalar(votes[:, NT:2 * NT], anyhit[:], unit_up[:], None, ALU.mult))
                    v.wait_ge(used, ET + RING)
                    for i in range(NT):
                        link(nc.vector.tensor_copy(adj[:, i, :], ps[0:TN, i * N:(i + 1) * N]))
                    v.sem_inc(ready, 1)
                    v.wait_ge(zeroed, 1)
                    link(nc.vector.tensor_reduce(best[:], ps[0:2 * NT, 0:UNITS], X_AXIS, ALU.max))
                    v.sem_inc(ready, 1)
                    v.wait_ge(zeroed, 2)
                    link(nc.vector.tensor_copy(row[:], ps[0:1, BANK:BANK + 2 * NT]))
                    link(nc.vector.tensor_scalar(row[:, 0:NT], row[:, 0:NT], -1.0, float(UNITS), ALU.mult, ALU.add))
                    link(nc.vector.tensor_scalar(row[:, 0:NT], row[:, 0:NT], float(UNITS - 1), None, ALU.min))
                    link(nc.vector.tensor_tensor(row[:, NT:2 * NT], row[:, NT:2 * NT], row[:, 0:NT], ALU.subtract))
                    link(nc.vector.tensor_scalar(row[:, NT:2 * NT], row[:, NT:2 * NT], 1.0, None, ALU.max))
                    link(nc.vector.tensor_copy(bounds[:], row[:]))
                    link(nc.vector.tensor_copy(count[:], ps[0:TN, 2 * BANK:2 * BANK + NT]))
                    link(nc.vector.tensor_scalar(t1[:], count[:], 1.0, None, ALU.max))
                    link(nc.vector.reciprocal(rcount[:], t1[:]))
                    link(nc.vector.tensor_scalar(t1[:], count[:], 1.0, None, ALU.add))
                    v.sem_inc(ready, 1)
                    v.wait_ge(zeroed, 3)
                    link(nc.vector.reciprocal(dis[:], root[:]))
                    newton_rsqrt(nc, link, dis[:], t1[:], t2[:])
                    for i in range(NT):
                        link(nc.vector.tensor_tensor(adj[:, i, i * TN:(i + 1) * TN], adj[:, i, i * TN:(i + 1) * TN], ident[0:TN, 0:TN], ALU.add))

                @block.scalar
                def _(a):
                    a.wait_ge(ready, 4)
                    nc.scalar.activation(root[:], t1[:], ACT.Sqrt).then_inc(zeroed, 1)

                @block.tensor
                def _(pe):
                    pe.wait_ge(ready, 1)
                    for b in range(7):
                        m = nc.tensor.matmul(ps[0:TN, b * BANK:(b + 1) * BANK], zeros[:, 0:TN], zeros[:], start=True, stop=False, skip_group_check=True)
                    m.then_inc(used, RING)
                    with pe.Fori(0, ET // RING) as i:
                        for r in range(RING):
                            pe.wait_ge(hots, i * (2 * RING) + (2 * r + 2))
                            for at, s, d0, n in pieces:
                                m = nc.tensor.matmul(ps[0:TN, at:at + n], hot_s[r][:, s * TN:(s + 1) * TN], hot_d[r][:, d0:d0 + n], start=False, stop=True, skip_group_check=True)
                            m.then_inc(used, 1)
                    pe.wait_ge(ready, 2)
                    nc.tensor.transpose(ps[0:2 * NT, 0:UNITS], votes[:], ident[0:UNITS, 0:UNITS]).then_inc(zeroed, 1)
                    pe.wait_ge(ready, 3)
                    nc.tensor.transpose(ps[0:1, BANK:BANK + 2 * NT], best[:], ident[0:2 * NT, 0:2 * NT])
                    for j in range(NT):
                        for s in range(NT):
                            m = nc.tensor.matmul(ps[0:TN, 2 * BANK + j:2 * BANK + j + 1], adj[:, s, j * TN:(j + 1) * TN], ones[0:TN, :], start=(s == 0), stop=(s == NT - 1), skip_group_check=True)
                    m.then_inc(zeroed, 1)


def newton_rsqrt(nc, link, r, v, t):
    link(nc.vector.tensor_tensor(t, r, r, ALU.mult))
    link(nc.vector.tensor_tensor(t, t, v, ALU.mult))
    link(nc.vector.tensor_scalar(t, t, -0.5, 1.5, ALU.mult, ALU.add))
    link(nc.vector.tensor_tensor(r, r, t, ALU.mult))


def stage_layernorm(nc, tag, ident, x, xn, xt=None, chunk=None, tiles=NT):
    chunk = chunk or (lambda c: slice(c * 128, (c + 1) * 128))
    with ExitStack() as ctx:
        stats = ctx.enter_context(nc.sbuf_tensor(tag + "_stats", [TN, tiles, 6], F32))
        mv = ctx.enter_context(nc.sbuf_tensor(tag + "_mv", [TN, tiles, 2], F32))
        var = ctx.enter_context(nc.sbuf_tensor(tag + "_var", [TN, tiles], F32))
        root = ctx.enter_context(nc.sbuf_tensor(tag + "_root", [TN, tiles], F32))
        r = ctx.enter_context(nc.sbuf_tensor(tag + "_r", [TN, tiles], F32))
        t = ctx.enter_context(nc.sbuf_tensor(tag + "_t", [TN, tiles], F32))
        ps = [ctx.enter_context(nc.psum_tensor(f"{tag}_ps{b}", [128, BANK], F32)) for b in range(2)]
        step = new_semaphore(nc, tag + "_step")
        var_ready = new_semaphore(nc, tag + "_var_ready")
        rooted = new_semaphore(nc, tag + "_rooted")
        normed = new_semaphore(nc, tag + "_normed")
        turned = new_semaphore(nc, tag + "_turned")
        moved = new_semaphore(nc, tag + "_moved")
        with nc.Block() as block:
            @block.vector
            def _(v):
                link = linker(v, step)
                for i in range(tiles):
                    last = nc.vector.bn_stats(stats[:, i, :], x[:, i, :])
                link(last)
                for i in range(tiles):
                    last = nc.vector.bn_aggr(mv[:, i, :], stats[:, i, :])
                link(last)
                nc.vector.tensor_scalar(var[:], mv[:, :, 1], LN_EPS, None, ALU.add).then_inc(var_ready, 1)
                v.wait_ge(rooted, 1)
                link(nc.vector.reciprocal(r[:], root[:]))
                newton_rsqrt(nc, link, r[:], var[:], t[:])
                for i in range(tiles):
                    nc.vector.tensor_scalar(xn[:, i, :], x[:, i, :], mv[:, i, 0:1], r[:, i:i + 1], ALU.subtract, ALU.mult).then_inc(normed, 1)

            @block.scalar
            def _(a):
                a.wait_ge(var_ready, 1)
                nc.scalar.activation(root[:], var[:], ACT.Sqrt).then_inc(rooted, 1)
                if xt is not None:
                    for i in range(tiles):
                        a.wait_ge(turned, i + 1)
                        nc.scalar.copy(xt[:, :, i * TN:(i + 1) * TN], ps[i % 2][:, 0:KC * TN].rearrange("p (c n) -> p c n", c=KC)).then_inc(moved, 1)

            if xt is not None:
                @block.tensor
                def _(pe):
                    for i in range(tiles):
                        pe.wait_ge(normed, i + 1)
                        if i >= 2:
                            pe.wait_ge(moved, i - 1)
                        for c in range(KC):
                            m = nc.tensor.transpose(ps[i % 2][:, c * TN:(c + 1) * TN], xn[:, i, chunk(c)], ident[0:TN, 0:TN])
                        m.then_inc(turned, 1)


def stage_aggregate(nc, tag, src, adj, out_t):
    with ExitStack() as ctx:
        ps = [ctx.enter_context(nc.psum_tensor(f"{tag}_ps{b}", [128, BANK], F32)) for b in range(4)]
        summed = new_semaphore(nc, tag + "_summed")
        moved = new_semaphore(nc, tag + "_moved")
        jobs = [(c, at, n) for c in range(KC) for at, n in HALVES]
        with nc.Block() as block:
            @block.tensor
            def _(pe):
                for k, (c, at, n) in enumerate(jobs):
                    if k >= 4:
                        pe.wait_ge(moved, k - 3)
                    for s in range(NT):
                        m = nc.tensor.matmul(ps[k % 4][:, 0:n], src[:, s, c * 128:(c + 1) * 128], adj[:, s, at:at + n], start=(s == 0), stop=(s == NT - 1))
                    m.then_inc(summed, 1)

            @block.scalar
            def _(a):
                for k, (c, at, n) in enumerate(jobs):
                    a.wait_ge(summed, k + 1)
                    nc.scalar.copy(out_t[:, c, at:at + n], ps[k % 4][:, 0:n]).then_inc(moved, 1)


def stage_scale_rows(nc, tag, out, x, col):
    done = new_semaphore(nc, tag + "_scaled")
    with nc.Block() as block:
        @block.vector
        def _(v):
            for i in range(NT):
                nc.vector.tensor_scalar(out[:, i, :], x[:, i, :], col[:, i:i + 1], None, ALU.mult).then_inc(done, 1)
            v.wait_ge(done, NT)


def stage_gcn_project(nc, tag, z_t, w, bias, dis, out, x):
    with ExitStack() as ctx:
        tmp = [ctx.enter_context(nc.sbuf_tensor(f"{tag}_tmp{b}", [TN, D], F32)) for b in range(2)]
        ps = [ctx.enter_context(nc.psum_tensor(f"{tag}_ps{b}", [128, BANK], F32)) for b in range(2)]
        ready = new_semaphore(nc, tag + "_ready")
        read = new_semaphore(nc, tag + "_read")
        done = new_semaphore(nc, tag + "_done")
        with nc.Block() as block:
            @block.tensor
            def _(pe):
                for i in range(NT):
                    if i >= 2:
                        pe.wait_ge(read, i - 1)
                    for c in range(KC):
                        m = nc.tensor.matmul(ps[i % 2][0:TN, :], z_t[:, c, i * TN:(i + 1) * TN], w[:, c, :], start=(c == 0), stop=(c == KC - 1))
                    m.then_inc(ready, 1)

            @block.vector
            def _(v):
                for i in range(NT):
                    v.wait_ge(ready, i + 1)
                    nc.vector.scalar_tensor_tensor(tmp[i % 2][:], ps[i % 2][0:TN, :], dis[:, i:i + 1], bias[:], ALU.mult, ALU.add).then_inc(read, 1)
                    v.wait_ge(read, i + 1)
                    if out is not None:
                        nc.vector.tensor_scalar(out[:, i, :], tmp[i % 2][:], 0.0, dis[:, i:i + 1], ALU.max, ALU.mult).then_inc(done, 1)
                    else:
                        nc.vector.tensor_tensor(x[:, i, :], x[:, i, :], tmp[i % 2][:], ALU.add).then_inc(done, 1)
                v.wait_ge(done, NT)


def rows(vec, parts):
    return vec.broadcast_to([parts, vec.shape[1]])


def layer_gcn(nc, x, ident, adj, dis, w1_in, b1_in, w2_in, b2_in):
    with ExitStack() as ctx:
        def sb(name, shape):
            return ctx.enter_context(nc.sbuf_tensor(name, shape, F32))
        w1, w2 = sb("gcn_w1", [128, KC, D]), sb("gcn_w2", [128, KC, D])
        b1, b2 = sb("gcn_b1", [TN, D]), sb("gcn_b2", [TN, D])
        xn, h, z_t = sb("gcn_xn", [TN, NT, D]), sb("gcn_h", [TN, NT, D]), sb("gcn_zt", [128, KC, N])
        load_all(nc, "gcn", [(w1[:], w1_in.rearrange("(c k) n -> k c n", k=128)), (w2[:], w2_in.rearrange("(c k) n -> k c n", k=128)),
                             (b1[:], rows(b1_in, TN)), (b2[:], rows(b2_in, TN))])
        stage_layernorm(nc, "gcn_ln", ident, x, xn)
        stage_scale_rows(nc, "gcn_xs", h, xn, dis)
        stage_aggregate(nc, "gcn_a1", h, adj, z_t)
        stage_gcn_project(nc, "gcn_p1", z_t, w1, b1, dis, h, None)
        stage_aggregate(nc, "gcn_a2", h, adj, z_t)
        stage_gcn_project(nc, "gcn_p2", z_t, w2, b2, dis, None, x)


def layer_experts(nc, x, ident, ones, ws_in, bs_in, w1_in, b1_in, w2_in, b2_in):
    with ExitStack() as ctx:
        def sb(name, shape, dt=F32):
            return ctx.enter_context(nc.sbuf_tensor(name, shape, dt))
        ws, bs = sb("moe_ws", [128, KC, EXPERTS]), sb("moe_bs", [TN, EXPERTS])
        w1, b1 = sb("moe_w1", [128, EXPERTS, KC, EXPERT_F]), sb("moe_b1", [128, EXPERTS])
        w2, b2 = sb("moe_w2", [128, EXPERTS, D]), sb("moe_b2", [1, EXPERTS, D])
        xn, xt = sb("moe_xn", [TN, NT, D]), sb("moe_xt", [128, KC, N])
        lg, mx = sb("moe_logits", [TN, NT, EXPERTS]), sb("moe_max", [TN, NT, 8])
        at, atf = sb("moe_at", [TN, NT, 8], U32), sb("moe_atf", [TN, NT])
        neg, total, pmax = sb("moe_neg", [TN, NT]), sb("moe_sum", [TN, NT]), sb("moe_pmax", [TN, NT])
        ex, gate = sb("moe_exp", [TN, NT, EXPERTS]), sb("moe_gate", [TN, NT, EXPERTS])
        no_i, no_f = sb("moe_no_i", [TN, EXPERTS], I32), sb("moe_no", [TN, EXPERTS])
        onesrow = sb("moe_ones", [1, TN])
        h_t = [sb(f"moe_h{b}", [128, N]) for b in range(2)]
        load_all(nc, "moe", [(ws[:], ws_in.rearrange("(c k) e -> k c e", k=128)), (bs[:], rows(bs_in, TN)),
                             (b1[:], b1_in), (w2[:], w2_in.rearrange("e f d -> f e d")), (b2[:], b2_in.rearrange("e d -> (e d)").rearrange("(a e d) -> a e d", a=1, d=D))]
                 + [(w1[:, e], w1_in[e].rearrange("(c k) f -> k c f", k=128)) for e in range(EXPERTS)])
        stage_layernorm(nc, "moe_ln", ident, x, xn, xt)
        ps_l = ctx.enter_context(nc.psum_tensor("moe_psl", [128, BANK], F32))
        ps_h = [ctx.enter_context(nc.psum_tensor(f"moe_psh{b}", [128, BANK], F32)) for b in range(2)]
        ps_y = [ctx.enter_context(nc.psum_tensor(f"moe_psy{b}", [128, BANK], F32)) for b in range(4)]
        S = {k: new_semaphore(nc, "moe_" + k) for k in ("step", "no_made", "lg_ready", "neg_ready", "exp_ready", "h_raw", "h_ready", "y_ready", "y_used")}
        with nc.Block() as block:
            @block.gpsimd
            def _(g):
                nc.gpsimd.iota(no_i[:], pattern=[[1, EXPERTS]], base=0, channel_multiplier=0).then_inc(S["no_made"], 1)
                nc.gpsimd.memset(onesrow[:], 1.0).then_inc(S["no_made"], 1)

            @block.tensor
            def _(pe):
                for i in range(NT):
                    for c in range(KC):
                        m = nc.tensor.matmul(ps_l[0:TN, i * EXPERTS:(i + 1) * EXPERTS], xt[:, c, i * TN:(i + 1) * TN], ws[:, c, :], start=(c == 0), stop=(c == KC - 1), skip_group_check=True)
                m.then_inc(S["lg_ready"], 1)
                pe.wait_ge(S["no_made"], 2)

                def up(e):
                    if e >= 1:
                        pe.wait_ge(S["h_ready"], 2 * e)
                    for b, (a0, n) in enumerate(HALVES):
                        for c in range(KC):
                            m = nc.tensor.matmul(ps_h[b][:, 0:n], w1[:, e, c, :], xt[:, c, a0:a0 + n], start=(c == 0), stop=(c == KC - 1))
                        m.then_inc(S["h_raw"], 1)

                def down(e):
                    pe.wait_ge(S["h_ready"], 2 * e + 2)
                    for i in range(NT):
                        k = e * NT + i
                        if k >= 4:
                            pe.wait_ge(S["y_used"], k - 3)
                        nc.tensor.matmul(ps_y[k % 4][0:TN, :], onesrow[:], b2[:, e, :], start=True, stop=False)
                        nc.tensor.matmul(ps_y[k % 4][0:TN, :], h_t[e % 2][:, i * TN:(i + 1) * TN], w2[:, e, :], start=False, stop=True).then_inc(S["y_ready"], 1)

                up(0)
                for e in range(EXPERTS):
                    if e + 1 < EXPERTS:
                        up(e + 1)
                    down(e)

            @block.scalar
            def _(a):
                a.wait_ge(S["neg_ready"], 1)
                for i in range(NT):
                    last = nc.scalar.activation(ex[:, i, :], lg[:, i, :], ACT.Exp, bias=neg[:, i:i + 1], accum_out=total[:, i:i + 1])
                last.then_inc(S["exp_ready"], 1)
                for e in range(EXPERTS):
                    if e >= 2:
                        a.wait_ge(S["y_ready"], (e - 1) * NT)
                    for b, (a0, n) in enumerate(HALVES):
                        a.wait_ge(S["h_raw"], 2 * e + b + 1)
                        nc.scalar.activation(h_t[e % 2][:, a0:a0 + n], ps_h[b][:, 0:n], ACT.Gelu, bias=b1[:, e:e + 1]).then_inc(S["h_ready"], 1)

            @block.vector
            def _(v):
                link = linker(v, S["step"])
                v.wait_ge(S["no_made"], 1)
                link(nc.vector.tensor_copy(no_f[:], no_i[:]))
                v.wait_ge(S["lg_ready"], 1)
                for i in range(NT):
                    link(nc.vector.tensor_tensor(lg[:, i, :], ps_l[0:TN, i * EXPERTS:(i + 1) * EXPERTS], bs[:], ALU.add))
                    link(nc.vector.max(mx[:, i, :], lg[:, i, :]))
                    link(nc.vector.max_index(at[:, i, :], mx[:, i, :], lg[:, i, :]))
                link(nc.vector.tensor_scalar(neg[:], mx[:, :, 0], -1.0, None, ALU.mult))
                v.sem_inc(S["neg_ready"], 1)
                link(nc.vector.tensor_copy(atf[:], at[:, :, 0]))
                v.wait_ge(S["exp_ready"], 1)
                link(nc.vector.reciprocal(pmax[:], total[:]))
                for i in range(NT):
                    link(nc.vector.tensor_scalar(gate[:, i, :], no_f[:], atf[:, i:i + 1], pmax[:, i:i + 1], ALU.is_equal, ALU.mult))
                for e in range(EXPERTS):
                    for i in range(NT):
                        v.wait_ge(S["y_ready"], e * NT + i + 1)
                        if e >= 1:
                            v.wait_ge(S["y_used"], (e - 1) * NT + i + 1)
                        nc.vector.scalar_tensor_tensor(x[:, i, :], ps_y[(e * NT + i) % 4][0:TN, :], gate[:, i, e:e + 1], x[:, i, :], ALU.mult, ALU.add).then_inc(S["y_used"], 1)


def stage_edge_mlp(nc, feats_in, w1_in, w2_in, w3_in, h3_dram):
    CH = 500
    PAIRS = E // CH // 2
    with ExitStack() as ctx:
        def sb(name, shape, dt=F32):
            return ctx.enter_context(nc.sbuf_tensor(name, shape, dt))
        w1, w2, w3 = sb("mlp_w1", [RADIAL, HIDDEN]), sb("mlp_w2", [HIDDEN, HIDDEN]), sb("mlp_w3", [HIDDEN, HIDDEN])
        f = [sb(f"mlp_f{b}", [RADIAL, CH]) for b in range(2)]
        h = [[sb(f"mlp_h{b}{l}", [HIDDEN, CH]) for l in range(3)] for b in range(2)]
        ps = [[ctx.enter_context(nc.psum_tensor(f"mlp_ps{b}{l}", [128, BANK], F32)) for l in range(3)] for b in range(2)]
        load_all(nc, "mlp", [(w1[:], w1_in), (w2[:], w2_in), (w3[:], w3_in)])
        fed = [new_semaphore(nc, f"mlp_fed{b}") for b in range(2)]
        stored = [new_semaphore(nc, f"mlp_stored{b}") for b in range(2)]
        raw = [new_semaphore(nc, f"mlp_raw{b}") for b in range(2)]
        acted = [new_semaphore(nc, f"mlp_acted{b}") for b in range(2)]
        seen = new_semaphore(nc, "mlp_seen")
        scales = (1 / RADIAL ** 0.5, SILU_2MOM / HIDDEN ** 0.5, SILU_2MOM / HIDDEN ** 0.5)
        with nc.Block() as block:
            @block.sync
            def _(sp):
                with sp.Fori(0, PAIRS) as i:
                    for b in range(2):
                        sp.wait_ge(acted[b], i * 3 + 1)
                        sp.dma_start(f[b][:], feats_in[:, ds(i * (2 * CH) + b * CH, CH)]).then_inc(fed[b], 16)
                    for b in range(2):
                        sp.wait_ge(acted[b], i * 3 + 4)
                        sp.dma_start(h3_dram[:, ds(i * (2 * CH) + b * CH, CH)], h[b][2][:]).then_inc(stored[b], 16)
                for b in range(2):
                    sp.wait_ge(stored[b], 16 * PAIRS + 16)

            @block.tensor
            def _(pe):
                with pe.Fori(0, PAIRS) as i:
                    for l in range(3):
                        for b in range(2):
                            if l == 0:
                                pe.wait_ge(fed[b], i * 16 + 16)
                            pe.wait_ge(acted[b], i * 3 + (l + 1))
                            pe.sem_inc(seen, 1)
                            nc.tensor.matmul(ps[b][l][0:HIDDEN, 0:CH], (w1, w2, w3)[l][:], f[b][:] if l == 0 else h[b][l - 1][:], start=True, stop=True).then_inc(raw[b], 1)

            @block.scalar
            def _(a):
                for b in range(2):
                    a.sem_inc(acted[b], 1)
                    a.sem_inc(stored[b], 16)
                with a.Fori(0, PAIRS) as i:
                    for l in range(3):
                        for b in range(2):
                            a.wait_ge(raw[b], i * 3 + (l + 1))
                            if l == 2:
                                a.wait_ge(stored[b], i * 16 + 16)
                            nc.scalar.activation(h[b][l][:], ps[b][l][0:HIDDEN, 0:CH], ACT.Silu, scale=scales[l]).then_inc(acted[b], 1)


def stage_up(nc, xt, up0_in, up1_in, up_dram):
    with ExitStack() as ctx:
        w0 = ctx.enter_context(nc.sbuf_tensor("up_w0", [MUL, MUL], F32))
        w1 = ctx.enter_context(nc.sbuf_tensor("up_w1", [MUL, MUL], F32))
        up = ctx.enter_context(nc.sbuf_tensor("up_rows", [TN, NT, D], F32))
        ps = [ctx.enter_context(nc.psum_tensor(f"up_ps{b}", [128, BANK], F32)) for b in range(NT)]
        load_all(nc, "up", [(w0[:], up0_in), (w1[:], up1_in)])
        ready, moved, stored = (new_semaphore(nc, "up_" + k) for k in ("ready", "moved", "stored"))
        with nc.Block() as block:
            @block.tensor
            def _(pe):
                for i in range(NT):
                    for c in range(4):
                        m = nc.tensor.matmul(ps[i][0:TN, c * MUL:(c + 1) * MUL], xt[:, c, i * TN:(i + 1) * TN], (w0 if c == 0 else w1)[:], start=True, stop=True, skip_group_check=True)
                    m.then_inc(ready, 1)

            @block.vector
            def _(v):
                for i in range(NT):
                    v.wait_ge(ready, i + 1)
                    nc.vector.tensor_scalar(up[:, i, :], ps[i][0:TN, :], MUL ** -0.5, None, ALU.mult).then_inc(moved, 1)

            @block.sync
            def _(sp):
                sp.wait_ge(moved, NT)
                sp.dma_start(up_dram.rearrange("(i p) d -> p i d", p=TN), up[:]).then_inc(stored, 16)
                sp.wait_ge(stored, 16)


def stage_messages(nc, j, up_dram, h3_dram, w4, src_i, dst_f, y, y3, iota, zeros, bounds, msg):
    tag = f"msg{j}"
    with ExitStack() as ctx:
        def sb(name, shape, dt=F32):
            return ctx.enter_context(nc.sbuf_tensor(f"{tag}_{name}", shape, dt))
        idx = [sb(f"idx{a}", [TE, 1], I32) for a in range(2)]
        snd = [sb(f"snd{a}", [TE, D]) for a in range(2)]
        h3 = [sb(f"h3{a}", [HIDDEN, UNIT]) for a in range(2)]
        hot = [sb(f"hot{a}", [TE, TN]) for a in range(2)]
        ws0 = [sb(f"ws0{a}", [TE, MUL]) for a in range(2)]
        dot = sb("dot", [TE, MUL])
        m = [sb(f"m{a}", [TE, 1024]) for a in range(2)]
        ps_w = [ctx.enter_context(nc.psum_tensor(f"{tag}_psw{a}", [128, BANK], F32)) for a in range(2)]
        acc = [ctx.enter_context(nc.psum_tensor(f"{tag}_acc{a}", [128, BANK], F32)) for a in range(2)]
        S = {k: new_semaphore(nc, f"{tag}_{k}") for k in ("hot", "tpw", "wused", "ws0", "dot", "vec", "p2", "summed", "idx", "out", "seen")}
        h3_in = new_semaphore(nc, f"{tag}_h3_in")
        snd_in = [new_semaphore(nc, f"{tag}_snd_in{a}") for a in range(2)]
        first_max, count_max = UNITS - 1, UNITS

        def bound(eng, k, lo, hi):
            return eng.snap(eng.value_load(bounds[0:1, k:k + 1], min_val=lo, max_val=hi), min_val=lo, max_val=hi)

        with nc.Block() as block:
            @block.sync
            def _(sp):
                first, count = bound(sp, j, 0, first_max), bound(sp, NT + j, 1, count_max)
                with sp.Fori(0, count) as i:
                    unit = nc.s_assert_within(first + i, 0, first_max, skip_runtime_bounds_check_because="first + count is at most the number of units")
                    sp.wait_ge(S["tpw"], i * 2 + 2)
                    sp.dma_start(h3[0][:], h3_dram[:, ds(unit * UNIT, UNIT)]).then_inc(h3_in, 16)

            @block.gpsimd
            def _(g):
                first, count = bound(g, j, 0, first_max), bound(g, NT + j, 1, count_max)
                with g.Fori(0, count) as i:
                    unit = nc.s_assert_within(first + i, 0, first_max, skip_runtime_bounds_check_because="first + count is at most the number of units")
                    for a in range(2):
                        g.wait_ge(S["p2"], i * 2 + (a + 1))
                        g.wait_ge(S["vec"], i * 2 + (a + 1))
                        nc.gpsimd.tensor_copy(idx[a][:], src_i[:, ds(unit * 2 + a, 1)]).then_inc(S["idx"], 1)
                        g.wait_ge(S["idx"], i * 2 + (a + 1))
                        g.sem_inc(S["seen"], 1)
                        nc.gpsimd.indirect_dma_start(out=snd[a][:], out_offset=None, in_=up_dram,
                                                     in_offset=bass.IndirectOffsetOnAxis(ap=idx[a][:].bitcast(U32), axis=0)).then_inc(snd_in[a], 16)

            @block.tensor
            def _(pe):
                count = bound(pe, NT + j, 1, count_max)
                for b in range(2):
                    nc.tensor.matmul(acc[b][0:TN, :], zeros[:, 0:TN], zeros[:], start=True, stop=False, skip_group_check=True)
                pe.sem_inc(S["tpw"], 2)
                with pe.Fori(0, count) as i:
                    pe.wait_ge(h3_in, i * 16 + 16)
                    for a in range(2):
                        pe.wait_ge(S["wused"], i * 2 + (a + 1))
                        nc.tensor.matmul(ps_w[a][0:TE, :], h3[0][:, a * TE:(a + 1) * TE], w4[:], start=True, stop=True).then_inc(S["tpw"], 1)
                    for a in range(2):
                        pe.wait_ge(S["vec"], i * 2 + (a + 3))
                        pe.wait_ge(S["p2"], i * 2 + (a + 3))
                        for b in range(2):
                            mm = nc.tensor.matmul(acc[b][0:TN, :], hot[a][:], m[a][:, b * BANK:(b + 1) * BANK], start=False, stop=True, skip_group_check=True)
                        mm.then_inc(S["summed"], 1)

            @block.scalar
            def _(s):
                first, count = bound(s, j, 0, first_max), bound(s, NT + j, 1, count_max)
                s.sem_inc(S["p2"], 2)
                with s.Fori(0, count) as i:
                    unit = nc.s_assert_within(first + i, 0, first_max, skip_runtime_bounds_check_because="first + count is at most the number of units")
                    for a in range(2):
                        s.wait_ge(S["ws0"], i * 2 + (a + 1))
                        s.wait_ge(S["summed"], i * 2 + (a + 1))
                        for k, at in enumerate((256, 512, 768)):
                            last = nc.scalar.activation(m[a][:, at:at + 128], ws0[a][:], ACT.Copy, scale=y[:, ds(unit * 8 + (a * 4 + 1 + k), 1)])
                        last.then_inc(S["p2"], 1)

            @block.vector
            def _(v):
                first, count = bound(v, j, 0, first_max), bound(v, NT + j, 1, count_max)
                v.sem_inc(S["wused"], 2)
                v.sem_inc(S["vec"], 2)
                v.sem_inc(S["summed"], 2)
                with v.Fori(0, count) as i:
                    unit = nc.s_assert_within(first + i, 0, first_max, skip_runtime_bounds_check_because="first + count is at most the number of units")
                    for a in range(2):
                        wait = i * 2 + (a + 1)
                        y_at = lambda q: y[:, ds(unit * 8 + (a * 4 + q), 1)]
                        y3_at = lambda q: y3[:, ds(unit * 8 + (a * 4 + q), 1)]
                        w = lambda q: ps_w[a][0:TE, q * MUL:(q + 1) * MUL]
                        v.wait_ge(S["summed"], wait)
                        nc.vector.tensor_scalar(hot[a][:], iota[0:TE, j * TN:(j + 1) * TN], dst_f[:, ds(unit * 2 + a, 1)], None, ALU.is_equal).then_inc(S["hot"], 1)
                        v.wait_ge(snd_in[a], i * 16 + 16)
                        s0 = snd[a][:, 0:MUL]
                        s1 = lambda q: snd[a][:, MUL * (q + 1):MUL * (q + 2)]
                        nc.vector.tensor_scalar(dot[:], s1(0), y3_at(1), None, ALU.mult).then_inc(S["dot"], 1)
                        v.wait_ge(S["tpw"], i * 2 + (a + 3))
                        nc.vector.tensor_tensor(ws0[a][:], w(1), s0, ALU.mult).then_inc(S["ws0"], 1)
                        v.wait_ge(S["dot"], i * 6 + (3 * a + 1))
                        nc.vector.scalar_tensor_tensor(dot[:], s1(1), y3_at(2), dot[:], ALU.mult, ALU.add).then_inc(S["dot"], 1)
                        nc.vector.scalar_tensor_tensor(m[a][:, 0:128], w(0), y_at(0), s0, ALU.mult, ALU.mult).then_inc(S["out"], 1)
                        v.wait_ge(S["dot"], i * 6 + (3 * a + 2))
                        nc.vector.scalar_tensor_tensor(dot[:], s1(2), y3_at(3), dot[:], ALU.mult, ALU.add).then_inc(S["dot"], 1)
                        for q, at in enumerate((384, 640, 896)):
                            nc.vector.scalar_tensor_tensor(m[a][:, at:at + 128], w(2), y_at(0), s1(q), ALU.mult, ALU.mult).then_inc(S["out"], 1)
                        v.wait_ge(S["dot"], i * 6 + (3 * a + 3))
                        nc.vector.tensor_tensor(m[a][:, 128:256], w(3), dot[:], ALU.mult).then_inc(S["vec"], 1)
                        v.wait_ge(S["vec"], i * 2 + (a + 3))
                        v.sem_inc(S["wused"], 1)
                v.wait_ge(S["summed"], count * 2 + 2)
                for b in range(2):
                    nc.vector.tensor_copy(msg[:, j, b * BANK:(b + 1) * BANK], acc[b][0:TN, :]).then_inc(S["hot"], 1)


def stage_message_out(nc, msg, wo0_in, wo1_in, ident, x):
    with ExitStack() as ctx:
        w0 = ctx.enter_context(nc.sbuf_tensor("out_w0", [128, 2, MUL], F32))
        w1 = ctx.enter_context(nc.sbuf_tensor("out_w1", [128, 2, MUL], F32))
        mt = [ctx.enter_context(nc.sbuf_tensor(f"out_mt{b}", [128, 8, TN], F32)) for b in range(2)]
        ps_t = [ctx.enter_context(nc.psum_tensor(f"out_pst{b}", [128, BANK], F32)) for b in range(4)]
        ps_o = [ctx.enter_context(nc.psum_tensor(f"out_pso{b}", [128, BANK], F32)) for b in range(2)]
        load_all(nc, "mout", [(w0[:], wo0_in.rearrange("(c k) n -> k c n", k=128)), (w1[:], wo1_in.rearrange("(c k) n -> k c n", k=128))])
        turned, moved, ready, used = (new_semaphore(nc, "mout_" + k) for k in ("turned", "moved", "ready", "used"))
        scale = (2 * MUL) ** -0.5 / 10.0
        with nc.Block() as block:
            @block.tensor
            def _(pe):
                for i in range(NT):
                    for b in range(2):
                        k = 2 * i + b
                        if k >= 4:
                            pe.wait_ge(moved, k - 3)
                        for c in range(4):
                            m = nc.tensor.transpose(ps_t[k % 4][:, c * TN:(c + 1) * TN], msg[:, i, (4 * b + c) * 128:(4 * b + c + 1) * 128], ident[0:TN, 0:TN])
                        m.then_inc(turned, 1)
                    pe.wait_ge(moved, 2 * i + 2)
                    if i >= 2:
                        pe.wait_ge(used, i - 1)
                    for c in range(4):
                        for half in range(2):
                            m = nc.tensor.matmul(ps_o[i % 2][0:TN, c * MUL:(c + 1) * MUL], mt[i % 2][:, 2 * c + half, :], (w0 if c == 0 else w1)[:, half, :], start=(half == 0), stop=(half == 1), skip_group_check=True)
                    m.then_inc(ready, 1)

            @block.scalar
            def _(a):
                for i in range(NT):
                    if i >= 2:
                        a.wait_ge(ready, i - 1)
                    for b in range(2):
                        k = 2 * i + b
                        a.wait_ge(turned, k + 1)
                        nc.scalar.copy(mt[i % 2][:, 4 * b:4 * b + 4, :], ps_t[k % 4][:, 0:4 * TN].rearrange("p (c n) -> p c n", c=4)).then_inc(moved, 1)

            @block.vector
            def _(v):
                for i in range(NT):
                    v.wait_ge(ready, i + 1)
                    nc.vector.scalar_tensor_tensor(x[:, i, 0:MUL], ps_o[i % 2][0:TN, 0:MUL], scale, x[:, i, 0:MUL], ALU.mult, ALU.add)
                    vec = x[:, i, MUL:D].rearrange("p (u m) -> p m u", m=3)
                    nc.vector.scalar_tensor_tensor(vec, ps_o[i % 2][0:TN, MUL:D].rearrange("p (m u) -> p m u", m=3), scale, vec, ALU.mult, ALU.add).then_inc(used, 1)


def layer_tensor_product(nc, x, ident, iota, src_i, dst_f, bounds, attrs_in, feats_in, up0_in, up1_in, w1_in, w2_in, w3_in, w4_in,
                         wo0_in, wo1_in, up_dram, h3_dram):
    stage_edge_mlp(nc, feats_in, w1_in, w2_in, w3_in, h3_dram)
    with ExitStack() as ctx:
        def sb(name, shape, dt=F32):
            return ctx.enter_context(nc.sbuf_tensor(name, shape, dt))
        y, y3, w4 = sb("tp_y", [TE, ET * 4]), sb("tp_y3", [TE, ET * 4]), sb("tp_w4", [HIDDEN, D])
        xn, xt = sb("tp_xn", [TN, NT, D]), sb("tp_xt", [128, 4, N])
        zeros, msg, iota_f = sb("tp_zeros", [128, BANK]), sb("tp_msg", [TN, NT, 1024]), sb("tp_iota", [128, N])
        load_all(nc, "tp", [(y[:], attrs_in), (w4[:], w4_in)])
        stage_layernorm(nc, "tp_ln", ident, x, xn, xt, lambda c: slice(0, MUL) if c == 0 else slice(MUL + c - 1, D, 3))
        stage_up(nc, xt, up0_in, up1_in, up_dram)
        step = new_semaphore(nc, "tp_step")
        with nc.Block() as block:
            @block.vector
            def _(v):
                link = linker(v, step)
                link(nc.vector.tensor_scalar(y[:], y[:], SILU_2MOM / HIDDEN ** 0.5, None, ALU.mult))
                link(nc.vector.tensor_scalar(y3[:], y[:], 3.0 ** -0.5, None, ALU.mult))
                link(nc.vector.memset(zeros[:], 0.0))
                link(nc.vector.tensor_copy(iota_f[:], iota[:]))
        for j in range(NT):
            stage_messages(nc, j, up_dram, h3_dram, w4, src_i, dst_f, y, y3, iota_f, zeros, bounds, msg)
        stage_message_out(nc, msg, wo0_in, wo1_in, ident, x)


def layer_ode(nc, x, ident, ones, w1t_in, b1_in, w2t_in, b2_in, b2_row_in, w3_in, w3t_in, b3_in, b3_row_in, whh_in, whh):
    STEPS = N - 1
    DT = 1.0 / STEPS
    UN = 4
    CHUNK = GATES // 2
    with ExitStack() as ctx:
        def sb(name, shape, dt=F32):
            return ctx.enter_context(nc.sbuf_tensor(name, shape, dt))
        xn, xt = sb("ode_xn", [TN, 1, D]), sb("ode_xt", [128, KC, TN])
        w1t, w2t, w3, w3t = sb("ode_w1t", [128, KC, 128]), sb("ode_w2t", [128, 128]), sb("ode_w3", [128, KC, 128]), sb("ode_w3t", [128, D])
        b1, b2, b3, b3r = sb("ode_b1", [128, 1]), sb("ode_b2", [128, 1]), sb("ode_b3", [128, KC]), sb("ode_b3r", [1, D])
        mt_half, mt_full, mt_sixth = (sb("ode_mt" + k, [128, 128]) for k in ("_half", "_full", "_sixth"))
        m0h, m0f, z0, zh, zf = (sb("ode_" + k, [128, 1]) for k in ("m0h", "m0f", "z0", "zh", "zf"))
        b2_wide, m0_wide = (sb("ode_" + k, [96, 128]) for k in ("b2_wide", "m0_wide"))
        b3_wide = sb("ode_b3_wide", [128, KC, 96])
        b2_parts, m0_parts, part16 = (sb("ode_" + k, [96, 128], BF16) for k in ("b2_parts", "m0_parts", "part16"))
        ones16 = sb("ode_ones16", [96, 1], BF16)
        a_col = sb("ode_a", [128, 1])
        warm = sb("ode_warm", [128, 1])
        busy_w, busy_x = sb("ode_busy_w", [128, 128], F16), sb("ode_busy_x", [128, 512], F16)
        b_col = [sb(f"ode_b_{q}", [128, 4]) for q in range(2)]
        part, psum_b = sb("ode_part", [128, 1]), sb("ode_p", [128, 1])
        sums = sb("ode_sums", [128, N])
        sums2 = sb("ode_sums2", [128, N])
        ramp_i, ramp = sb("ode_ramp_i", [1, N], I32), sb("ode_ramp", [1, N])
        onesrow = sb("ode_ones", [1, TN])
        ps_a, ps_u, ps_z = (ctx.enter_context(nc.psum_tensor("ode_ps" + k, [128, BANK], F32)) for k in "auz")
        ps_o = [ctx.enter_context(nc.psum_tensor(f"ode_pso{b}", [128, BANK], F32)) for b in range(2)]
        BUSY, BUSY_A, BUSY_B = 2, 512, 288
        ps_busy = ctx.enter_context(nc.psum_tensor("ode_busy", [128, BANK], F32))
        load_all(nc, "ode", [(w1t[:], w1t_in.rearrange("(c k) n -> k c n", k=128)), (w2t[:], w2t_in), (w3[:], w3_in.rearrange("(c k) n -> k c n", k=128)),
                             (w3t[:], w3t_in), (b1[:], b1_in), (b2[:], b2_in), (b3[:], b3_in), (b3r[:], b3_row_in),
                             (b2_wide[:], rows(b2_row_in, 96))])
        stage_layernorm(nc, "ode_ln", ident, x, xn, xt, tiles=1)
        S = {k: new_semaphore(nc, "ode_" + k) for k in ("step", "made", "b3_wide", "ps", "ps_z0", "setup", "a", "b", "wa", "wu", "wz", "zb", "p", "s", "out", "outused")}
        with nc.Block() as block:
            @block.gpsimd
            def _(g):
                nc.gpsimd.iota(ramp_i[:], pattern=[[1, N]], base=0, channel_multiplier=0).then_inc(S["made"], 1)
                nc.gpsimd.memset(onesrow[:], 1.0).then_inc(S["made"], 1)
                nc.gpsimd.memset(ones16[:], 1.0).then_inc(S["made"], 1)

            @block.tensor
            def _(pe):
                for c in range(KC):
                    m = nc.tensor.matmul(ps_a[:, 0:128], w3[:, c, :], w1t[:, c, :], start=(c == 0), stop=(c == KC - 1))
                m.then_inc(S["ps"], 1)
                for c in range(KC):
                    nc.tensor.matmul(ps_u[:, 0:1], w1t[:, c, :], b3[:, c:c + 1], start=(c == 0), stop=(c == KC - 1))
                for c in range(KC):
                    m = nc.tensor.matmul(ps_z[:, 0:1], w1t[:, c, :], xt[:, c, 0:1], start=(c == 0), stop=(c == KC - 1))
                m.then_inc(S["ps"], 1)
                pe.wait_ge(S["b3_wide"], KC)
                for c in range(KC):
                    m = nc.tensor.matmul(ps_o[0][0:96, 0:128], b3_wide[:, c, :], w1t[:, c, :], start=(c == 0), stop=(c == KC - 1))
                m.then_inc(S["ps"], 1)

            @block.vector
            def _(v):
                link = linker(v, S["step"])

                def split_rows(wide, parts):
                    link(nc.vector.memset(parts[:], 0.0))
                    for p in (0, 32, 64):
                        link(nc.vector.tensor_copy(part16[:], wide[:]))
                        link(nc.vector.tensor_copy(parts[p:p + 1, :], part16[p:p + 1, :]))
                        link(nc.vector.tensor_tensor(wide[:], wide[:], part16[:], ALU.subtract))

                link(nc.vector.memset(b3_wide[:], 0.0))
                for c in range(KC):
                    nc.vector.tensor_scalar(b3_wide[:, c, :], b3_wide[:, c, :], b3[:, c:c + 1], None, ALU.add).then_inc(S["b3_wide"], 1)
                split_rows(b2_wide, b2_parts)
                v.wait_ge(S["ps"], 3)
                link(nc.vector.tensor_scalar(m0_wide[:], ps_o[0][0:96, 0:128], DT, None, ALU.mult))
                split_rows(m0_wide, m0_parts)
                link(nc.vector.tensor_scalar(mt_half[:], ps_a[:, 0:128], DT / 2, None, ALU.mult))
                link(nc.vector.tensor_scalar(mt_full[:], ps_a[:, 0:128], DT, None, ALU.mult))
                link(nc.vector.tensor_scalar(mt_sixth[:], ps_a[:, 0:128], DT / 6, None, ALU.mult))
                link(nc.vector.tensor_scalar(m0f[:], ps_u[:, 0:1], DT, None, ALU.mult))
                link(nc.vector.tensor_scalar(m0h[:], ps_u[:, 0:1], DT / 2, None, ALU.mult))
                link(nc.vector.tensor_tensor(z0[:], ps_z[:, 0:1], b1[:], ALU.add))
                link(nc.vector.memset(sums[:, 0:1], 0.0))
                link(nc.vector.memset(busy_w[:], 0.0))
                link(nc.vector.memset(busy_x[:], 0.0))
                v.wait_ge(S["made"], 3)
                link(nc.vector.tensor_copy(ramp[:], ramp_i[:]))
                link(nc.vector.tensor_scalar(ramp[:], ramp[:], DT, None, ALU.mult))
        with nc.Block() as block:
            @block.tensor
            def _(pe):
                def busy(cols):
                    for _ in range(BUSY):
                        nc.tensor.matmul(ps_busy[:, 0:cols], busy_w[:], busy_x[:, 0:cols], start=True, stop=True)

                for _ in range(16):
                    busy(BANK)
                nc.tensor.matmul(ps_z[:, 0:1], ident[:], z0[:], start=True, stop=True).then_inc(S["wz"], 1)
                nc.tensor.matmul(ps_a[:, 0:1], b2_parts[:], ones16[:], start=True, stop=False, skip_group_check=True)
                with pe.Fori(0, STEPS // UN) as i:
                    for r in range(UN):
                        k = i * (4 * UN) + 4 * r
                        q = r % 2
                        for s in range(4):
                            busy(BUSY_A)
                            pe.wait_ge(S["a"], k + (s + 1))
                            nc.tensor.matmul(ps_a[:, 0:1], w2t[:], a_col[:], start=False, stop=True, skip_group_check=True).then_inc(S["wa"], 1)
                            if s < 3:
                                if s == 0:
                                    pe.wait_ge(S["zb"], i * UN + (r + 1))
                                nc.tensor.matmul(ps_u[:, 0:1], ident[:], (zf if s == 2 else zh)[:], start=True, stop=False, skip_group_check=True)
                            else:
                                nc.tensor.matmul(ps_z[:, 0:1], m0_parts[:], ones16[:], start=False, stop=False, skip_group_check=True)
                                pe.wait_ge(S["p"], i * UN + (r + 1))
                                nc.tensor.matmul(ps_z[:, 0:1], mt_sixth[:], psum_b[:], start=False, stop=False, skip_group_check=True)
                            busy(BUSY_B)
                            pe.wait_ge(S["b"], k + (s + 1))
                            if s < 3:
                                nc.tensor.matmul(ps_u[:, 0:1], (mt_full if s == 2 else mt_half)[:], b_col[q][:, s:s + 1], start=False, stop=True, skip_group_check=True).then_inc(S["wu"], 1)
                            else:
                                nc.tensor.matmul(ps_z[:, 0:1], mt_sixth[:], b_col[q][:, 3:4], start=False, stop=True, skip_group_check=True).then_inc(S["wz"], 1)
                            nc.tensor.matmul(ps_a[:, 0:1], b2_parts[:], ones16[:], start=True, stop=False, skip_group_check=True)

            @block.scalar
            def _(a):
                nc.scalar.activation(warm[:], b2[:], ACT.Tanh)
                with a.Fori(0, STEPS // UN) as i:
                    for r in range(UN):
                        q = r % 2
                        for s in range(4):
                            if s == 0:
                                a.wait_ge(S["wz"], i * UN + (r + 1))
                                nc.scalar.activation(a_col[:], ps_z[:, 0:1], ACT.Tanh).then_inc(S["a"], 1)
                            else:
                                a.wait_ge(S["wu"], i * (3 * UN) + (3 * r + s))
                                nc.scalar.activation(a_col[:], ps_u[:, 0:1], ACT.Tanh).then_inc(S["a"], 1)
                            a.wait_ge(S["wa"], i * (4 * UN) + (4 * r + s + 1))
                            nc.scalar.activation(b_col[q][:, s:s + 1], ps_a[:, 0:1], ACT.Tanh).then_inc(S["b"], 1)

            @block.vector
            def _(v):
                with v.Fori(0, STEPS // UN) as i:
                    for r in range(UN):
                        q = r % 2
                        kb = i * (4 * UN) + 4 * r
                        v.wait_ge(S["a"], kb + 1)
                        nc.vector.tensor_tensor(zh[:], ps_z[:, 0:1], m0h[:], ALU.add)
                        nc.vector.tensor_tensor(zf[:], ps_z[:, 0:1], m0f[:], ALU.add).then_inc(S["zb"], 1)
                        v.wait_ge(S["b"], kb + 2)
                        nc.vector.scalar_tensor_tensor(part[:], b_col[q][:, 1:2], 2.0, b_col[q][:, 0:1], ALU.mult, ALU.add).then_inc(S["s"], 1)
                        v.wait_ge(S["b"], kb + 3)
                        v.wait_ge(S["s"], i * UN + (r + 1))
                        nc.vector.scalar_tensor_tensor(psum_b[:], b_col[q][:, 2:3], 2.0, part[:], ALU.mult, ALU.add).then_inc(S["p"], 1)
                        v.wait_ge(S["b"], kb + 4)
                        v.wait_ge(S["p"], i * UN + (r + 1))
                        nc.vector.tensor_tensor(sums[:, ds(i * UN + (r + 1), 1)], psum_b[:], b_col[q][:, 3:4], ALU.add).then_inc(S["out"], 1)

            split_weights(nc, block, ctx, whh_in, whh)
        with nc.Block() as block:
            @block.vector
            def _(v):
                link = linker(v, new_semaphore(nc, "ode_scan"))
                a_buf, b_buf, w = sums, sums2, 1
                while w < N:
                    link(nc.vector.tensor_copy(b_buf[:, 0:w], a_buf[:, 0:w]))
                    link(nc.vector.tensor_tensor(b_buf[:, w:N], a_buf[:, w:N], a_buf[:, 0:N - w], ALU.add))
                    a_buf, b_buf, w = b_buf, a_buf, 2 * w
                assert a_buf is sums
                link(nc.vector.tensor_scalar(sums[:], sums[:], DT / 6, None, ALU.mult))
                v.sem_inc(S["setup"], 1)
                for i in range(NT):
                    v.wait_ge(S["ps_z0"], i + 1)
                    nc.vector.tensor_tensor(x[:, i, :], x[:, i, :], ps_o[i % 2][0:TN, :], ALU.add).then_inc(S["outused"], 1)

            @block.tensor
            def _(pe):
                pe.wait_ge(S["setup"], 1)
                for i in range(NT):
                    if i >= 2:
                        pe.wait_ge(S["outused"], i - 1)
                    nc.tensor.matmul(ps_o[i % 2][0:TN, :], onesrow[:], xn[0:1, 0, :], start=True, stop=False)
                    nc.tensor.matmul(ps_o[i % 2][0:TN, :], ramp[:, i * TN:(i + 1) * TN], b3r[:], start=False, stop=False)
                    nc.tensor.matmul(ps_o[i % 2][0:TN, :], sums[:, i * TN:(i + 1) * TN], w3t[:], start=False, stop=True).then_inc(S["ps_z0"], 1)


def split_weights(nc, block, ctx, whh_in, whh):
    PIECE = 1024
    PIECES = KC * GATES // PIECE
    raw = [ctx.enter_context(nc.sbuf_tensor(f"split_raw{b}", [128, PIECE], F32)) for b in range(2)]
    big = ctx.enter_context(nc.sbuf_tensor("split_big", [128, PIECE], F32))
    rest = ctx.enter_context(nc.sbuf_tensor("split_rest", [128, PIECE], F32))
    piece_in = [new_semaphore(nc, f"split_in{b}") for b in range(2)]
    scaled = new_semaphore(nc, "split_scaled")
    step = new_semaphore(nc, "split_step")
    seen = new_semaphore(nc, "split_seen")

    @block.sync
    def _(sp):
        sp.sem_inc(scaled, 2)
        with sp.Fori(0, CELLS) as s:
            for m in range(PIECES):
                sp.wait_ge(scaled, s * PIECES + (m + 1))
                c, half = m // 2, m % 2
                sp.dma_start(raw[m % 2][:], whh_in[:, ds((s * KC + c) * GATES + half * PIECE, PIECE)]).then_inc(piece_in[m % 2], 16)

    @block.gpsimd
    def _(g):
        with g.Fori(0, CELLS) as s:
            for m in range(PIECES):
                hi = whh[:, ds(s * CELL_COLS + m * PIECE, PIECE)]
                lo = whh[:, ds(s * CELL_COLS + KC * GATES + m * PIECE, PIECE)]
                k = s * (4 * PIECES) + 4 * m
                g.wait_ge(piece_in[m % 2], s * (8 * PIECES) + 16 * (m // 2 + 1))
                g.sem_inc(seen, 1)
                nc.gpsimd.tensor_scalar(big[:], raw[m % 2][:], 64.0, None, ALU.mult).then_inc(scaled, 1)
                g.wait_ge(scaled, s * PIECES + (m + 3))
                g.sem_inc(seen, 1)
                nc.gpsimd.tensor_copy(hi, big[:]).then_inc(step, 1)
                g.wait_ge(step, k + 1)
                g.sem_inc(seen, 1)
                nc.gpsimd.tensor_tensor(rest[:], big[:], hi, ALU.subtract).then_inc(step, 1)
                g.wait_ge(step, k + 2)
                g.sem_inc(seen, 1)
                nc.gpsimd.tensor_scalar(rest[:], rest[:], 2048.0, None, ALU.mult).then_inc(step, 1)
                g.wait_ge(step, k + 3)
                g.sem_inc(seen, 1)
                nc.gpsimd.tensor_copy(lo, rest[:]).then_inc(step, 1)


def stage_mean_project(nc, tag, xt, z_t, w_self, w_mean, bias, rcount, h):
    with ExitStack() as ctx:
        tmp = [ctx.enter_context(nc.sbuf_tensor(f"{tag}_tmp{b}", [TN, D], F32)) for b in range(2)]
        ps = [ctx.enter_context(nc.psum_tensor(f"{tag}_ps{b}", [128, BANK], F32)) for b in range(4)]
        ready = new_semaphore(nc, tag + "_ready")
        read = new_semaphore(nc, tag + "_read")
        done = new_semaphore(nc, tag + "_done")
        with nc.Block() as block:
            @block.tensor
            def _(pe):
                for i in range(NT):
                    if i >= 2:
                        pe.wait_ge(done, i - 1)
                    for b, (lhs, w) in enumerate(((xt, w_self), (z_t, w_mean))):
                        for c in range(KC):
                            m = nc.tensor.matmul(ps[2 * (i % 2) + b][0:TN, :], lhs[:, c, i * TN:(i + 1) * TN], w[:, c, :], start=(c == 0), stop=(c == KC - 1))
                    m.then_inc(ready, 1)

            @block.vector
            def _(v):
                for i in range(NT):
                    v.wait_ge(ready, i + 1)
                    nc.vector.scalar_tensor_tensor(tmp[i % 2][:], ps[2 * (i % 2) + 1][0:TN, :], rcount[:, i:i + 1], bias[:], ALU.mult, ALU.add).then_inc(read, 1)
                    v.wait_ge(read, i + 1)
                    nc.vector.tensor_tensor(h[:, i, :], ps[2 * (i % 2)][0:TN, :], tmp[i % 2][:], ALU.add).then_inc(done, 1)
                v.wait_ge(done, NT)


def stage_add(nc, tag, x, parts):
    step = new_semaphore(nc, tag + "_added")
    with nc.Block() as block:
        @block.vector
        def _(v):
            link = linker(v, step)
            for part in parts:
                for i in range(NT):
                    last = nc.vector.tensor_tensor(x[:, i, :], x[:, i, :], part[:, i, :], ALU.add)
                link(last)


def layer_mean(nc, x, ident, adj, rcount, w_in, b_in):
    with ExitStack() as ctx:
        def sb(name, shape):
            return ctx.enter_context(nc.sbuf_tensor(name, shape, F32))
        w, b = sb("sage_w", [128, 2 * KC, D]), sb("sage_b", [TN, D])
        xn, xt, z_t = sb("sage_xn", [TN, NT, D]), sb("sage_xt", [128, KC, N]), sb("sage_zt", [128, KC, N])
        load_all(nc, "sage", [(w[:], w_in.rearrange("(c k) n -> k c n", k=128)), (b[:], rows(b_in, TN))])
        stage_layernorm(nc, "sage_ln", ident, x, xn, xt)
        stage_aggregate(nc, "sage_a", xn, adj, z_t)
        stage_mean_project(nc, "sage_p", xt, z_t, w[:, 0:KC, :], w[:, KC:2 * KC, :], b, rcount, xn)
        stage_add(nc, "sage", x, [xn])


GATE_SLOT = (0, 1, 3, 2)


def stage_input_gates(nc, xt, wih_in, bias_a_in, bias_b_in, xg):
    TOK = 125
    with ExitStack() as ctx:
        def sb(name, shape, dt=F32):
            return ctx.enter_context(nc.sbuf_tensor(name, shape, dt))
        w = sb("ig_w", [128, KC, GATES])
        out = sb("ig_out", [128, TOK, 16])
        ba, bb = sb("ig_ba", [128, CELLS * 16]), sb("ig_bb", [128, CELLS * 16])
        ps = [ctx.enter_context(nc.psum_tensor(f"ig_ps{b}", [128, BANK], F32)) for b in range(4)]
        load_all(nc, "ig", [(ba[:], bias_a_in), (bb[:], bias_b_in)])
        S = {k: new_semaphore(nc, "ig_" + k) for k in ("w_in", "ready", "moved", "stored", "bias")}
        jobs = [(s, t, c, j) for s in range(CELLS) for t in range(N // TOK) for c in range(KC) for j in range(4)]
        with nc.Block() as block:
            @block.sync
            def _(sp):
                for s in range(CELLS):
                    if s >= 1:
                        sp.wait_ge(S["ready"], s * 80)
                    sp.dma_start(w[:], wih_in[s].rearrange("(c k) g -> k c g", k=128)).then_inc(S["w_in"], 16)
                    for t in range(N // TOK):
                        k = s * (N // TOK) + t
                        sp.wait_ge(S["moved"], 16 * (k + 1))
                        sp.dma_start(xg[s, :, t * TOK:(t + 1) * TOK, :], out[:]).then_inc(S["stored"], 16)
                sp.wait_ge(S["stored"], 16 * CELLS * (N // TOK))

            @block.tensor
            def _(pe):
                for k, (s, t, c, j) in enumerate(jobs):
                    if k % 80 == 0:
                        pe.wait_ge(S["w_in"], 16 * (s + 1))
                    if k >= 4:
                        pe.wait_ge(S["moved"], k - 3)
                    for kc in range(KC):
                        m = nc.tensor.matmul(ps[k % 4][:, 0:TOK], w[:, kc, j * D + c * 128:j * D + (c + 1) * 128], xt[:, kc, t * TOK:(t + 1) * TOK], start=(kc == 0), stop=(kc == KC - 1))
                    m.then_inc(S["ready"], 1)

            @block.vector
            def _(v):
                nc.vector.tensor_tensor(ba[:], ba[:], bb[:], ALU.add).then_inc(S["bias"], 1)
                v.wait_ge(S["bias"], 1)
                for k, (s, t, c, j) in enumerate(jobs):
                    v.wait_ge(S["ready"], k + 1)
                    if k % 16 == 0 and k:
                        v.wait_ge(S["stored"], k)
                    q = s * 16 + c * 4 + j
                    nc.vector.tensor_scalar(out[:, :, GATE_SLOT[j] * 4 + c], ps[k % 4][:, 0:TOK], ba[:, q:q + 1], 1.0 if j == 2 else 0.5, ALU.add, ALU.mult).then_inc(S["moved"], 1)


def stage_input_logits(nc, xt, wselx, bsel, xsel):
    with ExitStack() as ctx:
        ps = [ctx.enter_context(nc.psum_tensor(f"il_ps{b}", [128, BANK], F32)) for b in range(8)]
        cleared, ready, step = (new_semaphore(nc, "il_" + k) for k in ("cleared", "ready", "step"))
        with nc.Block() as block:
            @block.tensor
            def _(pe):
                for s in range(CELLS):
                    for b, (at, n) in enumerate(HALVES):
                        for c in range(KC):
                            m = nc.tensor.matmul(ps[2 * s + b][0:1, 0:n], wselx[:, c, s:s + 1], xt[:, c, at:at + n], start=(c == 0), stop=(c == KC - 1))
                m.then_inc(ready, 1)

            @block.vector
            def _(v):
                link = linker(v, step)
                link(nc.vector.memset(xsel[:], 0.0))
                link(nc.vector.memset(xsel[0:1, :], PAD_LOGIT))
                v.wait_ge(ready, 1)
                row = xsel[0:1, :].rearrange("p (t e) -> p t e", e=8)
                for s in range(CELLS):
                    for b, (at, n) in enumerate(HALVES):
                        last = nc.vector.tensor_scalar(row[:, at:at + n, s], ps[2 * s + b][0:1, 0:n], bsel[0:1, s:s + 1], None, ALU.add)
                link(last)


def stage_lstm(nc, whh, xg, xsel, wsel, ident, gsel, hist):
    UN = 8
    LOOPS = (N - 1) // UN
    GROUP = 4
    PIECES = ((0, 1), (1, 2), (2, 4))
    assert 1 + LOOPS * UN == N
    with ExitStack() as ctx:
        def sb(name, shape, dt=F32):
            return ctx.enter_context(nc.sbuf_tensor(name, shape, dt))
        xgb = sb("xg_buf", [128, 2, CELLS, GROUP * 16])
        xg0 = sb("xg_first", [128, 16])
        hpair = sb("h_pair", [128, KC, 6], F16)
        hcur = sb("h_now", [128, KC])
        act = sb("gates_and_c", [128, 20])
        ccur = act[:, 16:20]
        parts = sb("input_and_forget_part", [128, 2 * KC])
        gsb = sb("gate_rows", [128, D])
        ok, tc = sb("out_gate", [128, KC]), sb("tanh_c", [128, KC])
        ones = sb("lstm_ones", [128, 1])
        mx, idx = sb("best", [1, 8]), sb("best_at", [1, 8], U32)
        psg, psc, psl = (ctx.enter_context(nc.psum_tensor(n, [128, BANK], F32)) for n in ("ps_rows", "ps_gates", "ps_logits"))
        busy_w, busy_x = sb("lstm_busy_w", [128, 128], F16), sb("lstm_busy_x", [128, 512], F16)
        BUSY = {"c": 2, "h": 1, "best": 3, "rows": 2}
        ps_busy = ctx.enter_context(nc.psum_tensor("lstm_busy", [128, BANK], F32))
        xg_in = [new_semaphore(nc, f"xg_in{g}") for g in range(2)]
        S = {k: new_semaphore(nc, "lstm_" + k) for k in (
            "xg0_in", "init", "c_ready", "h_ready", "hp_ready", "h_part", "logits", "best", "rows", "evac",
            "gates", "acted", "fi", "tanh_c", "kept", "max", "seen_v", "seen_pe", "xg_used")}
        with nc.Block() as block:
            @block.sync
            def _(sp):
                sp.dma_start(xg0[:], xg[0, :, 0, :]).then_inc(S["xg0_in"], 16)
                with sp.Fori(0, LOOPS) as i:
                    for g in range(2):
                        sp.wait_ge(S["xg_used"], i * UN + GROUP * (g + 1))
                        for s in range(CELLS):
                            sp.dma_start(xgb[:, g, s, :], xg[s, :, ds(i * UN + (1 + GROUP * g), GROUP), :].rearrange("p t g -> p (t g)")).then_inc(xg_in[g], 16)

            @block.vector
            def _(v):
                nc.vector.memset(hpair[:], 0.0).then_inc(S["init"], 1)
                nc.vector.memset(psg[:], 0.0).then_inc(S["init"], 1)
                nc.vector.memset(ccur, 0.0).then_inc(S["init"], 1)
                nc.vector.memset(ones[:], 1.0).then_inc(S["init"], 1)
                nc.vector.memset(busy_w[:], 0.0).then_inc(S["init"], 1)
                nc.vector.memset(busy_x[:], 0.0).then_inc(S["init"], 1)
                v.wait_ge(S["init"], 6)

                def cell(k):
                    v.wait_ge(S["acted"], k + 1)
                    nc.vector.scalar_tensor_tensor(parts[:], act[:, 0:8], 1.0, act[:, 12:20], ALU.add, ALU.mult).then_inc(S["fi"], 1)
                    v.wait_ge(S["fi"], k + 1)
                    nc.vector.scalar_tensor_tensor(ccur, parts[:, KC:2 * KC], 0.5, parts[:, 0:KC], ALU.mult, ALU.add).then_inc(S["c_ready"], 1)
                    nc.vector.tensor_scalar(ok[:], act[:, 8:12], 1.0, 1024.0, ALU.add, ALU.mult).then_inc(S["h_part"], 1)
                    v.wait_ge(S["tanh_c"], k + 1)
                    v.wait_ge(S["h_part"], k * 2 + 1)
                    nc.vector.tensor_tensor(hcur[:], ok[:], tc[:], ALU.mult).then_inc(S["h_ready"], 1)
                    nc.vector.tensor_tensor(hpair[:, :, 2], ok[:], tc[:], ALU.mult).then_inc(S["h_part"], 1)
                    v.wait_ge(S["h_ready"], k + 1)
                    v.wait_ge(S["h_part"], k * 2 + 2)
                    nc.vector.tensor_tensor(hpair[:, :, 3], hcur[:], hpair[:, :, 2], ALU.subtract).then_inc(S["hp_ready"], 1)

                cell(0)
                with v.Fori(0, LOOPS) as i:
                    for q in range(UN):
                        k = i * UN + (q + 1)
                        v.wait_ge(S["logits"], k)
                        v.sem_inc(S["seen_v"], 1)
                        nc.vector.max(mx[:], psl[0:1, 0:8]).then_inc(S["max"], 1)
                        v.wait_ge(S["max"], k)
                        v.sem_inc(S["seen_v"], 1)
                        nc.vector.max_index(idx[:], mx[:], psl[0:1, 0:8]).then_inc(S["best"], 1)
                        v.wait_ge(S["kept"], k)
                        cell(k)

            @block.scalar
            def _(a):
                def cell(k):
                    a.wait_ge(S["gates"], k + 1)
                    nc.scalar.activation(act[:, 0:16], psc[:, 0:16], ACT.Tanh).then_inc(S["acted"], 1)
                    a.wait_ge(S["c_ready"], k + 1)
                    nc.scalar.activation(tc[:], ccur, ACT.Tanh, scale=0.5).then_inc(S["tanh_c"], 1)

                cell(0)
                with a.Fori(0, LOOPS) as i:
                    for q in range(UN):
                        k = i * UN + (q + 1)
                        a.wait_ge(S["rows"], k)
                        for lo, hi in PIECES:
                            nc.scalar.copy(gsb[:, lo * 128:hi * 128], psg[:, lo * 128:hi * 128]).then_inc(S["evac"], 1)
                        cell(k)

            @block.gpsimd
            def _(g):
                g.wait_ge(S["h_ready"], 1)
                nc.gpsimd.tensor_copy(hist[:, 0:1, :], hcur[:]).then_inc(S["kept"], 1)
                with g.Fori(0, LOOPS) as i:
                    for q in range(UN):
                        k = i * UN + (q + 1)
                        g.wait_ge(S["h_ready"], k + 1)
                        nc.gpsimd.tensor_copy(hist[:, ds(k, 1), :], hcur[:]).then_inc(S["kept"], 1)

            @block.tensor
            def _(pe):
                pe.wait_ge(S["init"], 6)
                pe.wait_ge(S["xg0_in"], 16)

                def busy(n):
                    for _ in range(n):
                        nc.tensor.matmul(ps_busy[:, 0:BANK], busy_w[:], busy_x[:, 0:BANK], start=True, stop=True)

                pe.sem_inc(S["xg_used"], UN)
                nc.tensor.matmul(psc[:, 0:16], ident[:], xg0[:], start=True, stop=True).then_inc(S["gates"], 1)
                with pe.Fori(0, LOOPS) as i:
                    for q in range(UN):
                        k = i * UN + (q + 1)
                        nc.tensor.matmul(psl[0:1, 0:8], ones[:], xsel[:, ds(k * 8, 8)], start=True, stop=False, skip_group_check=True)
                        busy(BUSY["c"])
                        pe.wait_ge(S["c_ready"], k)
                        for c in range(KC):
                            nc.tensor.matmul(psl[0:1, 0:4], ccur[:, c:c + 1], wsel[:, KC + c, :], start=False, stop=False, skip_group_check=True)
                        busy(BUSY["h"])
                        pe.wait_ge(S["h_ready"], k)
                        for c in range(KC):
                            m = nc.tensor.matmul(psl[0:1, 0:4], hcur[:, c:c + 1], wsel[:, c, :], start=False, stop=(c == KC - 1), skip_group_check=True)
                        m.then_inc(S["logits"], 1)
                        busy(BUSY["best"])
                        pe.wait_ge(S["hp_ready"], k)
                        pe.wait_ge(S["best"], k)
                        pe.sem_inc(S["seen_pe"], 1)
                        s = pe.value_load(idx[0:1, 0:1])

                        def recurrent(e):
                            for part in range(2):
                                for c in range(KC):
                                    for j in range(4):
                                        at = e * CELL_COLS + (part * KC + c) * GATES + j * D
                                        m = nc.tensor.matmul(psg[32 * j:32 * j + 4, :], hpair[:, c, 2 - 2 * part:6 - 2 * part],
                                                             whh[:, at:at + D], start=(part == 0 and c == 0), stop=(part == 1 and c == KC - 1))
                            m.then_inc(S["rows"], 1)

                        with pe.If(s < 2):
                            with pe.If(s < 1):
                                recurrent(0)
                            with pe.Else():
                                recurrent(1)
                        with pe.Else():
                            with pe.If(s < 3):
                                recurrent(2)
                            with pe.Else():
                                recurrent(3)
                        s = pe.snap(s, min_val=0, max_val=CELLS - 1)
                        if q % GROUP == 0:
                            pe.wait_ge(xg_in[q // GROUP], i * (16 * CELLS) + 16 * CELLS)
                        nc.tensor.matmul(psc[:, 0:16], ident[:], xgb[:, q // GROUP, :, :].rearrange("p s t -> p (s t)")[:, ds(s * (GROUP * 16) + (q % GROUP) * 16, 16)], start=True, stop=False, skip_group_check=True).then_inc(S["xg_used"], 1)
                        busy(BUSY["rows"])
                        for c in range(KC):
                            for n, (lo, hi) in enumerate(PIECES):
                                if c == lo:
                                    pe.wait_ge(S["evac"], i * (UN * len(PIECES)) + (q * len(PIECES) + n + 1))
                            m = nc.tensor.matmul(psc[:, c:16:4], gsb[:, c * 128:(c + 1) * 128], gsel[:], start=False, stop=(c == KC - 1), skip_group_check=True)
                        m.then_inc(S["gates"], 1)


def stage_hist_out(nc, hist, ident, x):
    with ExitStack() as ctx:
        ps = [ctx.enter_context(nc.psum_tensor(f"ho_ps{b}", [128, BANK], F32)) for b in range(2)]
        turned, used = new_semaphore(nc, "ho_turned"), new_semaphore(nc, "ho_used")
        with nc.Block() as block:
            @block.tensor
            def _(pe):
                for i in range(NT):
                    if i >= 2:
                        pe.wait_ge(used, i - 1)
                    for c in range(KC):
                        m = nc.tensor.transpose(ps[i % 2][0:TN, c * 128:(c + 1) * 128], hist[:, i * TN:(i + 1) * TN, c], ident[:])
                    m.then_inc(turned, 1)

            @block.vector
            def _(v):
                for i in range(NT):
                    v.wait_ge(turned, i + 1)
                    nc.vector.scalar_tensor_tensor(x[:, i, :], ps[i % 2][0:TN, :], 1.0 / 2048, x[:, i, :], ALU.mult, ALU.add).then_inc(used, 1)


def layer_lstm(nc, x, ident, whh, wih_in, bih_in, bhh_in, wsel_h_in, wsel_x_in, bsel_in, gsel_in, xg):
    with ExitStack() as ctx:
        def sb(name, shape):
            return ctx.enter_context(nc.sbuf_tensor(name, shape, F32))
        wsel, bsel, gsel = sb("l_wsel", [128, 2 * KC, CELLS]), sb("l_bsel", [1, CELLS]), sb("l_gsel", [128, 4])
        hist = sb("l_hist", [128, N, KC])
        xt = hist[:].rearrange("p n c -> p (n c)").rearrange("p (c n) -> p c n", c=KC)
        with nc.sbuf_tensor("l_xn", [TN, NT, D], F32) as xn:
            stage_layernorm(nc, "l_ln", ident, x, xn, xt)
        stage_input_gates(nc, xt, wih_in, bih_in, bhh_in, xg)
        wselx = sb("l_wselx", [128, KC, CELLS])
        xsel = sb("l_xsel", [128, N * 8])
        load_all(nc, "lsel", [(wsel[:], wsel_h_in), (wselx[:], wsel_x_in), (bsel[:], bsel_in), (gsel[:], gsel_in)])
        stage_input_logits(nc, xt, wselx, bsel, xsel)
        scaled = new_semaphore(nc, "l_wsel_scaled")
        with nc.Block() as block:
            @block.vector
            def _(v):
                nc.vector.tensor_scalar(wsel[:, 0:KC, :], wsel[:, 0:KC, :], 1.0 / 2048, None, ALU.mult).then_inc(scaled, 1)
                nc.vector.tensor_scalar(wsel[:, KC:, :], wsel[:, KC:, :], 0.5, None, ALU.mult).then_inc(scaled, 1)
                v.wait_ge(scaled, 2)
        stage_lstm(nc, whh, xg, xsel, wsel, ident, gsel, hist)
        stage_hist_out(nc, hist, ident, x)


def layer_batchnorm(nc, x, ident, adj, rcount, wl_in, bl_in, wr_in, gamma_in, beta_in):
    with ExitStack() as ctx:
        def sb(name, shape):
            return ctx.enter_context(nc.sbuf_tensor(name, shape, F32))
        wl, wr, bl = sb("bn_wl", [128, KC, D]), sb("bn_wr", [128, KC, D]), sb("bn_bl", [TN, D])
        gamma, beta = sb("bn_gamma", [TN, D]), sb("bn_beta", [TN, D])
        xn, xt, z_t, h = sb("bn_xn", [TN, NT, D]), sb("bn_xt", [128, KC, N]), sb("bn_zt", [128, KC, N]), sb("bn_h", [TN, NT, D])
        sq = sb("bn_sq", [TN, NT, D])
        mean, var, root, r, t = (sb("bn_" + k, [TN, D]) for k in ("mean", "var", "root", "r", "t"))
        allones = sb("bn_ones", [TN, TN])
        load_all(nc, "bn", [(wl[:], wl_in.rearrange("(c k) n -> k c n", k=128)), (wr[:], wr_in.rearrange("(c k) n -> k c n", k=128)),
                            (bl[:], rows(bl_in, TN)), (gamma[:], rows(gamma_in, TN)), (beta[:], rows(beta_in, TN))])
        stage_layernorm(nc, "bn_ln", ident, x, xn, xt)
        stage_aggregate(nc, "bn_a", xn, adj, z_t)
        stage_mean_project(nc, "bn_p", xt, z_t, wr, wl, bl, rcount, h)
        ps = [ctx.enter_context(nc.psum_tensor(f"bn_ps{b}", [128, BANK], F32)) for b in range(2)]
        made, ready, step, squared, summed, rooted = (new_semaphore(nc, "bn_" + k) for k in ("made", "ready", "step", "squared", "summed", "rooted"))
        with nc.Block() as block:
            @block.gpsimd
            def _(g):
                nc.gpsimd.memset(allones[:], 1.0).then_inc(made, 1)

            @block.tensor
            def _(pe):
                pe.wait_ge(made, 1)
                for i in range(NT):
                    m = nc.tensor.matmul(ps[0][0:TN, :], allones[:], h[:, i, :], start=(i == 0), stop=(i == NT - 1))
                m.then_inc(summed, 1)
                for i in range(NT):
                    pe.wait_ge(squared, i + 1)
                    m = nc.tensor.matmul(ps[1][0:TN, :], allones[:], sq[:, i, :], start=(i == 0), stop=(i == NT - 1))
                m.then_inc(summed, 1)

            @block.scalar
            def _(a):
                for i in range(NT):
                    a.wait_ge(ready, i + 1)
                    nc.scalar.activation(sq[:, i, :], h[:, i, :], ACT.Square).then_inc(squared, 1)
                a.wait_ge(ready, NT + 1)
                nc.scalar.activation(root[:], var[:], ACT.Sqrt).then_inc(rooted, 1)

            @block.vector
            def _(v):
                link = linker(v, step)
                v.wait_ge(summed, 1)
                link(nc.vector.tensor_scalar(mean[:], ps[0][0:TN, :], 1.0 / N, None, ALU.mult))
                for i in range(NT):
                    nc.vector.tensor_tensor(h[:, i, :], h[:, i, :], mean[:], ALU.subtract).then_inc(ready, 1)
                v.wait_ge(summed, 2)
                nc.vector.tensor_scalar(var[:], ps[1][0:TN, :], 1.0 / N, LN_EPS, ALU.mult, ALU.add).then_inc(ready, 1)
                v.wait_ge(rooted, 1)
                link(nc.vector.reciprocal(r[:], root[:]))
                newton_rsqrt(nc, link, r[:], var[:], t[:])
                link(nc.vector.tensor_tensor(r[:], r[:], gamma[:], ALU.mult))
                for i in range(NT):
                    last = nc.vector.tensor_tensor(sq[:, i, :], h[:, i, :], r[:], ALU.mult)
                link(last)
                for i in range(NT):
                    last = nc.vector.tensor_tensor(h[:, i, :], sq[:, i, :], beta[:], ALU.add)
                link(last)
                for i in range(NT):
                    last = nc.vector.scalar_tensor_tensor(sq[:, i, :], h[:, i, :], 0.0, xn[:, i, :], ALU.max, ALU.add)
                link(last)
        stage_add(nc, "bn", x, [sq])


def layer_peer(nc, x, ident, wq_in, keys_in, wd_in, wu_in):
    with ExitStack() as ctx:
        def sb(name, shape, dt=F32):
            return ctx.enter_context(nc.sbuf_tensor(name, shape, dt))
        wq, keys = sb("pe_wq", [128, KC, D]), sb("pe_keys", [128, 2, KEYS])
        wd, wu = sb("pe_wd", [128, KC, KEYS]), sb("pe_wu", [128, 2, D])
        xn, xt, qt = sb("pe_xn", [TN, NT, D]), sb("pe_xt", [128, KC, N]), sb("pe_qt", [128, KC, N])
        load_all(nc, "pe", [(wq[:], wq_in.rearrange("(c k) n -> k c n", k=128)), (keys[:], keys_in), (wd[:], wd_in), (wu[:], wu_in.rearrange("(c k) n -> k c n", k=128))])
        stage_layernorm(nc, "pe_ln", ident, x, xn, xt)
        ps_q = [ctx.enter_context(nc.psum_tensor(f"pe_psq{b}", [128, BANK], F32)) for b in range(2)]
        ps_s = ctx.enter_context(nc.psum_tensor("pe_pss", [128, 4 * BANK], F32))
        ps_t = ctx.enter_context(nc.psum_tensor("pe_pst", [128, BANK], F32))
        ps_o = ctx.enter_context(nc.psum_tensor("pe_pso", [128, BANK], F32))
        jobs = [(c, at, n) for c in range(KC) for at, n in HALVES]
        q_ready, q_moved = new_semaphore(nc, "pe_q_ready"), new_semaphore(nc, "pe_q_moved")
        with nc.Block() as block:
            @block.tensor
            def _(pe):
                for k, (c, at, n) in enumerate(jobs):
                    if k >= 2:
                        pe.wait_ge(q_moved, k - 1)
                    for kc in range(KC):
                        m = nc.tensor.matmul(ps_q[k % 2][:, 0:n], wq[:, kc, c * 128:(c + 1) * 128], xt[:, kc, at:at + n], start=(kc == 0), stop=(kc == KC - 1))
                    m.then_inc(q_ready, 1)

            @block.scalar
            def _(a):
                for k, (c, at, n) in enumerate(jobs):
                    a.wait_ge(q_ready, k + 1)
                    nc.scalar.activation(qt[:, c, at:at + n], ps_q[k % 2][:, 0:n], ACT.Copy, scale=float(1.0 / np.sqrt(1.0 + 1e-5))).then_inc(q_moved, 1)
        vals, places, places_f = sb("pe_vals", [TN, TOPK]), sb("pe_places", [TN, TOPK], U32), sb("pe_places_f", [TN, TOPK])
        sim = sb("pe_sim", [TN, KEYS])
        grid, grid1, grid2 = (sb("pe_" + k, [TN, KEYS]) for k in ("grid", "grid1", "grid2"))
        top, top2, neg = sb("pe_top", [TN, 8]), sb("pe_top2", [TN, 8]), sb("pe_neg", [TN, 1])
        ex, pick, total, inv = sb("pe_ex", [TN, KEYS]), sb("pe_pick", [TN, KEYS]), sb("pe_total", [TN, 1]), sb("pe_inv", [TN, 1])
        weight = sb("pe_weight", [TN, KEYS])
        gelu = [sb(f"pe_gelu{b}", [TN, KEYS]) for b in range(2)]
        w_t = sb("pe_wt", [128, 2, TN])
        S = {k: new_semaphore(nc, "pe_" + k) for k in ("sims", "step", "neg", "exp", "heads", "gated", "down", "gelu", "turned", "wt", "out", "added", "seen")}
        STEPS_HEAD = 14
        with nc.Block() as block:
            @block.tensor
            def _(pe):
                for i in range(NT):
                    if i >= 1:
                        pe.wait_ge(S["heads"], HEADS * i)
                    for h in range(HEADS):
                        g = 32 * (h % 4)
                        m = nc.tensor.matmul(ps_s[0:TN, (h % 4) * BANK + (h // 4) * KEYS:(h % 4) * BANK + (h // 4 + 1) * KEYS], qt[g:g + 32, h // 4, i * TN:(i + 1) * TN], keys[g:g + 32, h // 4, :], start=True, stop=True, skip_group_check=True)
                    m.then_inc(S["sims"], 1)
                    if i >= 1:
                        pe.wait_ge(S["gelu"], i)
                    for c in range(KC):
                        m = nc.tensor.matmul(ps_q[0][0:TN, 0:KEYS], qt[:, c, i * TN:(i + 1) * TN], wd[:, c, :], start=(c == 0), stop=(c == KC - 1))
                    m.then_inc(S["down"], 1)
                    pe.wait_ge(S["gated"], i + 1)
                    for c in range(2):
                        m = nc.tensor.transpose(ps_t[:, c * TN:(c + 1) * TN], weight[:, c * 128:(c + 1) * 128], ident[0:TN, 0:TN])
                    m.then_inc(S["turned"], 1)
                    pe.wait_ge(S["wt"], i + 1)
                    if i >= 1:
                        pe.wait_ge(S["added"], i)
                    for c in range(2):
                        m = nc.tensor.matmul(ps_o[0:TN, :], w_t[:, c, :], wu[:, c, :], start=(c == 0), stop=(c == 1))
                    m.then_inc(S["out"], 1)

            @block.scalar
            def _(a):
                for i in range(NT):
                    a.wait_ge(S["down"], i + 1)
                    if i >= 2:
                        a.wait_ge(S["gated"], i - 1)
                    nc.scalar.activation(gelu[i % 2][:], ps_q[0][0:TN, 0:KEYS], ACT.Gelu_apprx_tanh).then_inc(S["gelu"], 1)
                    with a.Fori(0, HEADS) as h:
                        a.wait_ge(S["neg"], h + (i * HEADS + 1))
                        nc.scalar.activation(ex[:], grid[:], ACT.Exp, bias=neg[:]).then_inc(S["exp"], 1)
                    a.wait_ge(S["turned"], i + 1)
                    nc.scalar.copy(w_t[:], ps_t[:, 0:2 * TN].rearrange("p (c n) -> p c n", c=2)).then_inc(S["wt"], 1)

            @block.vector
            def _(v):
                for i in range(NT):
                    if i >= 1:
                        v.wait_ge(S["turned"], i)
                    nc.vector.memset(weight[:], 0.0)
                    v.wait_ge(S["sims"], i + 1)
                    with v.Fori(0, HEADS) as h:
                        base = i * HEADS * STEPS_HEAD
                        n = [0]

                        def link(ins):
                            n[0] += 1
                            ins.then_inc(S["step"], 1)
                            v.wait_ge(S["step"], h * STEPS_HEAD + (base + n[0]))
                            v.sem_inc(S["seen"], 1)

                        link(nc.vector.tensor_copy(sim[:], ps_s[0:TN, ds(h * KEYS, KEYS)]))
                        for half in range(2):
                            link(nc.vector.max(vals[:, 8 * half:8 * half + 8], sim[:]))
                            link(nc.vector.max_index(places[:, 8 * half:8 * half + 8], vals[:, 8 * half:8 * half + 8], sim[:]))
                            if half == 0:
                                link(nc.vector.match_replace(sim[:], vals[:, 0:8], sim[:], SENTINEL))
                        link(nc.vector.tensor_copy(places_f[:], places[:]))
                        link(nc.vector.tensor_tensor(grid[:].rearrange("p (a b) -> p a b", a=TOPK), vals[:].unsqueeze(2).broadcast_to([TN, TOPK, TOPK]),
                                                     places_f[:].unsqueeze(1).broadcast_to([TN, TOPK, TOPK]), ALU.add))
                        link(nc.vector.max(top[:], grid[:]))
                        nc.vector.tensor_scalar(neg[:], top[:, 0:1], -1.0, None, ALU.mult).then_inc(S["neg"], 1)
                        link(nc.vector.match_replace(grid1[:], top[:], grid[:], SENTINEL))
                        link(nc.vector.max(top2[:], grid1[:]))
                        link(nc.vector.match_replace(grid2[:], top2[:], grid1[:], SENTINEL))
                        v.wait_ge(S["exp"], h + (i * HEADS + 1))
                        link(nc.vector.scalar_tensor_tensor(pick[:], grid2[:], SENTINEL, ex[:], ALU.is_equal, ALU.mult, accum_out=total[:]))
                        link(nc.vector.reciprocal(inv[:], total[:]))
                        assert n[0] == STEPS_HEAD
                        nc.vector.scalar_tensor_tensor(weight[:], pick[:], inv[:], weight[:], ALU.mult, ALU.add).then_inc(S["heads"], 1)
                    v.wait_ge(S["heads"], HEADS * (i + 1))
                    v.wait_ge(S["gelu"], i + 1)
                    nc.vector.tensor_tensor(weight[:], weight[:], gelu[i % 2][:], ALU.mult).then_inc(S["gated"], 1)
                    v.wait_ge(S["out"], i + 1)
                    nc.vector.tensor_tensor(x[:, i, :], x[:, i, :], ps_o[0:TN, :], ALU.add).then_inc(S["added"], 1)


def stage_store(nc, x, out):
    stored = new_semaphore(nc, "x_stored")
    with nc.Block() as block:
        @block.sync
        def _(sp):
            sp.dma_start(out.rearrange("(i p) d -> p i d", p=TN), x[:]).then_inc(stored, 16)
            sp.wait_ge(stored, 16)


STAGES = ("gcn", "moe", "tp", "ode", "sage", "lstm", "bn", "peer")


def build(nc, a, out, stages=STAGES):
    LIVE.clear()
    up_dram = nc.dram_tensor("up_scratch", [N, D], F32, kind="Internal").ap()
    h3_dram = nc.dram_tensor("h3_scratch", [HIDDEN, E], F32, kind="Internal").ap()
    xg = nc.dram_tensor("xg_scratch", [CELLS, 128, N, 16], F32, kind="Internal").ap()
    with ExitStack() as ctx:
        def sb(name, shape, dt=F32):
            return ctx.enter_context(nc.sbuf_tensor(name, shape, dt))
        x = sb("x_rows", [TN, NT, D])
        ident, ones = sb("ident", [128, 128]), sb("ones", [128, 1])
        adj = sb("adj", [TN, NT, N])
        count, dis, rcount = sb("count", [TN, NT]), sb("dis", [TN, NT]), sb("rcount", [TN, NT])
        bounds = sb("bounds", [1, 2 * NT], I32)
        with ExitStack() as graph:
            iota = graph.enter_context(nc.sbuf_tensor("iota", [128, N], I32))
            src_i = graph.enter_context(nc.sbuf_tensor("src_i", [TE, ET], I32))
            dst_f = graph.enter_context(nc.sbuf_tensor("dst_f", [TE, ET], F32))
            stage_constants(nc, a["x"], x, ident, ones, iota)
            stage_graph(nc, a["src_t"], a["dst_t"], a["dst_rows"], iota, ident, ones, src_i, dst_f, adj, count, dis, rcount, bounds)
            if "gcn" in stages:
                layer_gcn(nc, x, ident, adj, dis, a["L0_gnn_W1"], a["L0_gnn_b1"], a["L0_gnn_W2"], a["L0_gnn_b2"])
                end_of_layer(nc)
            cleared = new_semaphore(nc, "diag_cleared")
            with nc.Block() as block:
                @block.vector
                def _(v):
                    for i in range(NT):
                        nc.vector.tensor_tensor(adj[:, i, i * TN:(i + 1) * TN], adj[:, i, i * TN:(i + 1) * TN], ident[0:TN, 0:TN], ALU.subtract).then_inc(cleared, 1)
                    v.wait_ge(cleared, NT)
            if "moe" in stages:
                layer_experts(nc, x, ident, ones, a["L0_ffn_Ws"], a["L0_ffn_bs"], a["L0_ffn_W1"], a["L0_ffn_b1T"], a["L0_ffn_W2"], a["L0_ffn_b2"])
                end_of_layer(nc)
            if "tp" in stages:
                layer_tensor_product(nc, x, ident, iota, src_i, dst_f, bounds, a["attrs_t"], a["feats_t"], a["L1_gnn_W_up0"], a["L1_gnn_W_up1"],
                                     a["L1_gnn_W_mlp1"], a["L1_gnn_W_mlp2"], a["L1_gnn_W_mlp3"], a["L1_gnn_W_mlp4"], a["L1_gnn_W_out0"], a["L1_gnn_W_out1"],
                                     up_dram, h3_dram)
                end_of_layer(nc)
        with nc.sbuf_tensor("whh", [128, CELLS * CELL_COLS], F16) as whh:
            if "ode" in stages or "lstm" in stages:
                layer_ode(nc, x, ident, ones, a["L1_ffn_W1T"], a["L1_ffn_b1"], a["L1_ffn_W2T"], a["L1_ffn_b2"], a["L1_ffn_b2_row"], a["L1_ffn_W3"], a["L1_ffn_W3T"],
                          a["L1_ffn_b3T"], a["L1_ffn_b3"], a["whh_t"], whh)
                end_of_layer(nc)
            if "sage" in stages:
                layer_mean(nc, x, ident, adj, rcount, a["L2_gnn_WT"], a["L2_gnn_b"])
                end_of_layer(nc)
            if "lstm" in stages:
                layer_lstm(nc, x, ident, whh, a["wih_t"], a["bih_t"], a["bhh_t"], a["wsel_h"], a["wsel_x"], a["L2_ffn_b_sel"], a["gsel"], xg)
                end_of_layer(nc)
        if "bn" in stages:
            layer_batchnorm(nc, x, ident, adj, rcount, a["L3_gnn_W_lT"], a["L3_gnn_b_l"], a["L3_gnn_W_rT"], a["L3_gnn_gamma"], a["L3_gnn_beta"])
            end_of_layer(nc)
        if "peer" in stages:
            layer_peer(nc, x, ident, a["L3_ffn_w_q"], a["keys_t"], a["wd_t"], a["wu"])
            end_of_layer(nc)
        stage_store(nc, x, out)


def lay_out(i):
    c = np.ascontiguousarray
    i = {k: np.asarray(v) for k, v in i.items()}
    a = {"x": i["x"]}
    a["src_t"] = i["src"].reshape(ET, TE).T
    a["dst_t"] = i["dst"].reshape(ET, TE).T
    a["dst_rows"] = i["dst"].reshape(UNITS, UNIT)
    a["attrs_t"] = i["edge_attr_4"].reshape(ET, TE, 4).transpose(1, 0, 2).reshape(TE, ET * 4)
    a["feats_t"] = i["edge_attr_8"].T
    for k in ("L0_gnn_W1", "L0_gnn_W2", "L0_ffn_Ws", "L0_ffn_W1", "L0_ffn_W2", "L0_ffn_b2", "L1_gnn_W_up0", "L1_gnn_W_up1", "L1_gnn_W_mlp1",
              "L1_gnn_W_mlp2", "L1_gnn_W_mlp3", "L1_gnn_W_mlp4", "L1_gnn_W_out0", "L1_gnn_W_out1", "L1_ffn_W3", "L3_ffn_w_q"):
        a[k] = i[k]
    for k in ("L0_gnn_b1", "L0_gnn_b2", "L0_ffn_bs", "L1_ffn_b3", "L2_gnn_b", "L2_ffn_b_sel", "L3_gnn_b_l", "L3_gnn_gamma", "L3_gnn_beta"):
        a[k] = i[k].reshape(1, -1)
    for k in ("L1_ffn_b1", "L1_ffn_b2"):
        a[k] = i[k].reshape(-1, 1)
    for k in ("L1_ffn_W1", "L1_ffn_W2", "L1_ffn_W3", "L2_gnn_W", "L3_gnn_W_l", "L3_gnn_W_r"):
        a[k + "T"] = i[k].T
    a["L1_ffn_b2_row"] = i["L1_ffn_b2"].reshape(1, -1)
    a["L0_ffn_b1T"] = i["L0_ffn_b1"].T
    a["L1_ffn_b3T"] = i["L1_ffn_b3"].reshape(KC, 128).T
    a["whh_t"] = i["L2_ffn_W_hh"].transpose(2, 0, 1).reshape(KC, 128, CELLS, GATES).transpose(1, 2, 0, 3).reshape(128, -1)
    a["wih_t"] = i["L2_ffn_W_ih"].transpose(0, 2, 1)
    for k, n in (("bih_t", "L2_ffn_b_ih"), ("bhh_t", "L2_ffn_b_hh")):
        a[k] = i[n].reshape(CELLS, 4, KC, 128).transpose(3, 0, 2, 1).reshape(128, CELLS * 16)
    a["wsel_h"] = i["L2_ffn_W_sel"][:, :2 * D].reshape(CELLS, 2 * KC, 128).transpose(2, 1, 0)
    a["wsel_x"] = i["L2_ffn_W_sel"][:, 2 * D:].reshape(CELLS, KC, 128).transpose(2, 1, 0)
    keys = i["L3_ffn_keys"][:, :, 0, :]
    a["keys_t"] = keys.reshape(2, 4, KEYS, KEY).transpose(1, 3, 0, 2).reshape(128, 2, KEYS)
    a["wd_t"] = i["L3_ffn_weight_down_embed"][:KEYS].T.reshape(KC, 128, KEYS).transpose(1, 0, 2)
    a["wu"] = i["L3_ffn_weight_up_embed"][:KEYS]
    gsel = np.zeros((128, 4), np.float32)
    for j in range(4):
        half = 1.0 if j == 2 else 0.5
        gsel[32 * j:32 * j + 2, GATE_SLOT[j]] = half * 2.0 ** -17
        gsel[32 * j + 2:32 * j + 4, GATE_SLOT[j]] = half * 2.0 ** -28
    a["gsel"] = gsel
    return {k: c(v) for k, v in a.items()}


def kernel(**inputs):
    import concourse.bacc as bacc
    from concourse.bass_utils import run_bass_kernel_spmd

    arrays = lay_out(inputs)
    nc = bacc.Bacc("TRN2", target_bir_lowering=False, num_devices=1)
    args = {k: nc.dram_tensor("in_" + k, v.shape, mybir.dt.from_np(v.dtype), kind="ExternalInput").ap() for k, v in arrays.items()}
    out = nc.dram_tensor("out_x", [N, D], F32, kind="ExternalOutput").ap()
    build(nc, args, out)
    r = run_bass_kernel_spmd(nc, [{"in_" + k: v for k, v in arrays.items()}], core_ids=[0])
    return r.results[0]["out_x"]
```

```python
from contextlib import ExitStack

import numpy as np

import concourse.bass as bass
from concourse import mybir

F32 = mybir.dt.float32
F16 = mybir.dt.float16
BF16 = mybir.dt.bfloat16
I32 = mybir.dt.int32
U32 = mybir.dt.uint32
ALU = mybir.AluOpType
ACT = mybir.ActivationFunctionType
X_AXIS = mybir.AxisListType.X
ds = bass.ds

N = 625
D = 512
NT, TN = 5, 125
KC = D // 128
E = 20000
TE = 125
ET = E // TE
UNIT = 4 * TE
UNITS = E // UNIT
LN_EPS = 1e-5
HALVES = ((0, 313), (313, 312))
BANK = 512
EXPERTS, EXPERT_F = 8, 128
MUL, HIDDEN, RADIAL = 128, 64, 8
SILU_2MOM = 1.679177
CELLS, GATES = 4, 4 * D
CELL_COLS = 2 * KC * GATES
PAD_LOGIT = -1e30
HEADS, KEY, KEYS, TOPK = 8, 32, 256, 16
SENTINEL = -3e38


LIVE = []


def new_semaphore(nc, name):
    sem = nc.alloc_semaphore(name)
    LIVE.append(sem)
    return sem


def end_of_layer(nc):
    nc.clear_and_free_semaphores(LIVE)
    LIVE.clear()
    nc.all_engine_barrier()


def linker(eng, sem):
    count = [0]

    def link(ins):
        count[0] += 1
        ins.then_inc(sem, 1)
        eng.wait_ge(sem, count[0])

    return link


def load_all(nc, name, pairs):
    loaded = new_semaphore(nc, name + "_loaded")
    with nc.Block() as block:
        @block.sync
        def _(sp):
            for dst, src in pairs:
                sp.dma_start(dst, src).then_inc(loaded, 16)
            sp.wait_ge(loaded, 16 * len(pairs))


def stage_constants(nc, x_in, x, ident, ones, iota):
    loaded = new_semaphore(nc, "x_loaded")
    made = new_semaphore(nc, "constants_made")
    with nc.Block() as block:
        @block.sync
        def _(sp):
            sp.dma_start(x[:], x_in.rearrange("(i p) d -> p i d", p=TN)).then_inc(loaded, 16)
            sp.wait_ge(loaded, 16)

        @block.gpsimd
        def _(g):
            nc.gpsimd.memset(ident[:], 0.0).then_inc(made, 1)
            nc.gpsimd.memset(ones[:], 1.0).then_inc(made, 1)
            g.wait_ge(made, 2)
            nc.gpsimd.affine_select(out=ident[:], in_=ident[:], compare_op=ALU.not_equal, fill=1.0, base=0,
                                    pattern=[[-1, 128]], channel_multiplier=1).then_inc(made, 1)
            nc.gpsimd.iota(iota[:], pattern=[[1, N]], base=0, channel_multiplier=0).then_inc(made, 1)
            g.wait_ge(made, 4)


def stage_graph(nc, src_in, dst_in, dst_rows_in, iota, ident, ones, src_i, dst_f, adj, count, dis, rcount, bounds, more):
    RING = 4
    pieces = []
    for i in range(NT):
        at, end = i * N, (i + 1) * N
        while at < end:
            n = min(end, (at // BANK + 1) * BANK) - at
            pieces.append((at, i, at - i * N, n))
            at += n
    with ExitStack() as ctx:
        def sb(name, shape, dt):
            return ctx.enter_context(nc.sbuf_tensor(name, shape, dt))
        dst_i = sb("dst_i", [TE, ET], I32)
        src_f = sb("src_f", [TE, ET], F32)
        iota_h = sb("iota_h", [128, N], F16)
        zeros = sb("zeros_h", [128, BANK], F16)
        hot_s = [sb(f"hot_s{r}", [TE, N], F16) for r in range(RING)]
        hot_d = [sb(f"hot_d{r}", [TE, N], F16) for r in range(RING)]
        rows_i = sb("rows_i", [UNITS, UNIT], I32)
        rows_f = sb("rows_f", [UNITS, UNIT], F32)
        tile_of = sb("tile_of", [UNITS, UNIT], F32)
        hit = sb("hit", [UNITS, UNIT], F32)
        anyhit = sb("anyhit", [UNITS, NT], F32)
        unit_no = sb("unit_no", [UNITS, 1], F32)
        unit_i = sb("unit_i", [UNITS, 1], I32)
        unit_up = sb("unit_up", [UNITS, 1], F32)
        unit_dn = sb("unit_dn", [UNITS, 1], F32)
        votes = sb("votes", [UNITS, 2 * NT], F32)
        best = sb("vote_best", [2 * NT, 1], F32)
        row = sb("vote_row", [1, 2 * NT], F32)
        root = sb("deg_root", [TN, NT], F32)
        t1 = sb("deg_t1", [TN, NT], F32)
        t2 = sb("deg_t2", [TN, NT], F32)
        loaded = new_semaphore(nc, "edges_loaded")
        more_loaded = new_semaphore(nc, "more_loaded")
        ready = new_semaphore(nc, "graph_ready")
        hots = new_semaphore(nc, "hots_ready")
        used = new_semaphore(nc, "hots_used")
        zeroed = new_semaphore(nc, "adj_zeroed")
        unit_made = new_semaphore(nc, "unit_made")
        step = new_semaphore(nc, "graph_dve_step")
        with nc.psum_tensor("ps_adj", [128, 8 * BANK], F32) as ps:
            with nc.Block() as block:
                @block.sync
                def _(sp):
                    sp.dma_start(src_i[:], src_in).then_inc(loaded, 16)
                    sp.dma_start(dst_i[:], dst_in).then_inc(loaded, 16)
                    sp.dma_start(rows_i[:], dst_rows_in).then_inc(loaded, 16)
                    sp.wait_ge(loaded, 48)
                    for dst, src in more:
                        sp.dma_start(dst, src).then_inc(more_loaded, 16)
                    sp.wait_ge(more_loaded, 16 * len(more))

                @block.gpsimd
                def _(g):
                    nc.gpsimd.iota(unit_i[:], pattern=[[1, 1]], base=0, channel_multiplier=1).then_inc(unit_made, 1)

                @block.vector
                def _(v):
                    link = linker(v, step)
                    v.wait_ge(loaded, 48)
                    link(nc.vector.tensor_copy(src_f[:], src_i[:]))
                    link(nc.vector.tensor_copy(dst_f[:], dst_i[:]))
                    link(nc.vector.tensor_copy(rows_f[:], rows_i[:]))
                    link(nc.vector.tensor_copy(iota_h[:], iota[:]))
                    link(nc.vector.memset(zeros[:], 0.0))
                    v.sem_inc(ready, 1)
                    with v.Fori(0, ET // RING) as i:
                        for r in range(RING):
                            v.wait_ge(used, i * RING + (r + 1))
                            nc.vector.tensor_scalar(hot_s[r][:], iota_h[0:TE, :], src_f[:, ds(i * RING + r, 1)], None, ALU.is_equal).then_inc(hots, 1)
                            nc.vector.tensor_scalar(hot_d[r][:], iota_h[0:TE, :], dst_f[:, ds(i * RING + r, 1)], None, ALU.is_equal).then_inc(hots, 1)
                    v.wait_ge(unit_made, 1)
                    link(nc.vector.tensor_copy(unit_no[:], unit_i[:]))
                    link(nc.vector.tensor_scalar(unit_up[:], unit_no[:], 1.0, None, ALU.add))
                    link(nc.vector.tensor_scalar(unit_dn[:], unit_no[:], -1.0, float(UNITS), ALU.mult, ALU.add))
                    link(nc.vector.tensor_scalar(tile_of[:], rows_f[:], float(TN), None, ALU.is_ge))
                    for j in range(2, NT):
                        link(nc.vector.scalar_tensor_tensor(tile_of[:], rows_f[:], float(TN * j), tile_of[:], ALU.is_ge, ALU.add))
                    for j in range(NT):
                        link(nc.vector.tensor_scalar(hit[:], tile_of[:], float(j), None, ALU.is_equal))
                        link(nc.vector.tensor_reduce(anyhit[:, j:j + 1], hit[:], X_AXIS, ALU.max))
                    link(nc.vector.tensor_scalar(votes[:, 0:NT], anyhit[:], unit_dn[:], None, ALU.mult))
                    link(nc.vector.tensor_scalar(votes[:, NT:2 * NT], anyhit[:], unit_up[:], None, ALU.mult))
                    v.wait_ge(used, ET + RING)
                    for i in range(NT):
                        link(nc.vector.tensor_copy(adj[:, i, :], ps[0:TN, i * N:(i + 1) * N]))
                    v.sem_inc(ready, 1)
                    v.wait_ge(zeroed, 1)
                    link(nc.vector.tensor_reduce(best[:], ps[0:2 * NT, 0:UNITS], X_AXIS, ALU.max))
                    v.sem_inc(ready, 1)
                    v.wait_ge(zeroed, 2)
                    link(nc.vector.tensor_copy(row[:], ps[0:1, BANK:BANK + 2 * NT]))
                    link(nc.vector.tensor_scalar(row[:, 0:NT], row[:, 0:NT], -1.0, float(UNITS), ALU.mult, ALU.add))
                    link(nc.vector.tensor_scalar(row[:, 0:NT], row[:, 0:NT], float(UNITS - 1), None, ALU.min))
                    link(nc.vector.tensor_tensor(row[:, NT:2 * NT], row[:, NT:2 * NT], row[:, 0:NT], ALU.subtract))
                    link(nc.vector.tensor_scalar(row[:, NT:2 * NT], row[:, NT:2 * NT], 1.0, None, ALU.max))
                    link(nc.vector.tensor_copy(bounds[:], row[:]))
                    link(nc.vector.tensor_copy(count[:], ps[0:TN, 2 * BANK:2 * BANK + NT]))
                    link(nc.vector.tensor_scalar(t1[:], count[:], 1.0, None, ALU.max))
                    link(nc.vector.reciprocal(rcount[:], t1[:]))
                    link(nc.vector.tensor_scalar(t1[:], count[:], 1.0, None, ALU.add))
                    v.sem_inc(ready, 1)
                    v.wait_ge(zeroed, 3)
                    link(nc.vector.reciprocal(dis[:], root[:]))
                    newton_rsqrt(nc, link, dis[:], t1[:], t2[:])
                    for i in range(NT):
                        link(nc.vector.tensor_tensor(adj[:, i, i * TN:(i + 1) * TN], adj[:, i, i * TN:(i + 1) * TN], ident[0:TN, 0:TN], ALU.add))

                @block.scalar
                def _(a):
                    a.wait_ge(ready, 4)
                    nc.scalar.activation(root[:], t1[:], ACT.Sqrt).then_inc(zeroed, 1)

                @block.tensor
                def _(pe):
                    pe.wait_ge(ready, 1)
                    for b in range(7):
                        m = nc.tensor.matmul(ps[0:TN, b * BANK:(b + 1) * BANK], zeros[:, 0:TN], zeros[:], start=True, stop=False, skip_group_check=True)
                    m.then_inc(used, RING)
                    with pe.Fori(0, ET // RING) as i:
                        for r in range(RING):
                            pe.wait_ge(hots, i * (2 * RING) + (2 * r + 2))
                            for at, s, d0, n in pieces:
                                m = nc.tensor.matmul(ps[0:TN, at:at + n], hot_s[r][:, s * TN:(s + 1) * TN], hot_d[r][:, d0:d0 + n], start=False, stop=True, skip_group_check=True)
                            m.then_inc(used, 1)
                    pe.wait_ge(ready, 2)
                    nc.tensor.transpose(ps[0:2 * NT, 0:UNITS], votes[:], ident[0:UNITS, 0:UNITS]).then_inc(zeroed, 1)
                    pe.wait_ge(ready, 3)
                    nc.tensor.transpose(ps[0:1, BANK:BANK + 2 * NT], best[:], ident[0:2 * NT, 0:2 * NT])
                    for j in range(NT):
                        for s in range(NT):
                            m = nc.tensor.matmul(ps[0:TN, 2 * BANK + j:2 * BANK + j + 1], adj[:, s, j * TN:(j + 1) * TN], ones[0:TN, :], start=(s == 0), stop=(s == NT - 1), skip_group_check=True)
                    m.then_inc(zeroed, 1)


def newton_rsqrt(nc, link, r, v, t):
    link(nc.vector.tensor_tensor(t, r, r, ALU.mult))
    link(nc.vector.tensor_tensor(t, t, v, ALU.mult))
    link(nc.vector.tensor_scalar(t, t, -0.5, 1.5, ALU.mult, ALU.add))
    link(nc.vector.tensor_tensor(r, r, t, ALU.mult))


def stage_layernorm(nc, tag, ident, x, xn, xt=None, chunk=None, tiles=NT):
    chunk = chunk or (lambda c: slice(c * 128, (c + 1) * 128))
    with ExitStack() as ctx:
        stats = ctx.enter_context(nc.sbuf_tensor(tag + "_stats", [TN, tiles, 6], F32))
        mv = ctx.enter_context(nc.sbuf_tensor(tag + "_mv", [TN, tiles, 2], F32))
        var = ctx.enter_context(nc.sbuf_tensor(tag + "_var", [TN, tiles], F32))
        root = ctx.enter_context(nc.sbuf_tensor(tag + "_root", [TN, tiles], F32))
        r = ctx.enter_context(nc.sbuf_tensor(tag + "_r", [TN, tiles], F32))
        t = ctx.enter_context(nc.sbuf_tensor(tag + "_t", [TN, tiles], F32))
        ps = [ctx.enter_context(nc.psum_tensor(f"{tag}_ps{b}", [128, BANK], F32)) for b in range(2)]
        step = new_semaphore(nc, tag + "_step")
        var_ready = new_semaphore(nc, tag + "_var_ready")
        rooted = new_semaphore(nc, tag + "_rooted")
        normed = new_semaphore(nc, tag + "_normed")
        turned = new_semaphore(nc, tag + "_turned")
        moved = new_semaphore(nc, tag + "_moved")
        with nc.Block() as block:
            @block.vector
            def _(v):
                link = linker(v, step)
                for i in range(tiles):
                    last = nc.vector.bn_stats(stats[:, i, :], x[:, i, :])
                link(last)
                for i in range(tiles):
                    last = nc.vector.bn_aggr(mv[:, i, :], stats[:, i, :])
                link(last)
                nc.vector.tensor_scalar(var[:], mv[:, :, 1], LN_EPS, None, ALU.add).then_inc(var_ready, 1)
                v.wait_ge(rooted, 1)
                link(nc.vector.reciprocal(r[:], root[:]))
                newton_rsqrt(nc, link, r[:], var[:], t[:])
                for i in range(tiles):
                    nc.vector.tensor_scalar(xn[:, i, :], x[:, i, :], mv[:, i, 0:1], r[:, i:i + 1], ALU.subtract, ALU.mult).then_inc(normed, 1)

            @block.scalar
            def _(a):
                a.wait_ge(var_ready, 1)
                nc.scalar.activation(root[:], var[:], ACT.Sqrt).then_inc(rooted, 1)
                if xt is not None:
                    for i in range(tiles):
                        a.wait_ge(turned, i + 1)
                        nc.scalar.copy(xt[:, :, i * TN:(i + 1) * TN], ps[i % 2][:, 0:KC * TN].rearrange("p (c n) -> p c n", c=KC)).then_inc(moved, 1)

            if xt is not None:
                @block.tensor
                def _(pe):
                    for i in range(tiles):
                        pe.wait_ge(normed, i + 1)
                        if i >= 2:
                            pe.wait_ge(moved, i - 1)
                        for c in range(KC):
                            m = nc.tensor.transpose(ps[i % 2][:, c * TN:(c + 1) * TN], xn[:, i, chunk(c)], ident[0:TN, 0:TN])
                        m.then_inc(turned, 1)


def stage_aggregate(nc, tag, src, adj, out_t):
    with ExitStack() as ctx:
        ps = [ctx.enter_context(nc.psum_tensor(f"{tag}_ps{b}", [128, BANK], F32)) for b in range(4)]
        summed = new_semaphore(nc, tag + "_summed")
        moved = new_semaphore(nc, tag + "_moved")
        jobs = [(c, at, n) for c in range(KC) for at, n in HALVES]
        with nc.Block() as block:
            @block.tensor
            def _(pe):
                for k, (c, at, n) in enumerate(jobs):
                    if k >= 4:
                        pe.wait_ge(moved, k - 3)
                    for s in range(NT):
                        m = nc.tensor.matmul(ps[k % 4][:, 0:n], src[:, s, c * 128:(c + 1) * 128], adj[:, s, at:at + n], start=(s == 0), stop=(s == NT - 1))
                    m.then_inc(summed, 1)

            @block.scalar
            def _(a):
                for k, (c, at, n) in enumerate(jobs):
                    a.wait_ge(summed, k + 1)
                    nc.scalar.copy(out_t[:, c, at:at + n], ps[k % 4][:, 0:n]).then_inc(moved, 1)


def stage_scale_rows(nc, tag, out, x, col):
    done = new_semaphore(nc, tag + "_scaled")
    with nc.Block() as block:
        @block.vector
        def _(v):
            for i in range(NT):
                nc.vector.tensor_scalar(out[:, i, :], x[:, i, :], col[:, i:i + 1], None, ALU.mult).then_inc(done, 1)
            v.wait_ge(done, NT)


def stage_gcn_project(nc, tag, z_t, w, bias, dis, out, x):
    with ExitStack() as ctx:
        tmp = [ctx.enter_context(nc.sbuf_tensor(f"{tag}_tmp{b}", [TN, D], F32)) for b in range(2)]
        ps = [ctx.enter_context(nc.psum_tensor(f"{tag}_ps{b}", [128, BANK], F32)) for b in range(2)]
        ready = new_semaphore(nc, tag + "_ready")
        read = new_semaphore(nc, tag + "_read")
        done = new_semaphore(nc, tag + "_done")
        with nc.Block() as block:
            @block.tensor
            def _(pe):
                for i in range(NT):
                    if i >= 2:
                        pe.wait_ge(read, i - 1)
                    for c in range(KC):
                        m = nc.tensor.matmul(ps[i % 2][0:TN, :], z_t[:, c, i * TN:(i + 1) * TN], w[:, c, :], start=(c == 0), stop=(c == KC - 1))
                    m.then_inc(ready, 1)

            @block.vector
            def _(v):
                for i in range(NT):
                    v.wait_ge(ready, i + 1)
                    nc.vector.scalar_tensor_tensor(tmp[i % 2][:], ps[i % 2][0:TN, :], dis[:, i:i + 1], bias[:], ALU.mult, ALU.add).then_inc(read, 1)
                    v.wait_ge(read, i + 1)
                    if out is not None:
                        nc.vector.tensor_scalar(out[:, i, :], tmp[i % 2][:], 0.0, dis[:, i:i + 1], ALU.max, ALU.mult).then_inc(done, 1)
                    else:
                        nc.vector.tensor_tensor(x[:, i, :], x[:, i, :], tmp[i % 2][:], ALU.add).then_inc(done, 1)
                v.wait_ge(done, NT)


def rows(vec, parts):
    return vec.broadcast_to([parts, vec.shape[1]])


def weights_gcn(sb, w1_in, b1_in, w2_in, b2_in):
    w1, w2 = sb("gcn_w1", [128, KC, D]), sb("gcn_w2", [128, KC, D])
    b1, b2 = sb("gcn_b1", [TN, D]), sb("gcn_b2", [TN, D])
    return (w1, b1, w2, b2), [(w1[:], w1_in.rearrange("(c k) n -> k c n", k=128)), (w2[:], w2_in.rearrange("(c k) n -> k c n", k=128)),
                              (b1[:], rows(b1_in, TN)), (b2[:], rows(b2_in, TN))]


def layer_gcn(nc, x, ident, adj, dis, w1, b1, w2, b2):
    with ExitStack() as ctx:
        def sb(name, shape):
            return ctx.enter_context(nc.sbuf_tensor(name, shape, F32))
        xn, h, z_t = sb("gcn_xn", [TN, NT, D]), sb("gcn_h", [TN, NT, D]), sb("gcn_zt", [128, KC, N])
        stage_layernorm(nc, "gcn_ln", ident, x, xn)
        stage_scale_rows(nc, "gcn_xs", h, xn, dis)
        stage_aggregate(nc, "gcn_a1", h, adj, z_t)
        stage_gcn_project(nc, "gcn_p1", z_t, w1, b1, dis, h, None)
        stage_aggregate(nc, "gcn_a2", h, adj, z_t)
        stage_gcn_project(nc, "gcn_p2", z_t, w2, b2, dis, None, x)


def weights_experts(sb, ws_in, bs_in, w1_in, b1_in, w2_in, b2_in):
    ws, bs = sb("moe_ws", [128, KC, EXPERTS]), sb("moe_bs", [TN, EXPERTS])
    w1, b1 = sb("moe_w1", [128, EXPERTS, KC, EXPERT_F]), sb("moe_b1", [128, EXPERTS])
    w2, b2 = sb("moe_w2", [128, EXPERTS, D]), sb("moe_b2", [EXPERTS, D])
    return (ws, bs, w1, b1, w2, b2), ([(ws[:], ws_in.rearrange("(c k) e -> k c e", k=128)), (bs[:], rows(bs_in, TN)),
                                       (b1[:], b1_in), (w2[:], w2_in.rearrange("e f d -> f e d")), (b2[:], b2_in)]
                                      + [(w1[:, e], w1_in[e].rearrange("(c k) f -> k c f", k=128)) for e in range(EXPERTS)])


def layer_experts(nc, x, ident, ones, ws, bs, w1, b1, w2, b2):
    with ExitStack() as ctx:
        def sb(name, shape, dt=F32):
            return ctx.enter_context(nc.sbuf_tensor(name, shape, dt))
        xn, xt = sb("moe_xn", [TN, NT, D]), sb("moe_xt", [128, KC, N])
        lg, mx = sb("moe_logits", [TN, NT, EXPERTS]), sb("moe_max", [TN, NT, 8])
        at, atf = sb("moe_at", [TN, NT, 8], U32), sb("moe_atf", [TN, NT])
        neg, total, pmax = sb("moe_neg", [TN, NT]), sb("moe_sum", [TN, NT]), sb("moe_pmax", [TN, NT])
        ex, gate = sb("moe_exp", [TN, NT, EXPERTS]), sb("moe_gate", [TN, NT, EXPERTS])
        no_i, no_f = sb("moe_no_i", [TN, EXPERTS], I32), sb("moe_no", [TN, EXPERTS])
        gate_t = sb("moe_gate_t", [EXPERTS, N])
        h_t = [sb(f"moe_h{b}", [128, N]) for b in range(2)]
        stage_layernorm(nc, "moe_ln", ident, x, xn, xt)
        ps_l = ctx.enter_context(nc.psum_tensor("moe_psl", [128, BANK], F32))
        ps_h = [ctx.enter_context(nc.psum_tensor(f"moe_psh{b}", [128, BANK], F32)) for b in range(2)]
        ps_y = [ctx.enter_context(nc.psum_tensor(f"moe_psy{b}", [128, BANK], F32)) for b in range(4)]
        S = {k: new_semaphore(nc, "moe_" + k) for k in ("step", "no_made", "lg_ready", "neg_ready", "exp_ready", "h_raw", "h_ready", "y_ready", "y_used", "g_turned", "g_moved")}
        with nc.Block() as block:
            @block.gpsimd
            def _(g):
                nc.gpsimd.iota(no_i[:], pattern=[[1, EXPERTS]], base=0, channel_multiplier=0).then_inc(S["no_made"], 1)

            @block.tensor
            def _(pe):
                for i in range(NT):
                    for c in range(KC):
                        m = nc.tensor.matmul(ps_l[0:TN, i * EXPERTS:(i + 1) * EXPERTS], xt[:, c, i * TN:(i + 1) * TN], ws[:, c, :], start=(c == 0), stop=(c == KC - 1), skip_group_check=True)
                m.then_inc(S["lg_ready"], 1)

                def up(e):
                    if e >= 1:
                        pe.wait_ge(S["h_ready"], 2 * e)
                    for b, (a0, n) in enumerate(HALVES):
                        for c in range(KC):
                            m = nc.tensor.matmul(ps_h[b][:, 0:n], w1[:, e, c, :], xt[:, c, a0:a0 + n], start=(c == 0), stop=(c == KC - 1))
                        m.then_inc(S["h_raw"], 1)

                def down(e):
                    pe.wait_ge(S["h_ready"], 2 * e + 2)
                    for i in range(NT):
                        k = e * NT + i
                        if k >= 4:
                            pe.wait_ge(S["y_used"], k - 3)
                        nc.tensor.matmul(ps_y[k % 4][0:TN, :], h_t[e % 2][:, i * TN:(i + 1) * TN], w2[:, e, :], start=True, stop=True).then_inc(S["y_ready"], 1)

                up(0)
                for e in range(EXPERTS):
                    if e + 1 < EXPERTS:
                        up(e + 1)
                    down(e)
                for i in range(NT):
                    k = EXPERTS * NT + i
                    pe.wait_ge(S["y_used"], k - 3)
                    nc.tensor.transpose(ps_y[k % 4][0:EXPERTS, 0:TN], gate[:, i, :], ident[0:TN, 0:TN]).then_inc(S["g_turned"], 1)
                    pe.wait_ge(S["g_moved"], i + 1)
                    nc.tensor.matmul(ps_y[k % 4][0:TN, :], gate_t[:, i * TN:(i + 1) * TN], b2[:], start=True, stop=True).then_inc(S["y_ready"], 1)

            @block.scalar
            def _(a):
                a.wait_ge(S["neg_ready"], 1)
                for i in range(NT):
                    last = nc.scalar.activation(ex[:, i, :], lg[:, i, :], ACT.Exp, bias=neg[:, i:i + 1], accum_out=total[:, i:i + 1])
                last.then_inc(S["exp_ready"], 1)
                for e in range(EXPERTS):
                    if e >= 2:
                        a.wait_ge(S["y_ready"], (e - 1) * NT)
                    for b, (a0, n) in enumerate(HALVES):
                        a.wait_ge(S["h_raw"], 2 * e + b + 1)
                        nc.scalar.activation(h_t[e % 2][:, a0:a0 + n], ps_h[b][:, 0:n], ACT.Gelu, bias=b1[:, e:e + 1]).then_inc(S["h_ready"], 1)
                for i in range(NT):
                    a.wait_ge(S["g_turned"], i + 1)
                    nc.scalar.copy(gate_t[:, i * TN:(i + 1) * TN], ps_y[(EXPERTS * NT + i) % 4][0:EXPERTS, 0:TN]).then_inc(S["g_moved"], 1)

            @block.vector
            def _(v):
                link = linker(v, S["step"])
                v.wait_ge(S["no_made"], 1)
                link(nc.vector.tensor_copy(no_f[:], no_i[:]))
                v.wait_ge(S["lg_ready"], 1)
                for i in range(NT):
                    link(nc.vector.tensor_tensor(lg[:, i, :], ps_l[0:TN, i * EXPERTS:(i + 1) * EXPERTS], bs[:], ALU.add))
                    link(nc.vector.max(mx[:, i, :], lg[:, i, :]))
                    link(nc.vector.max_index(at[:, i, :], mx[:, i, :], lg[:, i, :]))
                link(nc.vector.tensor_scalar(neg[:], mx[:, :, 0], -1.0, None, ALU.mult))
                v.sem_inc(S["neg_ready"], 1)
                link(nc.vector.tensor_copy(atf[:], at[:, :, 0]))
                v.wait_ge(S["exp_ready"], 1)
                link(nc.vector.reciprocal(pmax[:], total[:]))
                for i in range(NT):
                    link(nc.vector.tensor_scalar(gate[:, i, :], no_f[:], atf[:, i:i + 1], pmax[:, i:i + 1], ALU.is_equal, ALU.mult))
                for e in range(EXPERTS):
                    for i in range(NT):
                        v.wait_ge(S["y_ready"], e * NT + i + 1)
                        if e >= 1:
                            v.wait_ge(S["y_used"], (e - 1) * NT + i + 1)
                        nc.vector.scalar_tensor_tensor(x[:, i, :], ps_y[(e * NT + i) % 4][0:TN, :], gate[:, i, e:e + 1], x[:, i, :], ALU.mult, ALU.add).then_inc(S["y_used"], 1)
                for i in range(NT):
                    k = EXPERTS * NT + i
                    v.wait_ge(S["y_ready"], k + 1)
                    v.wait_ge(S["y_used"], k - NT + 1)
                    nc.vector.tensor_tensor(x[:, i, :], x[:, i, :], ps_y[k % 4][0:TN, :], ALU.add).then_inc(S["y_used"], 1)


def stage_edge_mlp(nc, feats_in, w1_in, w2_in, w3_in, h3_dram):
    CH = 500
    ROUNDS = E // CH // 4
    with ExitStack() as ctx:
        def sb(name, shape, dt=F32):
            return ctx.enter_context(nc.sbuf_tensor(name, shape, dt))
        w1, w2, w3 = sb("mlp_w1", [2 * RADIAL, 2 * HIDDEN]), sb("mlp_w2", [2 * HIDDEN, 2 * HIDDEN]), sb("mlp_w3", [2 * HIDDEN, 2 * HIDDEN])
        f = [sb(f"mlp_f{b}", [2 * RADIAL, CH]) for b in range(2)]
        h = [[sb(f"mlp_h{b}{l}", [2 * HIDDEN, CH]) for l in range(3)] for b in range(2)]
        warm = sb("mlp_warm", [1, 1])
        ps = [[ctx.enter_context(nc.psum_tensor(f"mlp_ps{b}{l}", [128, BANK], F32)) for l in range(3)] for b in range(2)]
        cleared = new_semaphore(nc, "mlp_cleared")
        with nc.Block() as block:
            @block.vector
            def _(v):
                for w in (w1, w2, w3):
                    nc.vector.memset(w[:], 0.0).then_inc(cleared, 1)
                nc.vector.memset(warm[:], 0.0).then_inc(cleared, 1)
                v.wait_ge(cleared, 4)
        load_all(nc, "mlp", [(w[half * k:(half + 1) * k, half * HIDDEN:(half + 1) * HIDDEN], w_in)
                             for w, w_in, k in ((w1, w1_in, RADIAL), (w2, w2_in, HIDDEN), (w3, w3_in, HIDDEN)) for half in range(2)])
        fed = [new_semaphore(nc, f"mlp_fed{b}") for b in range(2)]
        stored = [new_semaphore(nc, f"mlp_stored{b}") for b in range(2)]
        raw = [new_semaphore(nc, f"mlp_raw{b}") for b in range(2)]
        acted = [new_semaphore(nc, f"mlp_acted{b}") for b in range(2)]
        seen = new_semaphore(nc, "mlp_seen")
        scales = (1 / RADIAL ** 0.5, SILU_2MOM / HIDDEN ** 0.5, SILU_2MOM / HIDDEN ** 0.5)
        with nc.Block() as block:
            @block.sync
            def _(sp):
                with sp.Fori(0, ROUNDS) as i:
                    for b in range(2):
                        sp.wait_ge(acted[b], i * 3 + 6)
                        for half in range(2):
                            sp.dma_start(h3_dram[:, ds(i * (4 * CH) + (2 * b + half) * CH, CH)], h[b][2][half * HIDDEN:(half + 1) * HIDDEN, :]).then_inc(stored[b], 16)
                for b in range(2):
                    sp.wait_ge(stored[b], 32 * ROUNDS + 32)

            @block.gpsimd
            def _(g):
                with g.Fori(0, ROUNDS) as i:
                    for b in range(2):
                        g.wait_ge(acted[b], i * 3 + 1)
                        for half in range(2):
                            g.dma_start(f[b][half * RADIAL:(half + 1) * RADIAL, :], feats_in[:, ds(i * (4 * CH) + (2 * b + half) * CH, CH)]).then_inc(fed[b], 16)

            @block.tensor
            def _(pe):
                with pe.Fori(0, ROUNDS) as i:
                    for l in range(3):
                        for b in range(2):
                            if l == 0:
                                pe.wait_ge(fed[b], i * 32 + 32)
                            pe.wait_ge(acted[b], i * 3 + (l + 3 if l else 1))
                            nc.tensor.matmul(ps[b][l][:, 0:CH], (w1, w2, w3)[l][:], f[b][:] if l == 0 else h[b][l - 1][:], start=True, stop=True).then_inc(raw[b], 1)

            @block.scalar
            def _(a):
                nc.scalar.activation(warm[:], warm[:], ACT.Silu)
                for b in range(2):
                    a.sem_inc(acted[b], 3)
                    a.sem_inc(stored[b], 32)
                with a.Fori(0, ROUNDS) as i:
                    for l in range(3):
                        for b in range(2):
                            a.wait_ge(raw[b], i * 3 + (l + 1))
                            if l == 2:
                                a.wait_ge(stored[b], i * 32 + 32)
                            nc.scalar.activation(h[b][l][:], ps[b][l][:, 0:CH], ACT.Silu, scale=scales[l]).then_inc(acted[b], 1)


def stage_up(nc, xt, up0_in, up1_in, up_dram):
    with ExitStack() as ctx:
        w0 = ctx.enter_context(nc.sbuf_tensor("up_w0", [MUL, MUL], F32))
        w1 = ctx.enter_context(nc.sbuf_tensor("up_w1", [MUL, MUL], F32))
        up = ctx.enter_context(nc.sbuf_tensor("up_rows", [TN, NT, D], F32))
        ps = [ctx.enter_context(nc.psum_tensor(f"up_ps{b}", [128, BANK], F32)) for b in range(NT)]
        load_all(nc, "up", [(w0[:], up0_in), (w1[:], up1_in)])
        ready, moved, stored = (new_semaphore(nc, "up_" + k) for k in ("ready", "moved", "stored"))
        with nc.Block() as block:
            @block.tensor
            def _(pe):
                for i in range(NT):
                    for c in range(4):
                        m = nc.tensor.matmul(ps[i][0:TN, c * MUL:(c + 1) * MUL], xt[:, c, i * TN:(i + 1) * TN], (w0 if c == 0 else w1)[:], start=True, stop=True, skip_group_check=True)
                    m.then_inc(ready, 1)

            @block.vector
            def _(v):
                for i in range(NT):
                    v.wait_ge(ready, i + 1)
                    nc.vector.tensor_scalar(up[:, i, :], ps[i][0:TN, :], MUL ** -0.5, None, ALU.mult).then_inc(moved, 1)

            @block.sync
            def _(sp):
                sp.wait_ge(moved, NT)
                sp.dma_start(up_dram.rearrange("(i p) d -> p i d", p=TN), up[:]).then_inc(stored, 16)
                sp.wait_ge(stored, 16)


def stage_messages(nc, j, up_dram, h3_dram, w4, src_i, dst_f, y, y3, iota, zeros, bounds, msg):
    tag = f"msg{j}"
    T = UNIT // TE
    with ExitStack() as ctx:
        def sb(name, shape, dt=F32):
            return ctx.enter_context(nc.sbuf_tensor(f"{tag}_{name}", shape, dt))
        idx = [sb(f"idx{a}", [TE, 1], I32) for a in range(T)]
        snd = [sb(f"snd{a}", [TE, D]) for a in range(T)]
        h3 = [sb(f"h3{b}", [HIDDEN, 2 * TE]) for b in range(T // 2)]
        hot = [sb(f"hot{a}", [TE, TN]) for a in range(2)]
        ws0 = [sb(f"ws0{a}", [TE, MUL]) for a in range(2)]
        dot = [sb(f"dot{a}", [TE, MUL]) for a in range(2)]
        m = [sb(f"m{a}", [TE, 1024]) for a in range(2)]
        ps_w = [ctx.enter_context(nc.psum_tensor(f"{tag}_psw{a}", [128, BANK], F32)) for a in range(T)]
        acc = [ctx.enter_context(nc.psum_tensor(f"{tag}_acc{a}", [128, BANK], F32)) for a in range(2)]
        S = {k: new_semaphore(nc, f"{tag}_{k}") for k in ("hot", "tpw", "ws0", "dot", "vec", "p2", "summed", "idx", "out", "seen", "cleared")}
        h3_in = [new_semaphore(nc, f"{tag}_h3_in{b}") for b in range(T // 2)]
        snd_in = [new_semaphore(nc, f"{tag}_snd_in{a}") for a in range(T)]
        first_max, count_max = UNITS - 1, UNITS

        def bound(eng, k, lo, hi):
            return eng.snap(eng.value_load(bounds[0:1, k:k + 1], min_val=lo, max_val=hi), min_val=lo, max_val=hi)

        with nc.Block() as block:
            @block.sync
            def _(sp):
                first, count = bound(sp, j, 0, first_max), bound(sp, NT + j, 1, count_max)
                with sp.Fori(0, count) as i:
                    unit = nc.s_assert_within(first + i, 0, first_max, skip_runtime_bounds_check_because="first + count is at most the number of units")
                    for b in range(T // 2):
                        sp.wait_ge(S["tpw"], i * T + (2 * b + 2))
                        sp.dma_start(h3[b][:], h3_dram[:, ds(unit * UNIT + b * (2 * TE), 2 * TE)]).then_inc(h3_in[b], 16)

            @block.gpsimd
            def _(g):
                first, count = bound(g, j, 0, first_max), bound(g, NT + j, 1, count_max)
                with g.Fori(0, count) as i:
                    unit = nc.s_assert_within(first + i, 0, first_max, skip_runtime_bounds_check_because="first + count is at most the number of units")
                    for a in range(T):
                        g.wait_ge(S["vec"], i * T + (a + 1))
                        nc.gpsimd.tensor_copy(idx[a][:], src_i[:, ds(unit * T + a, 1)]).then_inc(S["idx"], 1)
                        g.wait_ge(S["idx"], i * T + (a + 1))
                        g.sem_inc(S["seen"], 1)
                        nc.gpsimd.indirect_dma_start(out=snd[a][:], out_offset=None, in_=up_dram,
                                                     in_offset=bass.IndirectOffsetOnAxis(ap=idx[a][:].bitcast(U32), axis=0)).then_inc(snd_in[a], 16)

            @block.tensor
            def _(pe):
                count = bound(pe, NT + j, 1, count_max)
                for b in range(2):
                    nc.tensor.matmul(acc[b][0:TN, :], zeros[:, 0:TN], zeros[:], start=True, stop=False, skip_group_check=True)
                pe.sem_inc(S["tpw"], T)

                def add_up(a):
                    for b in range(2):
                        mm = nc.tensor.matmul(acc[b][0:TN, :], hot[a % 2][:], m[a % 2][:, b * BANK:(b + 1) * BANK], start=False, stop=True, skip_group_check=True)
                    mm.then_inc(S["summed"], 1)

                with pe.Fori(0, count) as i:
                    for a in range(T):
                        if a % 2 == 0:
                            pe.wait_ge(h3_in[a // 2], i * 16 + 16)
                        pe.wait_ge(S["vec"], i * T + (a + 1))
                        nc.tensor.matmul(ps_w[a][0:TE, :], h3[a // 2][:, (a % 2) * TE:(a % 2 + 1) * TE], w4[:], start=True, stop=True).then_inc(S["tpw"], 1)
                        pe.wait_ge(S["vec"], i * T + (a + T))
                        pe.wait_ge(S["p2"], i * T + (a + T))
                        add_up(a - 1)
                pe.wait_ge(S["vec"], count * T + T)
                pe.wait_ge(S["p2"], count * T + T)
                add_up(T - 1)

            @block.scalar
            def _(s):
                first, count = bound(s, j, 0, first_max), bound(s, NT + j, 1, count_max)
                s.sem_inc(S["p2"], T)
                with s.Fori(0, count) as i:
                    unit = nc.s_assert_within(first + i, 0, first_max, skip_runtime_bounds_check_because="first + count is at most the number of units")
                    for a in range(T):
                        s.wait_ge(S["ws0"], i * T + (a + 1))
                        s.wait_ge(S["summed"], i * T + (a + 2))
                        for k, at in enumerate((256, 512, 768)):
                            last = nc.scalar.activation(m[a % 2][:, at:at + 128], ws0[a % 2][:], ACT.Copy, scale=y[:, ds(unit * (4 * T) + (a * 4 + 1 + k), 1)])
                        last.then_inc(S["p2"], 1)

            @block.vector
            def _(v):
                first, count = bound(v, j, 0, first_max), bound(v, NT + j, 1, count_max)
                nc.vector.memset(m[1][:], 0.0).then_inc(S["cleared"], 1)
                nc.vector.memset(hot[1][:], 0.0).then_inc(S["cleared"], 1)
                v.wait_ge(S["cleared"], 2)
                v.sem_inc(S["vec"], T)
                v.sem_inc(S["summed"], 2)
                with v.Fori(0, count) as i:
                    unit = nc.s_assert_within(first + i, 0, first_max, skip_runtime_bounds_check_because="first + count is at most the number of units")
                    for a in range(T):
                        y_at = lambda q: y[:, ds(unit * (4 * T) + (a * 4 + q), 1)]
                        y3_at = lambda q: y3[:, ds(unit * (4 * T) + (a * 4 + q), 1)]
                        w = lambda q: ps_w[a][0:TE, q * MUL:(q + 1) * MUL]
                        v.wait_ge(S["summed"], i * T + (a + 2))
                        nc.vector.tensor_scalar(hot[a % 2][:], iota[0:TE, j * TN:(j + 1) * TN], dst_f[:, ds(unit * T + a, 1)], None, ALU.is_equal).then_inc(S["hot"], 1)
                        v.wait_ge(snd_in[a], i * 16 + 16)
                        s0 = snd[a][:, 0:MUL]
                        s1 = lambda q: snd[a][:, MUL * (q + 1):MUL * (q + 2)]
                        nc.vector.tensor_scalar(dot[a % 2][:], s1(0), y3_at(1), None, ALU.mult).then_inc(S["dot"], 1)
                        v.wait_ge(S["tpw"], i * T + (a + T + 1))
                        nc.vector.tensor_tensor(ws0[a % 2][:], w(1), s0, ALU.mult).then_inc(S["ws0"], 1)
                        v.wait_ge(S["dot"], i * (3 * T) + (3 * a + 1))
                        nc.vector.scalar_tensor_tensor(dot[a % 2][:], s1(1), y3_at(2), dot[a % 2][:], ALU.mult, ALU.add).then_inc(S["dot"], 1)
                        nc.vector.scalar_tensor_tensor(m[a % 2][:, 0:128], w(0), y_at(0), s0, ALU.mult, ALU.mult).then_inc(S["out"], 1)
                        v.wait_ge(S["dot"], i * (3 * T) + (3 * a + 2))
                        nc.vector.scalar_tensor_tensor(dot[a % 2][:], s1(2), y3_at(3), dot[a % 2][:], ALU.mult, ALU.add).then_inc(S["dot"], 1)
                        p3 = m[a % 2][:, 256:1024].rearrange("p (c k f) -> p c k f", c=3, k=2)[:, :, 1, :]
                        nc.vector.scalar_tensor_tensor(p3, w(2).unsqueeze(1).broadcast_to([TE, 3, MUL]), y_at(0),
                                                       snd[a][:, MUL:D].rearrange("p (c f) -> p c f", c=3), ALU.mult, ALU.mult).then_inc(S["out"], 1)
                        v.wait_ge(S["dot"], i * (3 * T) + (3 * a + 3))
                        nc.vector.tensor_tensor(m[a % 2][:, 128:256], w(3), dot[a % 2][:], ALU.mult).then_inc(S["vec"], 1)
                v.wait_ge(S["summed"], count * T + 3)
                for b in range(2):
                    nc.vector.tensor_copy(msg[:, j, b * BANK:(b + 1) * BANK], acc[b][0:TN, :]).then_inc(S["hot"], 1)


def stage_message_out(nc, msg, wo0_in, wo1_in, ident, x):
    with ExitStack() as ctx:
        w0 = ctx.enter_context(nc.sbuf_tensor("out_w0", [128, 2, MUL], F32))
        w1 = ctx.enter_context(nc.sbuf_tensor("out_w1", [128, 2, MUL], F32))
        mt = [ctx.enter_context(nc.sbuf_tensor(f"out_mt{b}", [128, 8, TN], F32)) for b in range(2)]
        ps_t = [ctx.enter_context(nc.psum_tensor(f"out_pst{b}", [128, BANK], F32)) for b in range(4)]
        ps_o = [ctx.enter_context(nc.psum_tensor(f"out_pso{b}", [128, BANK], F32)) for b in range(2)]
        load_all(nc, "mout", [(w0[:], wo0_in.rearrange("(c k) n -> k c n", k=128)), (w1[:], wo1_in.rearrange("(c k) n -> k c n", k=128))])
        turned, moved, ready, used = (new_semaphore(nc, "mout_" + k) for k in ("turned", "moved", "ready", "used"))
        scale = (2 * MUL) ** -0.5 / 10.0
        with nc.Block() as block:
            @block.tensor
            def _(pe):
                for i in range(NT):
                    for b in range(2):
                        k = 2 * i + b
                        if k >= 4:
                            pe.wait_ge(moved, k - 3)
                        for c in range(4):
                            m = nc.tensor.transpose(ps_t[k % 4][:, c * TN:(c + 1) * TN], msg[:, i, (4 * b + c) * 128:(4 * b + c + 1) * 128], ident[0:TN, 0:TN])
                        m.then_inc(turned, 1)
                    pe.wait_ge(moved, 2 * i + 2)
                    if i >= 2:
                        pe.wait_ge(used, i - 1)
                    for c in range(4):
                        for half in range(2):
                            m = nc.tensor.matmul(ps_o[i % 2][0:TN, c * MUL:(c + 1) * MUL], mt[i % 2][:, 2 * c + half, :], (w0 if c == 0 else w1)[:, half, :], start=(half == 0), stop=(half == 1), skip_group_check=True)
                    m.then_inc(ready, 1)

            @block.scalar
            def _(a):
                for i in range(NT):
                    if i >= 2:
                        a.wait_ge(ready, i - 1)
                    for b in range(2):
                        k = 2 * i + b
                        a.wait_ge(turned, k + 1)
                        nc.scalar.copy(mt[i % 2][:, 4 * b:4 * b + 4, :], ps_t[k % 4][:, 0:4 * TN].rearrange("p (c n) -> p c n", c=4)).then_inc(moved, 1)

            @block.vector
            def _(v):
                for i in range(NT):
                    v.wait_ge(ready, i + 1)
                    nc.vector.scalar_tensor_tensor(x[:, i, 0:MUL], ps_o[i % 2][0:TN, 0:MUL], scale, x[:, i, 0:MUL], ALU.mult, ALU.add)
                    vec = x[:, i, MUL:D].rearrange("p (u m) -> p m u", m=3)
                    nc.vector.scalar_tensor_tensor(vec, ps_o[i % 2][0:TN, MUL:D].rearrange("p (m u) -> p m u", m=3), scale, vec, ALU.mult, ALU.add).then_inc(used, 1)


def layer_tensor_product(nc, x, ident, iota, src_i, dst_f, bounds, attrs_in, feats_in, up0_in, up1_in, w1_in, w2_in, w3_in, w4_in,
                         wo0_in, wo1_in, up_dram, h3_dram):
    stage_edge_mlp(nc, feats_in, w1_in, w2_in, w3_in, h3_dram)
    with ExitStack() as ctx:
        def sb(name, shape, dt=F32):
            return ctx.enter_context(nc.sbuf_tensor(name, shape, dt))
        y, y3, w4 = sb("tp_y", [TE, ET * 4]), sb("tp_y3", [TE, ET * 4]), sb("tp_w4", [HIDDEN, D])
        xn, xt = sb("tp_xn", [TN, NT, D]), sb("tp_xt", [128, 4, N])
        zeros, msg, iota_f = sb("tp_zeros", [128, BANK]), sb("tp_msg", [TN, NT, 1024]), sb("tp_iota", [128, N])
        load_all(nc, "tp", [(y[:], attrs_in), (w4[:], w4_in)])
        stage_layernorm(nc, "tp_ln", ident, x, xn, xt, lambda c: slice(0, MUL) if c == 0 else slice(MUL + c - 1, D, 3))
        stage_up(nc, xt, up0_in, up1_in, up_dram)
        step = new_semaphore(nc, "tp_step")
        with nc.Block() as block:
            @block.vector
            def _(v):
                link = linker(v, step)
                link(nc.vector.tensor_scalar(y[:], y[:], SILU_2MOM / HIDDEN ** 0.5, None, ALU.mult))
                link(nc.vector.tensor_scalar(y3[:], y[:], 3.0 ** -0.5, None, ALU.mult))
                link(nc.vector.memset(zeros[:], 0.0))
                link(nc.vector.tensor_copy(iota_f[:], iota[:]))
        for j in range(NT):
            stage_messages(nc, j, up_dram, h3_dram, w4, src_i, dst_f, y, y3, iota_f, zeros, bounds, msg)
        stage_message_out(nc, msg, wo0_in, wo1_in, ident, x)


def layer_ode(nc, x, ident, ones, w1t_in, b1_in, w2t_in, b2_in, b2_row_in, w3_in, w3t_in, b3_in, b3_row_in, whh_in, whh):
    STEPS = N - 1
    DT = 1.0 / STEPS
    UN = 4
    CHUNK = GATES // 2
    with ExitStack() as ctx:
        def sb(name, shape, dt=F32):
            return ctx.enter_context(nc.sbuf_tensor(name, shape, dt))
        xn, xt = sb("ode_xn", [TN, 1, D]), sb("ode_xt", [128, KC, TN])
        w1t, w2t, w3, w3t = sb("ode_w1t", [128, KC, 128]), sb("ode_w2t", [128, 128]), sb("ode_w3", [128, KC, 128]), sb("ode_w3t", [128, D])
        b1, b2, b3, b3r = sb("ode_b1", [128, 1]), sb("ode_b2", [128, 1]), sb("ode_b3", [128, KC]), sb("ode_b3r", [1, D])
        mt_half, mt_full, mt_sixth = (sb("ode_mt" + k, [128, 128]) for k in ("_half", "_full", "_sixth"))
        m0h, m0f, z0, zh, zf = (sb("ode_" + k, [128, 1]) for k in ("m0h", "m0f", "z0", "zh", "zf"))
        b2_wide, m0_wide = (sb("ode_" + k, [96, 128]) for k in ("b2_wide", "m0_wide"))
        b3_wide = sb("ode_b3_wide", [128, KC, 96])
        b2_parts, m0_parts, part16 = (sb("ode_" + k, [96, 128], BF16) for k in ("b2_parts", "m0_parts", "part16"))
        ones16 = sb("ode_ones16", [96, 1], BF16)
        a_col = sb("ode_a", [128, 1])
        warm = sb("ode_warm", [128, 1])
        busy_w, busy_x = sb("ode_busy_w", [128, 128], F16), sb("ode_busy_x", [128, 512], F16)
        b_col = [sb(f"ode_b_{q}", [128, 4]) for q in range(2)]
        part, psum_b = sb("ode_part", [128, 1]), sb("ode_p", [128, 1])
        sums = sb("ode_sums", [128, N])
        sums2 = sb("ode_sums2", [128, N])
        ramp_i, ramp = sb("ode_ramp_i", [1, N], I32), sb("ode_ramp", [1, N])
        onesrow = sb("ode_ones", [1, TN])
        ps_a, ps_u, ps_z = (ctx.enter_context(nc.psum_tensor("ode_ps" + k, [128, BANK], F32)) for k in "auz")
        ps_o = [ctx.enter_context(nc.psum_tensor(f"ode_pso{b}", [128, BANK], F32)) for b in range(2)]
        BUSY, BUSY_A, BUSY_B = 2, 512, 288
        ps_busy = ctx.enter_context(nc.psum_tensor("ode_busy", [128, BANK], F32))
        load_all(nc, "ode", [(w1t[:], w1t_in.rearrange("(c k) n -> k c n", k=128)), (w2t[:], w2t_in), (w3[:], w3_in.rearrange("(c k) n -> k c n", k=128)),
                             (w3t[:], w3t_in), (b1[:], b1_in), (b2[:], b2_in), (b3[:], b3_in), (b3r[:], b3_row_in),
                             (b2_wide[:], rows(b2_row_in, 96))])
        stage_layernorm(nc, "ode_ln", ident, x, xn, xt, tiles=1)
        S = {k: new_semaphore(nc, "ode_" + k) for k in ("step", "made", "b3_wide", "ps", "ps_z0", "setup", "a", "b", "wa", "wu", "wz", "zb", "p", "s", "out", "outused")}
        with nc.Block() as block:
            @block.gpsimd
            def _(g):
                nc.gpsimd.iota(ramp_i[:], pattern=[[1, N]], base=0, channel_multiplier=0).then_inc(S["made"], 1)
                nc.gpsimd.memset(onesrow[:], 1.0).then_inc(S["made"], 1)
                nc.gpsimd.memset(ones16[:], 1.0).then_inc(S["made"], 1)

            @block.tensor
            def _(pe):
                for c in range(KC):
                    m = nc.tensor.matmul(ps_a[:, 0:128], w3[:, c, :], w1t[:, c, :], start=(c == 0), stop=(c == KC - 1))
                m.then_inc(S["ps"], 1)
                for c in range(KC):
                    nc.tensor.matmul(ps_u[:, 0:1], w1t[:, c, :], b3[:, c:c + 1], start=(c == 0), stop=(c == KC - 1))
                for c in range(KC):
                    m = nc.tensor.matmul(ps_z[:, 0:1], w1t[:, c, :], xt[:, c, 0:1], start=(c == 0), stop=(c == KC - 1))
                m.then_inc(S["ps"], 1)
                pe.wait_ge(S["b3_wide"], KC)
                for c in range(KC):
                    m = nc.tensor.matmul(ps_o[0][0:96, 0:128], b3_wide[:, c, :], w1t[:, c, :], start=(c == 0), stop=(c == KC - 1))
                m.then_inc(S["ps"], 1)

            @block.vector
            def _(v):
                link = linker(v, S["step"])

                def split_rows(wide, parts):
                    link(nc.vector.memset(parts[:], 0.0))
                    for p in (0, 32, 64):
                        link(nc.vector.tensor_copy(part16[:], wide[:]))
                        link(nc.vector.tensor_copy(parts[p:p + 1, :], part16[p:p + 1, :]))
                        link(nc.vector.tensor_tensor(wide[:], wide[:], part16[:], ALU.subtract))

                link(nc.vector.memset(b3_wide[:], 0.0))
                for c in range(KC):
                    nc.vector.tensor_scalar(b3_wide[:, c, :], b3_wide[:, c, :], b3[:, c:c + 1], None, ALU.add).then_inc(S["b3_wide"], 1)
                split_rows(b2_wide, b2_parts)
                v.wait_ge(S["ps"], 3)
                link(nc.vector.tensor_scalar(m0_wide[:], ps_o[0][0:96, 0:128], DT, None, ALU.mult))
                split_rows(m0_wide, m0_parts)
                link(nc.vector.tensor_scalar(mt_half[:], ps_a[:, 0:128], DT / 2, None, ALU.mult))
                link(nc.vector.tensor_scalar(mt_full[:], ps_a[:, 0:128], DT, None, ALU.mult))
                link(nc.vector.tensor_scalar(mt_sixth[:], ps_a[:, 0:128], DT / 6, None, ALU.mult))
                link(nc.vector.tensor_scalar(m0f[:], ps_u[:, 0:1], DT, None, ALU.mult))
                link(nc.vector.tensor_scalar(m0h[:], ps_u[:, 0:1], DT / 2, None, ALU.mult))
                link(nc.vector.tensor_tensor(z0[:], ps_z[:, 0:1], b1[:], ALU.add))
                link(nc.vector.memset(sums[:, 0:1], 0.0))
                link(nc.vector.memset(busy_w[:], 0.0))
                link(nc.vector.memset(busy_x[:], 0.0))
                v.wait_ge(S["made"], 3)
                link(nc.vector.tensor_copy(ramp[:], ramp_i[:]))
                link(nc.vector.tensor_scalar(ramp[:], ramp[:], DT, None, ALU.mult))
        with nc.Block() as block:
            @block.tensor
            def _(pe):
                def busy(cols):
                    for _ in range(BUSY):
                        nc.tensor.matmul(ps_busy[:, 0:cols], busy_w[:], busy_x[:, 0:cols], start=True, stop=True)

                for _ in range(16):
                    busy(BANK)
                nc.tensor.matmul(ps_z[:, 0:1], ident[:], z0[:], start=True, stop=True).then_inc(S["wz"], 1)
                nc.tensor.matmul(ps_a[:, 0:1], b2_parts[:], ones16[:], start=True, stop=False, skip_group_check=True)
                with pe.Fori(0, STEPS // UN) as i:
                    for r in range(UN):
                        k = i * (4 * UN) + 4 * r
                        q = r % 2
                        for s in range(4):
                            busy(BUSY_A)
                            pe.wait_ge(S["a"], k + (s + 1))
                            nc.tensor.matmul(ps_a[:, 0:1], w2t[:], a_col[:], start=False, stop=True, skip_group_check=True).then_inc(S["wa"], 1)
                            if s < 3:
                                if s == 0:
                                    pe.wait_ge(S["zb"], i * UN + (r + 1))
                                nc.tensor.matmul(ps_u[:, 0:1], ident[:], (zf if s == 2 else zh)[:], start=True, stop=False, skip_group_check=True)
                            else:
                                nc.tensor.matmul(ps_z[:, 0:1], m0_parts[:], ones16[:], start=False, stop=False, skip_group_check=True)
                                pe.wait_ge(S["p"], i * UN + (r + 1))
                                nc.tensor.matmul(ps_z[:, 0:1], mt_sixth[:], psum_b[:], start=False, stop=False, skip_group_check=True)
                            busy(BUSY_B)
                            pe.wait_ge(S["b"], k + (s + 1))
                            if s < 3:
                                nc.tensor.matmul(ps_u[:, 0:1], (mt_full if s == 2 else mt_half)[:], b_col[q][:, s:s + 1], start=False, stop=True, skip_group_check=True).then_inc(S["wu"], 1)
                            else:
                                nc.tensor.matmul(ps_z[:, 0:1], mt_sixth[:], b_col[q][:, 3:4], start=False, stop=True, skip_group_check=True).then_inc(S["wz"], 1)
                            nc.tensor.matmul(ps_a[:, 0:1], b2_parts[:], ones16[:], start=True, stop=False, skip_group_check=True)

            @block.scalar
            def _(a):
                nc.scalar.activation(warm[:], b2[:], ACT.Tanh)
                with a.Fori(0, STEPS // UN) as i:
                    for r in range(UN):
                        q = r % 2
                        for s in range(4):
                            if s == 0:
                                a.wait_ge(S["wz"], i * UN + (r + 1))
                                nc.scalar.activation(a_col[:], ps_z[:, 0:1], ACT.Tanh).then_inc(S["a"], 1)
                            else:
                                a.wait_ge(S["wu"], i * (3 * UN) + (3 * r + s))
                                nc.scalar.activation(a_col[:], ps_u[:, 0:1], ACT.Tanh).then_inc(S["a"], 1)
                            a.wait_ge(S["wa"], i * (4 * UN) + (4 * r + s + 1))
                            nc.scalar.activation(b_col[q][:, s:s + 1], ps_a[:, 0:1], ACT.Tanh).then_inc(S["b"], 1)

            @block.vector
            def _(v):
                with v.Fori(0, STEPS // UN) as i:
                    for r in range(UN):
                        q = r % 2
                        kb = i * (4 * UN) + 4 * r
                        v.wait_ge(S["a"], kb + 1)
                        nc.vector.tensor_tensor(zh[:], ps_z[:, 0:1], m0h[:], ALU.add)
                        nc.vector.tensor_tensor(zf[:], ps_z[:, 0:1], m0f[:], ALU.add).then_inc(S["zb"], 1)
                        v.wait_ge(S["b"], kb + 2)
                        nc.vector.scalar_tensor_tensor(part[:], b_col[q][:, 1:2], 2.0, b_col[q][:, 0:1], ALU.mult, ALU.add).then_inc(S["s"], 1)
                        v.wait_ge(S["b"], kb + 3)
                        v.wait_ge(S["s"], i * UN + (r + 1))
                        nc.vector.scalar_tensor_tensor(psum_b[:], b_col[q][:, 2:3], 2.0, part[:], ALU.mult, ALU.add).then_inc(S["p"], 1)
                        v.wait_ge(S["b"], kb + 4)
                        v.wait_ge(S["p"], i * UN + (r + 1))
                        nc.vector.tensor_tensor(sums[:, ds(i * UN + (r + 1), 1)], psum_b[:], b_col[q][:, 3:4], ALU.add).then_inc(S["out"], 1)

            split_weights(nc, block, ctx, whh_in, whh)
        with nc.Block() as block:
            @block.vector
            def _(v):
                link = linker(v, new_semaphore(nc, "ode_scan"))
                a_buf, b_buf, w = sums, sums2, 1
                while w < N:
                    link(nc.vector.tensor_copy(b_buf[:, 0:w], a_buf[:, 0:w]))
                    link(nc.vector.tensor_tensor(b_buf[:, w:N], a_buf[:, w:N], a_buf[:, 0:N - w], ALU.add))
                    a_buf, b_buf, w = b_buf, a_buf, 2 * w
                assert a_buf is sums
                link(nc.vector.tensor_scalar(sums[:], sums[:], DT / 6, None, ALU.mult))
                v.sem_inc(S["setup"], 1)
                for i in range(NT):
                    v.wait_ge(S["ps_z0"], i + 1)
                    nc.vector.tensor_tensor(x[:, i, :], x[:, i, :], ps_o[i % 2][0:TN, :], ALU.add).then_inc(S["outused"], 1)

            @block.tensor
            def _(pe):
                pe.wait_ge(S["setup"], 1)
                for i in range(NT):
                    if i >= 2:
                        pe.wait_ge(S["outused"], i - 1)
                    nc.tensor.matmul(ps_o[i % 2][0:TN, :], onesrow[:], xn[0:1, 0, :], start=True, stop=False)
                    nc.tensor.matmul(ps_o[i % 2][0:TN, :], ramp[:, i * TN:(i + 1) * TN], b3r[:], start=False, stop=False)
                    nc.tensor.matmul(ps_o[i % 2][0:TN, :], sums[:, i * TN:(i + 1) * TN], w3t[:], start=False, stop=True).then_inc(S["ps_z0"], 1)


def split_weights(nc, block, ctx, whh_in, whh):
    PIECE = 1024
    PIECES = KC * GATES // PIECE
    raw = [ctx.enter_context(nc.sbuf_tensor(f"split_raw{b}", [128, PIECE], F32)) for b in range(2)]
    big = ctx.enter_context(nc.sbuf_tensor("split_big", [128, PIECE], F32))
    rest = ctx.enter_context(nc.sbuf_tensor("split_rest", [128, PIECE], F32))
    piece_in = [new_semaphore(nc, f"split_in{b}") for b in range(2)]
    scaled = new_semaphore(nc, "split_scaled")
    step = new_semaphore(nc, "split_step")
    seen = new_semaphore(nc, "split_seen")

    @block.sync
    def _(sp):
        sp.sem_inc(scaled, 2)
        with sp.Fori(0, CELLS) as s:
            for m in range(PIECES):
                sp.wait_ge(scaled, s * PIECES + (m + 1))
                c, half = m // 2, m % 2
                sp.dma_start(raw[m % 2][:], whh_in[:, ds((s * KC + c) * GATES + half * PIECE, PIECE)]).then_inc(piece_in[m % 2], 16)

    @block.gpsimd
    def _(g):
        with g.Fori(0, CELLS) as s:
            for m in range(PIECES):
                hi = whh[:, ds(s * CELL_COLS + m * PIECE, PIECE)]
                lo = whh[:, ds(s * CELL_COLS + KC * GATES + m * PIECE, PIECE)]
                k = s * (4 * PIECES) + 4 * m
                g.wait_ge(piece_in[m % 2], s * (8 * PIECES) + 16 * (m // 2 + 1))
                g.sem_inc(seen, 1)
                nc.gpsimd.tensor_scalar(big[:], raw[m % 2][:], 64.0, None, ALU.mult).then_inc(scaled, 1)
                g.wait_ge(scaled, s * PIECES + (m + 3))
                g.sem_inc(seen, 1)
                nc.gpsimd.tensor_copy(hi, big[:]).then_inc(step, 1)
                g.wait_ge(step, k + 1)
                g.sem_inc(seen, 1)
                nc.gpsimd.tensor_tensor(rest[:], big[:], hi, ALU.subtract).then_inc(step, 1)
                g.wait_ge(step, k + 2)
                g.sem_inc(seen, 1)
                nc.gpsimd.tensor_scalar(rest[:], rest[:], 2048.0, None, ALU.mult).then_inc(step, 1)
                g.wait_ge(step, k + 3)
                g.sem_inc(seen, 1)
                nc.gpsimd.tensor_copy(lo, rest[:]).then_inc(step, 1)


def stage_mean_project(nc, tag, xt, z_t, w_self, w_mean, bias, rcount, h):
    with ExitStack() as ctx:
        tmp = [ctx.enter_context(nc.sbuf_tensor(f"{tag}_tmp{b}", [TN, D], F32)) for b in range(2)]
        ps = [ctx.enter_context(nc.psum_tensor(f"{tag}_ps{b}", [128, BANK], F32)) for b in range(4)]
        ready = new_semaphore(nc, tag + "_ready")
        read = new_semaphore(nc, tag + "_read")
        done = new_semaphore(nc, tag + "_done")
        with nc.Block() as block:
            @block.tensor
            def _(pe):
                for i in range(NT):
                    if i >= 2:
                        pe.wait_ge(done, i - 1)
                    for b, (lhs, w) in enumerate(((xt, w_self), (z_t, w_mean))):
                        for c in range(KC):
                            m = nc.tensor.matmul(ps[2 * (i % 2) + b][0:TN, :], lhs[:, c, i * TN:(i + 1) * TN], w[:, c, :], start=(c == 0), stop=(c == KC - 1))
                    m.then_inc(ready, 1)

            @block.vector
            def _(v):
                for i in range(NT):
                    v.wait_ge(ready, i + 1)
                    nc.vector.scalar_tensor_tensor(tmp[i % 2][:], ps[2 * (i % 2) + 1][0:TN, :], rcount[:, i:i + 1], bias[:], ALU.mult, ALU.add).then_inc(read, 1)
                    v.wait_ge(read, i + 1)
                    nc.vector.tensor_tensor(h[:, i, :], ps[2 * (i % 2)][0:TN, :], tmp[i % 2][:], ALU.add).then_inc(done, 1)
                v.wait_ge(done, NT)


def stage_add(nc, tag, x, parts):
    step = new_semaphore(nc, tag + "_added")
    with nc.Block() as block:
        @block.vector
        def _(v):
            link = linker(v, step)
            for part in parts:
                for i in range(NT):
                    last = nc.vector.tensor_tensor(x[:, i, :], x[:, i, :], part[:, i, :], ALU.add)
                link(last)


def layer_mean(nc, x, ident, adj, rcount, w_in, b_in):
    with ExitStack() as ctx:
        def sb(name, shape):
            return ctx.enter_context(nc.sbuf_tensor(name, shape, F32))
        w, b = sb("sage_w", [128, 2 * KC, D]), sb("sage_b", [TN, D])
        xn, xt, z_t = sb("sage_xn", [TN, NT, D]), sb("sage_xt", [128, KC, N]), sb("sage_zt", [128, KC, N])
        load_all(nc, "sage", [(w[:], w_in.rearrange("(c k) n -> k c n", k=128)), (b[:], rows(b_in, TN))])
        stage_layernorm(nc, "sage_ln", ident, x, xn, xt)
        stage_aggregate(nc, "sage_a", xn, adj, z_t)
        stage_mean_project(nc, "sage_p", xt, z_t, w[:, 0:KC, :], w[:, KC:2 * KC, :], b, rcount, xn)
        stage_add(nc, "sage", x, [xn])


GATE_SLOT = (0, 1, 3, 2)


def stage_input_gates(nc, xt, wih_in, bias_a_in, bias_b_in, xg):
    TOKENS = ((0, 209), (209, 208), (417, 208))
    with ExitStack() as ctx:
        def sb(name, shape, dt=F32):
            return ctx.enter_context(nc.sbuf_tensor(name, shape, dt))
        w = [sb(f"ig_w{b}", [128, KC, 2 * D]) for b in range(2)]
        out = [sb(f"ig_out{b}", [128, TOKENS[0][1], 8]) for b in range(2)]
        ba, bb = sb("ig_ba", [128, CELLS * 16]), sb("ig_bb", [128, CELLS * 16])
        ps = [ctx.enter_context(nc.psum_tensor(f"ig_ps{b}", [128, BANK], F32)) for b in range(4)]
        load_all(nc, "ig", [(ba[:], bias_a_in), (bb[:], bias_b_in)])
        S = {k: new_semaphore(nc, "ig_" + k) for k in ("ready", "moved", "bias")}
        w_in = [new_semaphore(nc, f"ig_w_in{b}") for b in range(2)]
        stored = [new_semaphore(nc, f"ig_stored{b}") for b in range(2)]
        STORE = KC * 2
        loads = [(s, pair) for s in range(CELLS) for pair in range(2)]
        stores = [(l, s, pair, at, n) for l, (s, pair) in enumerate(loads) for at, n in TOKENS]
        jobs = [(t, l, s, pair, at, n, c, j) for t, (l, s, pair, at, n) in enumerate(stores) for c in range(KC) for j in range(2)]
        with nc.Block() as block:
            @block.sync
            def _(sp):
                for l, (s, pair) in enumerate(loads):
                    if l >= 2:
                        sp.wait_ge(S["ready"], (l - 1) * len(TOKENS) * STORE)
                    sp.dma_start(w[l % 2][:], wih_in[s][:, pair * 2 * D:(pair + 1) * 2 * D].rearrange("(c k) g -> k c g", k=128)).then_inc(w_in[l % 2], 16)

            @block.scalar
            def _(a):
                for t, (l, s, pair, at, n) in enumerate(stores):
                    a.wait_ge(S["moved"], STORE * (t + 1))
                    a.dma_start(xg[s, pair, :, at:at + n, :], out[t % 2][:, 0:n, :]).then_inc(stored[t % 2], 16)
                for b in range(2):
                    a.wait_ge(stored[b], 16 * len(stores) // 2)

            @block.tensor
            def _(pe):
                for k, (t, l, s, pair, at, n, c, j) in enumerate(jobs):
                    if k % (len(TOKENS) * STORE) == 0:
                        pe.wait_ge(w_in[l % 2], 16 * (l // 2 + 1))
                    if k >= 4:
                        pe.wait_ge(S["moved"], k - 3)
                    for kc in range(KC):
                        m = nc.tensor.matmul(ps[k % 4][:, 0:n], w[l % 2][:, kc, j * D + c * 128:j * D + (c + 1) * 128], xt[:, kc, at:at + n], start=(kc == 0), stop=(kc == KC - 1))
                    m.then_inc(S["ready"], 1)

            @block.vector
            def _(v):
                nc.vector.tensor_tensor(ba[:], ba[:], bb[:], ALU.add).then_inc(S["bias"], 1)
                v.wait_ge(S["bias"], 1)
                for k, (t, l, s, pair, at, n, c, j) in enumerate(jobs):
                    if k % STORE == 0 and t >= 2:
                        v.wait_ge(stored[t % 2], 16 * (t // 2))
                    v.wait_ge(S["ready"], k + 1)
                    gate = 2 * pair + j
                    q = s * 16 + c * 4 + gate
                    slot = GATE_SLOT[gate] - 2 * pair
                    nc.vector.tensor_scalar(out[t % 2][:, 0:n, slot * 4 + c], ps[k % 4][:, 0:n], ba[:, q:q + 1], 1.0 if gate == 2 else 0.5, ALU.add, ALU.mult).then_inc(S["moved"], 1)


def stage_input_logits(nc, xt, wselx, bsel, xsel):
    with ExitStack() as ctx:
        ps = [ctx.enter_context(nc.psum_tensor(f"il_ps{b}", [128, BANK], F32)) for b in range(8)]
        cleared, ready, step = (new_semaphore(nc, "il_" + k) for k in ("cleared", "ready", "step"))
        with nc.Block() as block:
            @block.tensor
            def _(pe):
                for s in range(CELLS):
                    for b, (at, n) in enumerate(HALVES):
                        for c in range(KC):
                            m = nc.tensor.matmul(ps[2 * s + b][0:1, 0:n], wselx[:, c, s:s + 1], xt[:, c, at:at + n], start=(c == 0), stop=(c == KC - 1))
                m.then_inc(ready, 1)

            @block.vector
            def _(v):
                link = linker(v, step)
                link(nc.vector.memset(xsel[:], 0.0))
                link(nc.vector.memset(xsel[0:1, :], PAD_LOGIT))
                v.wait_ge(ready, 1)
                row = xsel[0:1, :].rearrange("p (t e) -> p t e", e=8)
                for s in range(CELLS):
                    for b, (at, n) in enumerate(HALVES):
                        last = nc.vector.tensor_scalar(row[:, at:at + n, s], ps[2 * s + b][0:1, 0:n], bsel[0:1, s:s + 1], None, ALU.add)
                link(last)


def stage_lstm(nc, whh, xg, xsel, wsel, ident, gsel, hist):
    UN = 8
    LOOPS = (N - 1) // UN
    GROUP = 4
    PIECES = ((0, 1), (1, 2), (2, 4))
    assert 1 + LOOPS * UN == N
    with ExitStack() as ctx:
        def sb(name, shape, dt=F32):
            return ctx.enter_context(nc.sbuf_tensor(name, shape, dt))
        xgb = sb("xg_buf", [128, 2, 2, CELLS * GROUP * 8])
        xg0 = sb("xg_first", [128, 16])
        hpair = sb("h_pair", [128, KC, 6], F16)
        hcur = sb("h_now", [128, KC])
        act = sb("gates_and_c", [128, 20])
        ccur = act[:, 16:20]
        parts = sb("input_and_forget_part", [128, 2 * KC])
        gsb = sb("gate_rows", [128, D])
        ok, tc = sb("out_gate", [128, KC]), sb("tanh_c", [128, KC])
        ones = sb("lstm_ones", [128, 1])
        mx, idx = sb("best", [1, 8]), sb("best_at", [1, 8], U32)
        psg = [ctx.enter_context(nc.psum_tensor(f"ps_rows{e}", [128, BANK], F32)) for e in range(CELLS)]
        psc, psl = (ctx.enter_context(nc.psum_tensor(n, [128, BANK], F32)) for n in ("ps_gates", "ps_logits"))
        busy_w, busy_x = sb("lstm_busy_w", [128, 128], F16), sb("lstm_busy_x", [128, 512], F16)
        BUSY = {"c": 2, "h": 1, "rows": 2}
        ps_busy = ctx.enter_context(nc.psum_tensor("lstm_busy", [128, BANK], F32))
        xg_in = [new_semaphore(nc, f"xg_in{g}") for g in range(2)]
        S = {k: new_semaphore(nc, "lstm_" + k) for k in (
            "xg0_in", "init", "c_ready", "h_ready", "hp_ready", "h_part", "logits", "best", "rows", "evac",
            "gates", "acted", "fi", "tanh_c", "kept", "max", "seen_v", "seen_a", "seen_pe", "xg_used")}
        with nc.Block() as block:
            @block.sync
            def _(sp):
                sp.dma_start(xg0[:].rearrange("p (h e) -> p h e", h=2), xg[0, :, :, 0, :].rearrange("h p e -> p h e")).then_inc(S["xg0_in"], 16)
                with sp.Fori(0, LOOPS) as i:
                    for g in range(2):
                        sp.wait_ge(S["xg_used"], i * UN + GROUP * (g + 1))
                        for s in range(CELLS):
                            sp.dma_start(xgb[:, g, :, s * (GROUP * 8):(s + 1) * (GROUP * 8)], xg[s, :, :, ds(i * UN + (1 + GROUP * g), GROUP), :].rearrange("h p t e -> p h (t e)")).then_inc(xg_in[g], 16)

            @block.vector
            def _(v):
                nc.vector.memset(hpair[:], 0.0).then_inc(S["init"], 1)
                for e in range(CELLS):
                    nc.vector.memset(psg[e][:], 0.0).then_inc(S["init"], 1)
                nc.vector.memset(ccur, 0.0).then_inc(S["init"], 1)
                nc.vector.memset(ones[:], 1.0).then_inc(S["init"], 1)
                nc.vector.memset(busy_w[:], 0.0).then_inc(S["init"], 1)
                nc.vector.memset(busy_x[:], 0.0).then_inc(S["init"], 1)
                v.wait_ge(S["init"], CELLS + 5)

                def cell(k):
                    v.wait_ge(S["acted"], k + 1)
                    nc.vector.scalar_tensor_tensor(parts[:], act[:, 0:8], 1.0, act[:, 12:20], ALU.add, ALU.mult).then_inc(S["fi"], 1)
                    v.wait_ge(S["fi"], k + 1)
                    nc.vector.scalar_tensor_tensor(ccur, parts[:, KC:2 * KC], 0.5, parts[:, 0:KC], ALU.mult, ALU.add).then_inc(S["c_ready"], 1)
                    nc.vector.tensor_scalar(ok[:], act[:, 8:12], 1.0, 1024.0, ALU.add, ALU.mult).then_inc(S["h_part"], 1)
                    v.wait_ge(S["tanh_c"], k + 1)
                    v.wait_ge(S["h_part"], k * 2 + 1)
                    nc.vector.tensor_tensor(hcur[:], ok[:], tc[:], ALU.mult).then_inc(S["h_ready"], 1)
                    nc.vector.tensor_tensor(hpair[:, :, 2], ok[:], tc[:], ALU.mult).then_inc(S["h_part"], 1)
                    v.wait_ge(S["h_ready"], k + 1)
                    v.wait_ge(S["h_part"], k * 2 + 2)
                    nc.vector.tensor_tensor(hpair[:, :, 3], hcur[:], hpair[:, :, 2], ALU.subtract).then_inc(S["hp_ready"], 1)

                cell(0)
                with v.Fori(0, LOOPS) as i:
                    for q in range(UN):
                        k = i * UN + (q + 1)
                        v.wait_ge(S["logits"], k)
                        v.sem_inc(S["seen_v"], 1)
                        nc.vector.max(mx[:], psl[0:1, 0:8]).then_inc(S["max"], 1)
                        v.wait_ge(S["max"], k)
                        v.sem_inc(S["seen_v"], 1)
                        nc.vector.max_index(idx[:], mx[:], psl[0:1, 0:8]).then_inc(S["best"], 1)
                        v.wait_ge(S["kept"], k)
                        cell(k)

            @block.scalar
            def _(a):
                def cell(k):
                    a.wait_ge(S["gates"], k + 1)
                    nc.scalar.activation(act[:, 0:16], psc[:, 0:16], ACT.Tanh).then_inc(S["acted"], 1)
                    a.wait_ge(S["c_ready"], k + 1)
                    nc.scalar.activation(tc[:], ccur, ACT.Tanh, scale=0.5).then_inc(S["tanh_c"], 1)

                cell(0)
                with a.Fori(0, LOOPS) as i:
                    for q in range(UN):
                        k = i * UN + (q + 1)
                        a.wait_ge(S["best"], k)
                        a.sem_inc(S["seen_a"], 1)
                        s = a.value_load(idx[0:1, 0:1])

                        def move(e):
                            a.wait_ge(S["rows"], k)
                            for lo, hi in PIECES:
                                nc.scalar.copy(gsb[:, lo * 128:hi * 128], psg[e][:, lo * 128:hi * 128]).then_inc(S["evac"], 1)

                        with a.If(s < 2):
                            with a.If(s < 1):
                                move(0)
                            with a.Else():
                                move(1)
                        with a.Else():
                            with a.If(s < 3):
                                move(2)
                            with a.Else():
                                move(3)
                        cell(k)

            @block.gpsimd
            def _(g):
                g.wait_ge(S["h_ready"], 1)
                nc.gpsimd.tensor_copy(hist[:, 0:1, :], hcur[:]).then_inc(S["kept"], 1)
                with g.Fori(0, LOOPS) as i:
                    for q in range(UN):
                        k = i * UN + (q + 1)
                        g.wait_ge(S["h_ready"], k + 1)
                        nc.gpsimd.tensor_copy(hist[:, ds(k, 1), :], hcur[:]).then_inc(S["kept"], 1)

            @block.tensor
            def _(pe):
                pe.wait_ge(S["init"], CELLS + 5)
                pe.wait_ge(S["xg0_in"], 16)

                def busy(n):
                    for _ in range(n):
                        nc.tensor.matmul(ps_busy[:, 0:BANK], busy_w[:], busy_x[:, 0:BANK], start=True, stop=True)

                pe.sem_inc(S["xg_used"], UN)
                nc.tensor.matmul(psc[:, 0:16], ident[:], xg0[:], start=True, stop=True).then_inc(S["gates"], 1)
                with pe.Fori(0, LOOPS) as i:
                    for q in range(UN):
                        k = i * UN + (q + 1)
                        nc.tensor.matmul(psl[0:1, 0:8], ones[:], xsel[:, ds(k * 8, 8)], start=True, stop=False, skip_group_check=True)
                        busy(BUSY["c"])
                        pe.wait_ge(S["c_ready"], k)
                        for c in range(KC):
                            nc.tensor.matmul(psl[0:1, 0:4], ccur[:, c:c + 1], wsel[:, KC + c, :], start=False, stop=False, skip_group_check=True)
                        busy(BUSY["h"])
                        pe.wait_ge(S["h_ready"], k)
                        for c in range(KC):
                            m = nc.tensor.matmul(psl[0:1, 0:4], hcur[:, c:c + 1], wsel[:, c, :], start=False, stop=(c == KC - 1), skip_group_check=True)
                        m.then_inc(S["logits"], 1)

                        def products(e, part, c):
                            for j in range(4):
                                at = e * CELL_COLS + (part * KC + c) * GATES + j * D
                                m = nc.tensor.matmul(psg[e][32 * j:32 * j + 4, :], hpair[:, c, 2 - 2 * part:6 - 2 * part], whh[:, at:at + D],
                                                     start=(part == 0 and c == 0), stop=(part == 1 and c == KC - 1), skip_group_check=True)
                            return m

                        pe.wait_ge(S["hp_ready"], k)
                        for e in range(CELLS):
                            products(e, 0, 0)
                        pe.wait_ge(S["best"], k)
                        pe.sem_inc(S["seen_pe"], 1)
                        s = pe.value_load(idx[0:1, 0:1])

                        def recurrent(e):
                            for part in range(2):
                                for c in range(KC):
                                    if (part, c) != (0, 0):
                                        m = products(e, part, c)
                            m.then_inc(S["rows"], 1)

                        with pe.If(s < 2):
                            with pe.If(s < 1):
                                recurrent(0)
                            with pe.Else():
                                recurrent(1)
                        with pe.Else():
                            with pe.If(s < 3):
                                recurrent(2)
                            with pe.Else():
                                recurrent(3)
                        s = pe.snap(s, min_val=0, max_val=CELLS - 1)
                        if q % GROUP == 0:
                            pe.wait_ge(xg_in[q // GROUP], i * (16 * CELLS) + 16 * CELLS)
                        nc.tensor.matmul(psc[:, 0:16], ident[:], xgb[:, q // GROUP, :, ds(s * (GROUP * 8) + (q % GROUP) * 8, 8)], start=True, stop=False, skip_group_check=True).then_inc(S["xg_used"], 1)
                        busy(BUSY["rows"])
                        for c in range(KC):
                            for n, (lo, hi) in enumerate(PIECES):
                                if c == lo:
                                    pe.wait_ge(S["evac"], i * (UN * len(PIECES)) + (q * len(PIECES) + n + 1))
                            m = nc.tensor.matmul(psc[:, c:16:4], gsb[:, c * 128:(c + 1) * 128], gsel[:], start=False, stop=(c == KC - 1), skip_group_check=True)
                        m.then_inc(S["gates"], 1)


def stage_hist_out(nc, hist, ident, x):
    with ExitStack() as ctx:
        ps = [ctx.enter_context(nc.psum_tensor(f"ho_ps{b}", [128, BANK], F32)) for b in range(2)]
        turned, used = new_semaphore(nc, "ho_turned"), new_semaphore(nc, "ho_used")
        with nc.Block() as block:
            @block.tensor
            def _(pe):
                for i in range(NT):
                    if i >= 2:
                        pe.wait_ge(used, i - 1)
                    for c in range(KC):
                        m = nc.tensor.transpose(ps[i % 2][0:TN, c * 128:(c + 1) * 128], hist[:, i * TN:(i + 1) * TN, c], ident[:])
                    m.then_inc(turned, 1)

            @block.vector
            def _(v):
                for i in range(NT):
                    v.wait_ge(turned, i + 1)
                    nc.vector.scalar_tensor_tensor(x[:, i, :], ps[i % 2][0:TN, :], 1.0 / 2048, x[:, i, :], ALU.mult, ALU.add).then_inc(used, 1)


def layer_lstm(nc, x, ident, whh, wih_in, bih_in, bhh_in, wsel_h_in, wsel_x_in, bsel_in, gsel_in, xg):
    with ExitStack() as ctx:
        def sb(name, shape):
            return ctx.enter_context(nc.sbuf_tensor(name, shape, F32))
        wsel, bsel, gsel = sb("l_wsel", [128, 2 * KC, CELLS]), sb("l_bsel", [1, CELLS]), sb("l_gsel", [128, 4])
        hist = sb("l_hist", [128, N, KC])
        xt = hist[:].rearrange("p n c -> p (n c)").rearrange("p (c n) -> p c n", c=KC)
        with nc.sbuf_tensor("l_xn", [TN, NT, D], F32) as xn:
            stage_layernorm(nc, "l_ln", ident, x, xn, xt)
        stage_input_gates(nc, xt, wih_in, bih_in, bhh_in, xg)
        wselx = sb("l_wselx", [128, KC, CELLS])
        xsel = sb("l_xsel", [128, N * 8])
        load_all(nc, "lsel", [(wsel[:], wsel_h_in), (wselx[:], wsel_x_in), (bsel[:], bsel_in), (gsel[:], gsel_in)])
        stage_input_logits(nc, xt, wselx, bsel, xsel)
        scaled = new_semaphore(nc, "l_wsel_scaled")
        with nc.Block() as block:
            @block.vector
            def _(v):
                nc.vector.tensor_scalar(wsel[:, 0:KC, :], wsel[:, 0:KC, :], 1.0 / 2048, None, ALU.mult).then_inc(scaled, 1)
                nc.vector.tensor_scalar(wsel[:, KC:, :], wsel[:, KC:, :], 0.5, None, ALU.mult).then_inc(scaled, 1)
                v.wait_ge(scaled, 2)
        stage_lstm(nc, whh, xg, xsel, wsel, ident, gsel, hist)
        stage_hist_out(nc, hist, ident, x)


def layer_batchnorm(nc, x, ident, adj, rcount, wl_in, bl_in, wr_in, gamma_in, beta_in):
    with ExitStack() as ctx:
        def sb(name, shape):
            return ctx.enter_context(nc.sbuf_tensor(name, shape, F32))
        wl, wr, bl = sb("bn_wl", [128, KC, D]), sb("bn_wr", [128, KC, D]), sb("bn_bl", [TN, D])
        gamma, beta = sb("bn_gamma", [TN, D]), sb("bn_beta", [TN, D])
        xn, xt, z_t, h = sb("bn_xn", [TN, NT, D]), sb("bn_xt", [128, KC, N]), sb("bn_zt", [128, KC, N]), sb("bn_h", [TN, NT, D])
        sq = sb("bn_sq", [TN, NT, D])
        mean, var, root, r, t = (sb("bn_" + k, [TN, D]) for k in ("mean", "var", "root", "r", "t"))
        allones = sb("bn_ones", [TN, TN])
        load_all(nc, "bn", [(wl[:], wl_in.rearrange("(c k) n -> k c n", k=128)), (wr[:], wr_in.rearrange("(c k) n -> k c n", k=128)),
                            (bl[:], rows(bl_in, TN)), (gamma[:], rows(gamma_in, TN)), (beta[:], rows(beta_in, TN))])
        stage_layernorm(nc, "bn_ln", ident, x, xn, xt)
        stage_aggregate(nc, "bn_a", xn, adj, z_t)
        stage_mean_project(nc, "bn_p", xt, z_t, wr, wl, bl, rcount, h)
        ps = [ctx.enter_context(nc.psum_tensor(f"bn_ps{b}", [128, BANK], F32)) for b in range(2)]
        made, ready, step, squared, summed, rooted = (new_semaphore(nc, "bn_" + k) for k in ("made", "ready", "step", "squared", "summed", "rooted"))
        with nc.Block() as block:
            @block.gpsimd
            def _(g):
                nc.gpsimd.memset(allones[:], 1.0).then_inc(made, 1)

            @block.tensor
            def _(pe):
                pe.wait_ge(made, 1)
                for i in range(NT):
                    m = nc.tensor.matmul(ps[0][0:TN, :], allones[:], h[:, i, :], start=(i == 0), stop=(i == NT - 1))
                m.then_inc(summed, 1)
                for i in range(NT):
                    pe.wait_ge(squared, i + 1)
                    m = nc.tensor.matmul(ps[1][0:TN, :], allones[:], sq[:, i, :], start=(i == 0), stop=(i == NT - 1))
                m.then_inc(summed, 1)

            @block.scalar
            def _(a):
                for i in range(NT):
                    a.wait_ge(ready, i + 1)
                    nc.scalar.activation(sq[:, i, :], h[:, i, :], ACT.Square).then_inc(squared, 1)
                a.wait_ge(ready, NT + 1)
                nc.scalar.activation(root[:], var[:], ACT.Sqrt).then_inc(rooted, 1)

            @block.vector
            def _(v):
                link = linker(v, step)
                v.wait_ge(summed, 1)
                link(nc.vector.tensor_scalar(mean[:], ps[0][0:TN, :], 1.0 / N, None, ALU.mult))
                for i in range(NT):
                    nc.vector.tensor_tensor(h[:, i, :], h[:, i, :], mean[:], ALU.subtract).then_inc(ready, 1)
                v.wait_ge(summed, 2)
                nc.vector.tensor_scalar(var[:], ps[1][0:TN, :], 1.0 / N, LN_EPS, ALU.mult, ALU.add).then_inc(ready, 1)
                v.wait_ge(rooted, 1)
                link(nc.vector.reciprocal(r[:], root[:]))
                newton_rsqrt(nc, link, r[:], var[:], t[:])
                link(nc.vector.tensor_tensor(r[:], r[:], gamma[:], ALU.mult))
                for i in range(NT):
                    last = nc.vector.tensor_tensor(sq[:, i, :], h[:, i, :], r[:], ALU.mult)
                link(last)
                for i in range(NT):
                    last = nc.vector.tensor_tensor(h[:, i, :], sq[:, i, :], beta[:], ALU.add)
                link(last)
                for i in range(NT):
                    last = nc.vector.scalar_tensor_tensor(sq[:, i, :], h[:, i, :], 0.0, xn[:, i, :], ALU.max, ALU.add)
                link(last)
        stage_add(nc, "bn", x, [sq])


def layer_peer(nc, x, ident, wq_in, keys_in, wd_in, wu_in):
    with ExitStack() as ctx:
        def sb(name, shape, dt=F32):
            return ctx.enter_context(nc.sbuf_tensor(name, shape, dt))
        wq, keys = sb("pe_wq", [128, KC, D]), sb("pe_keys", [128, 2, KEYS])
        wd, wu = sb("pe_wd", [128, KC, KEYS]), sb("pe_wu", [128, 2, D])
        xn, xt, qt = sb("pe_xn", [TN, NT, D]), sb("pe_xt", [128, KC, N]), sb("pe_qt", [128, KC, N])
        load_all(nc, "pe", [(wq[:], wq_in.rearrange("(c k) n -> k c n", k=128)), (keys[:], keys_in), (wd[:], wd_in), (wu[:], wu_in.rearrange("(c k) n -> k c n", k=128))])
        stage_layernorm(nc, "pe_ln", ident, x, xn, xt)
        ps_q = [ctx.enter_context(nc.psum_tensor(f"pe_psq{b}", [128, BANK], F32)) for b in range(2)]
        ps_s = ctx.enter_context(nc.psum_tensor("pe_pss", [128, 4 * BANK], F32))
        ps_t = ctx.enter_context(nc.psum_tensor("pe_pst", [128, BANK], F32))
        ps_o = ctx.enter_context(nc.psum_tensor("pe_pso", [128, BANK], F32))
        jobs = [(c, at, n) for c in range(KC) for at, n in HALVES]
        q_ready, q_moved = new_semaphore(nc, "pe_q_ready"), new_semaphore(nc, "pe_q_moved")
        with nc.Block() as block:
            @block.tensor
            def _(pe):
                for k, (c, at, n) in enumerate(jobs):
                    if k >= 2:
                        pe.wait_ge(q_moved, k - 1)
                    for kc in range(KC):
                        m = nc.tensor.matmul(ps_q[k % 2][:, 0:n], wq[:, kc, c * 128:(c + 1) * 128], xt[:, kc, at:at + n], start=(kc == 0), stop=(kc == KC - 1))
                    m.then_inc(q_ready, 1)

            @block.scalar
            def _(a):
                for k, (c, at, n) in enumerate(jobs):
                    a.wait_ge(q_ready, k + 1)
                    nc.scalar.activation(qt[:, c, at:at + n], ps_q[k % 2][:, 0:n], ACT.Copy, scale=float(1.0 / np.sqrt(1.0 + 1e-5))).then_inc(q_moved, 1)
        def two(name, shape, dt=F32):
            return [sb(f"pe_{name}{p}", shape, dt) for p in range(2)]
        vals, places, places_f = two("vals", [TN, TOPK]), two("places", [TN, TOPK], U32), two("places_f", [TN, TOPK])
        sim, grid, grid1, grid2, ex, pick, weight = (two(k, [TN, KEYS]) for k in ("sim", "grid", "grid1", "grid2", "ex", "pick", "weight"))
        top, top2, neg, total, inv = (two(k, [TN, n]) for k, n in (("top", 8), ("top2", 8), ("neg", 1), ("total", 1), ("inv", 1)))
        gelu = two("gelu", [TN, KEYS])
        w_t = sb("pe_wt", [128, 2, TN])
        step = [new_semaphore(nc, f"pe_step{p}") for p in range(2)]
        S = {k: new_semaphore(nc, "pe_" + k) for k in ("sims", "neg", "exp", "heads", "joined", "gated", "down", "gelu", "turned", "wt", "out", "added", "seen", "cleared")}
        warm, warm_out = sb("pe_warm", [1, 1]), sb("pe_warm_out", [1, 1])
        STEPS_HEAD = 14
        with nc.Block() as block:
            @block.tensor
            def _(pe):
                for i in range(NT):
                    if i >= 1:
                        pe.wait_ge(S["heads"], HEADS * i)
                    for h in range(HEADS):
                        g = 32 * (h % 4)
                        m = nc.tensor.matmul(ps_s[0:TN, (h % 4) * BANK + (h // 4) * KEYS:(h % 4) * BANK + (h // 4 + 1) * KEYS], qt[g:g + 32, h // 4, i * TN:(i + 1) * TN], keys[g:g + 32, h // 4, :], start=True, stop=True, skip_group_check=True)
                    m.then_inc(S["sims"], 1)
                    if i >= 1:
                        pe.wait_ge(S["gelu"], i)
                    for c in range(KC):
                        m = nc.tensor.matmul(ps_q[0][0:TN, 0:KEYS], qt[:, c, i * TN:(i + 1) * TN], wd[:, c, :], start=(c == 0), stop=(c == KC - 1))
                    m.then_inc(S["down"], 1)
                    pe.wait_ge(S["gated"], i + 1)
                    for c in range(2):
                        m = nc.tensor.transpose(ps_t[:, c * TN:(c + 1) * TN], weight[0][:, c * 128:(c + 1) * 128], ident[0:TN, 0:TN])
                    m.then_inc(S["turned"], 1)
                    pe.wait_ge(S["wt"], i + 1)
                    if i >= 1:
                        pe.wait_ge(S["added"], i)
                    for c in range(2):
                        m = nc.tensor.matmul(ps_o[0:TN, :], w_t[:, c, :], wu[:, c, :], start=(c == 0), stop=(c == 1))
                    m.then_inc(S["out"], 1)

            @block.scalar
            def _(a):
                a.wait_ge(S["cleared"], 1)
                for i in range(NT):
                    a.wait_ge(S["down"], i + 1)
                    if i >= 2:
                        a.wait_ge(S["gated"], i - 1)
                    nc.scalar.activation(gelu[i % 2][:], ps_q[0][0:TN, 0:KEYS], ACT.Gelu_apprx_tanh).then_inc(S["gelu"], 1)
                    nc.scalar.activation(warm_out[:], warm[:], ACT.Exp)
                    with a.Fori(0, HEADS // 2) as h:
                        for p in range(2):
                            a.wait_ge(S["neg"], h * 2 + (i * HEADS + p + 1))
                            nc.scalar.activation(ex[p][:], grid[p][:], ACT.Exp, bias=neg[p][:]).then_inc(S["exp"], 1)
                    a.wait_ge(S["turned"], i + 1)
                    nc.scalar.copy(w_t[:], ps_t[:, 0:2 * TN].rearrange("p (c n) -> p c n", c=2)).then_inc(S["wt"], 1)

            @block.vector
            def _(v):
                nc.vector.memset(warm[:], 0.0).then_inc(S["cleared"], 1)
                for i in range(NT):
                    if i >= 1:
                        v.wait_ge(S["turned"], i)
                    for p in range(2):
                        nc.vector.memset(weight[p][:], 0.0)
                    v.wait_ge(S["sims"], i + 1)
                    with v.Fori(0, HEADS // 2) as h:
                        base = i * (HEADS // 2) * STEPS_HEAD
                        done = [0, 0]

                        def before(p):
                            v.wait_ge(step[p], h * STEPS_HEAD + (base + done[p]))
                            v.sem_inc(S["seen"], 1)

                        def both(make):
                            for p in range(2):
                                if done[p]:
                                    before(p)
                                make(p).then_inc(step[p], 1)
                                done[p] += 1

                        both(lambda p: nc.vector.tensor_copy(sim[p][:], ps_s[0:TN, ds(h * (2 * KEYS) + p * KEYS, KEYS)]))
                        for at in (0, 8):
                            both(lambda p: nc.vector.max(vals[p][:, at:at + 8], sim[p][:]))
                            both(lambda p: nc.vector.max_index(places[p][:, at:at + 8], vals[p][:, at:at + 8], sim[p][:]))
                            if at == 0:
                                both(lambda p: nc.vector.match_replace(sim[p][:], vals[p][:, 0:8], sim[p][:], SENTINEL))
                        both(lambda p: nc.vector.tensor_copy(places_f[p][:], places[p][:]))
                        both(lambda p: nc.vector.tensor_tensor(grid[p][:].rearrange("p (a b) -> p a b", a=TOPK), vals[p][:].unsqueeze(2).broadcast_to([TN, TOPK, TOPK]),
                                                               places_f[p][:].unsqueeze(1).broadcast_to([TN, TOPK, TOPK]), ALU.add))
                        both(lambda p: nc.vector.max(top[p][:], grid[p][:]))
                        for p in range(2):
                            before(p)
                            nc.vector.tensor_scalar(neg[p][:], top[p][:, 0:1], -1.0, None, ALU.mult).then_inc(S["neg"], 1)
                        both(lambda p: nc.vector.match_replace(grid1[p][:], top[p][:], grid[p][:], SENTINEL))
                        both(lambda p: nc.vector.max(top2[p][:], grid1[p][:]))
                        both(lambda p: nc.vector.match_replace(grid2[p][:], top2[p][:], grid1[p][:], SENTINEL))
                        v.wait_ge(S["exp"], h * 2 + (i * HEADS + 2))
                        both(lambda p: nc.vector.scalar_tensor_tensor(pick[p][:], grid2[p][:], SENTINEL, ex[p][:], ALU.is_equal, ALU.mult, accum_out=total[p][:]))
                        both(lambda p: nc.vector.reciprocal(inv[p][:], total[p][:]))
                        assert done == [STEPS_HEAD, STEPS_HEAD]
                        for p in range(2):
                            before(p)
                            nc.vector.scalar_tensor_tensor(weight[p][:], pick[p][:], inv[p][:], weight[p][:], ALU.mult, ALU.add).then_inc(S["heads"], 1)
                    v.wait_ge(S["heads"], HEADS * (i + 1))
                    nc.vector.tensor_tensor(weight[0][:], weight[0][:], weight[1][:], ALU.add).then_inc(S["joined"], 1)
                    v.wait_ge(S["joined"], i + 1)
                    v.wait_ge(S["gelu"], i + 1)
                    nc.vector.tensor_tensor(weight[0][:], weight[0][:], gelu[i % 2][:], ALU.mult).then_inc(S["gated"], 1)
                    v.wait_ge(S["out"], i + 1)
                    nc.vector.tensor_tensor(x[:, i, :], x[:, i, :], ps_o[0:TN, :], ALU.add).then_inc(S["added"], 1)


def stage_store(nc, x, out):
    stored = new_semaphore(nc, "x_stored")
    with nc.Block() as block:
        @block.sync
        def _(sp):
            sp.dma_start(out.rearrange("(i p) d -> p i d", p=TN), x[:]).then_inc(stored, 16)
            sp.wait_ge(stored, 16)


STAGES = ("gcn", "moe", "tp", "ode", "sage", "lstm", "bn", "peer")


def build(nc, a, out, stages=STAGES):
    LIVE.clear()
    up_dram = nc.dram_tensor("up_scratch", [N, D], F32, kind="Internal").ap()
    h3_dram = nc.dram_tensor("h3_scratch", [HIDDEN, E], F32, kind="Internal").ap()
    xg = nc.dram_tensor("xg_scratch", [CELLS, 2, 128, N, 8], F32, kind="Internal").ap()
    with ExitStack() as ctx:
        def sb(name, shape, dt=F32):
            return ctx.enter_context(nc.sbuf_tensor(name, shape, dt))
        x = sb("x_rows", [TN, NT, D])
        ident, ones = sb("ident", [128, 128]), sb("ones", [128, 1])
        adj = sb("adj", [TN, NT, N])
        count, dis, rcount = sb("count", [TN, NT]), sb("dis", [TN, NT]), sb("rcount", [TN, NT])
        bounds = sb("bounds", [1, 2 * NT], I32)
        with ExitStack() as graph:
            iota = graph.enter_context(nc.sbuf_tensor("iota", [128, N], I32))
            src_i = graph.enter_context(nc.sbuf_tensor("src_i", [TE, ET], I32))
            dst_f = graph.enter_context(nc.sbuf_tensor("dst_f", [TE, ET], F32))
            stage_constants(nc, a["x"], x, ident, ones, iota)
            early = graph.enter_context(ExitStack())

            def sb_early(name, shape):
                return early.enter_context(nc.sbuf_tensor(name, shape, F32))
            gcn, gcn_loads = weights_gcn(sb_early, a["L0_gnn_W1"], a["L0_gnn_b1"], a["L0_gnn_W2"], a["L0_gnn_b2"])
            moe, moe_loads = weights_experts(sb_early, a["L0_ffn_Ws"], a["L0_ffn_bs"], a["L0_ffn_W1"], a["L0_ffn_b1T"], a["L0_ffn_W2"], a["L0_ffn_b2"])
            stage_graph(nc, a["src_t"], a["dst_t"], a["dst_rows"], iota, ident, ones, src_i, dst_f, adj, count, dis, rcount, bounds, gcn_loads + moe_loads)
            if "gcn" in stages:
                layer_gcn(nc, x, ident, adj, dis, *gcn)
                end_of_layer(nc)
            cleared = new_semaphore(nc, "diag_cleared")
            with nc.Block() as block:
                @block.vector
                def _(v):
                    for i in range(NT):
                        nc.vector.tensor_tensor(adj[:, i, i * TN:(i + 1) * TN], adj[:, i, i * TN:(i + 1) * TN], ident[0:TN, 0:TN], ALU.subtract).then_inc(cleared, 1)
                    v.wait_ge(cleared, NT)
            if "moe" in stages:
                layer_experts(nc, x, ident, ones, *moe)
                end_of_layer(nc)
            early.close()
            if "tp" in stages:
                layer_tensor_product(nc, x, ident, iota, src_i, dst_f, bounds, a["attrs_t"], a["feats_t"], a["L1_gnn_W_up0"], a["L1_gnn_W_up1"],
                                     a["L1_gnn_W_mlp1"], a["L1_gnn_W_mlp2"], a["L1_gnn_W_mlp3"], a["L1_gnn_W_mlp4"], a["L1_gnn_W_out0"], a["L1_gnn_W_out1"],
                                     up_dram, h3_dram)
                end_of_layer(nc)
        with nc.sbuf_tensor("whh", [128, CELLS * CELL_COLS], F16) as whh:
            if "ode" in stages or "lstm" in stages:
                layer_ode(nc, x, ident, ones, a["L1_ffn_W1T"], a["L1_ffn_b1"], a["L1_ffn_W2T"], a["L1_ffn_b2"], a["L1_ffn_b2_row"], a["L1_ffn_W3"], a["L1_ffn_W3T"],
                          a["L1_ffn_b3T"], a["L1_ffn_b3"], a["whh_t"], whh)
                end_of_layer(nc)
            if "sage" in stages:
                layer_mean(nc, x, ident, adj, rcount, a["L2_gnn_WT"], a["L2_gnn_b"])
                end_of_layer(nc)
            if "lstm" in stages:
                layer_lstm(nc, x, ident, whh, a["wih_t"], a["bih_t"], a["bhh_t"], a["wsel_h"], a["wsel_x"], a["L2_ffn_b_sel"], a["gsel"], xg)
                end_of_layer(nc)
        if "bn" in stages:
            layer_batchnorm(nc, x, ident, adj, rcount, a["L3_gnn_W_lT"], a["L3_gnn_b_l"], a["L3_gnn_W_rT"], a["L3_gnn_gamma"], a["L3_gnn_beta"])
            end_of_layer(nc)
        if "peer" in stages:
            layer_peer(nc, x, ident, a["L3_ffn_w_q"], a["keys_t"], a["wd_t"], a["wu"])
            end_of_layer(nc)
        stage_store(nc, x, out)


def lay_out(i):
    c = np.ascontiguousarray
    i = {k: np.asarray(v) for k, v in i.items()}
    a = {"x": i["x"]}
    a["src_t"] = i["src"].reshape(ET, TE).T
    a["dst_t"] = i["dst"].reshape(ET, TE).T
    a["dst_rows"] = i["dst"].reshape(UNITS, UNIT)
    a["attrs_t"] = i["edge_attr_4"].reshape(ET, TE, 4).transpose(1, 0, 2).reshape(TE, ET * 4)
    a["feats_t"] = i["edge_attr_8"].T
    for k in ("L0_gnn_W1", "L0_gnn_W2", "L0_ffn_Ws", "L0_ffn_W1", "L0_ffn_W2", "L0_ffn_b2", "L1_gnn_W_up0", "L1_gnn_W_up1", "L1_gnn_W_mlp1",
              "L1_gnn_W_mlp2", "L1_gnn_W_mlp3", "L1_gnn_W_mlp4", "L1_gnn_W_out0", "L1_gnn_W_out1", "L1_ffn_W3", "L3_ffn_w_q"):
        a[k] = i[k]
    for k in ("L0_gnn_b1", "L0_gnn_b2", "L0_ffn_bs", "L1_ffn_b3", "L2_gnn_b", "L2_ffn_b_sel", "L3_gnn_b_l", "L3_gnn_gamma", "L3_gnn_beta"):
        a[k] = i[k].reshape(1, -1)
    for k in ("L1_ffn_b1", "L1_ffn_b2"):
        a[k] = i[k].reshape(-1, 1)
    for k in ("L1_ffn_W1", "L1_ffn_W2", "L1_ffn_W3", "L2_gnn_W", "L3_gnn_W_l", "L3_gnn_W_r"):
        a[k + "T"] = i[k].T
    a["L1_ffn_b2_row"] = i["L1_ffn_b2"].reshape(1, -1)
    a["L0_ffn_b1T"] = i["L0_ffn_b1"].T
    a["L1_ffn_b3T"] = i["L1_ffn_b3"].reshape(KC, 128).T
    a["whh_t"] = i["L2_ffn_W_hh"].transpose(2, 0, 1).reshape(KC, 128, CELLS, GATES).transpose(1, 2, 0, 3).reshape(128, -1)
    a["wih_t"] = i["L2_ffn_W_ih"].transpose(0, 2, 1)
    for k, n in (("bih_t", "L2_ffn_b_ih"), ("bhh_t", "L2_ffn_b_hh")):
        a[k] = i[n].reshape(CELLS, 4, KC, 128).transpose(3, 0, 2, 1).reshape(128, CELLS * 16)
    a["wsel_h"] = i["L2_ffn_W_sel"][:, :2 * D].reshape(CELLS, 2 * KC, 128).transpose(2, 1, 0)
    a["wsel_x"] = i["L2_ffn_W_sel"][:, 2 * D:].reshape(CELLS, KC, 128).transpose(2, 1, 0)
    keys = i["L3_ffn_keys"][:, :, 0, :]
    a["keys_t"] = keys.reshape(2, 4, KEYS, KEY).transpose(1, 3, 0, 2).reshape(128, 2, KEYS)
    a["wd_t"] = i["L3_ffn_weight_down_embed"][:KEYS].T.reshape(KC, 128, KEYS).transpose(1, 0, 2)
    a["wu"] = i["L3_ffn_weight_up_embed"][:KEYS]
    gsel = np.zeros((128, 4), np.float32)
    for j in range(4):
        half = 1.0 if j == 2 else 0.5
        gsel[32 * j:32 * j + 2, GATE_SLOT[j]] = half * 2.0 ** -17
        gsel[32 * j + 2:32 * j + 4, GATE_SLOT[j]] = half * 2.0 ** -28
    a["gsel"] = gsel
    return {k: c(v) for k, v in a.items()}


def kernel(**inputs):
    import concourse.bacc as bacc
    from concourse.bass_utils import run_bass_kernel_spmd

    arrays = lay_out(inputs)
    nc = bacc.Bacc("TRN2", target_bir_lowering=False, num_devices=1)
    args = {k: nc.dram_tensor("in_" + k, v.shape, mybir.dt.from_np(v.dtype), kind="ExternalInput").ap() for k, v in arrays.items()}
    out = nc.dram_tensor("out_x", [N, D], F32, kind="ExternalOutput").ap()
    build(nc, args, out)
    r = run_bass_kernel_spmd(nc, [{"in_" + k: v for k, v in arrays.items()}], core_ids=[0])
    return r.results[0]["out_x"]
```
